# Optimizing a Trainium2 kernel written in Bass

```python
import numpy as np
import jax
import jax.numpy as jnp

def _softmax(x, axis=-1):
    return jax.nn.softmax(x, axis=axis)

def _gelu(x):
    return jax.nn.gelu(x, approximate=True)

def _silu(x):
    return jax.nn.silu(x)

def _sigmoid(x):
    return jax.nn.sigmoid(x)

def _layernorm(x, axis=-1, eps=1e-05):
    m = jnp.mean(x, axis=axis, keepdims=True)
    v = jnp.var(x, axis=axis, keepdims=True)
    return (x - m) / jnp.sqrt(v + eps)

def _scatter_add(tgt, idx, src, axis=0):
    return tgt.at[idx].add(src)

def _segment_sum(src, seg, n):
    return jax.ops.segment_sum(src, seg, n)
kernel_name = 'mk_adaln_d2_jaxref_r8_6552eb'

def setup_inputs(seed: int=0):
    np.random.seed(seed)
    _w = jnp.asarray

    def _L0_attn_setup():
        import jax, jax.numpy as jnp
        import numpy as np
        B, L, H = (1, 256, 256)
        E, N, K, R = (512, 16, 4, 128)

        def _mamba_mixer(hidden_states, in_proj_w, conv_w, conv_b, x_proj_w, dt_proj_w, dt_proj_b, A_log, D, out_proj_w):
            proj = jnp.einsum('blh,eh->ble', hidden_states, in_proj_w)
            h, gate = jnp.split(proj, 2, axis=-1)
            h_c = h.transpose(0, 2, 1)
            h_c = jax.lax.conv_general_dilated(h_c, conv_w, window_strides=(1,), padding=[(K - 1, 0)], feature_group_count=E, dimension_numbers=('NCH', 'OIH', 'NCH'))
            h_c = h_c + conv_b[None, :, None]
            h = jax.nn.silu(h_c).transpose(0, 2, 1)
            ssm = jnp.einsum('ble,pe->blp', h, x_proj_w)
            dt, Bp, Cp = jnp.split(ssm, [R, R + N], axis=-1)
            dt = jax.nn.softplus(jnp.einsum('blr,er->ble', dt, dt_proj_w) + dt_proj_b)
            A = -jnp.exp(A_log)
            dA = jnp.exp(dt[..., None] * A)
            dBu = (dt * h)[..., None] * Bp[:, :, None, :]

            def step(s, xs):
                dA_t, dBu_t = xs
                s = s * dA_t + dBu_t
                return (s, s)
            s0 = jnp.zeros((h.shape[0], E, N), h.dtype)
            _, states = jax.lax.scan(step, s0, (dA.transpose(1, 0, 2, 3), dBu.transpose(1, 0, 2, 3)))
            y = jnp.einsum('lben,bln->ble', states, Cp)
            y = y + h * D
            y = y * jax.nn.silu(gate)
            return jnp.einsum('ble,he->blh', y, out_proj_w)
        key = jax.random.key(seed)
        ks = jax.random.split(key, 8)
        s = 0.02
        inp = {'hidden_states': jax.random.normal(ks[0], (B, L, H), jnp.float32), 'in_proj_w': jax.random.normal(ks[1], (2 * E, H), jnp.float32) * s, 'conv_w': jax.random.normal(ks[2], (E, 1, K), jnp.float32) * s, 'conv_b': jax.random.normal(ks[3], (E,), jnp.float32) * s, 'x_proj_w': jax.random.normal(ks[4], (R + 2 * N, E), jnp.float32) * s, 'dt_proj_w': jax.random.normal(ks[5], (E, R), jnp.float32) * s, 'dt_proj_b': jax.random.normal(ks[6], (E,), jnp.float32) * s, 'A_log': jnp.broadcast_to(jnp.log(jnp.arange(1, N + 1, dtype=jnp.float32))[None, :], (E, N)).copy(), 'D': jnp.ones((E,), jnp.float32), 'out_proj_w': jax.random.normal(ks[7], (H, E), jnp.float32) * s}
        return inp
    _L0_attn_in = _L0_attn_setup()

    def _L0_ffn_setup():
        import jax, jax.numpy as jnp
        import numpy as np
        LORA_ALPHA = 16.0
        TOP_K = 2
        key = jax.random.key(seed)
        k_x, k_w, k_g, k_a, k_b = jax.random.split(key, 5)
        B, S, H, O, E, R = (2, 256, 256, 256, 8, 16)
        x = jax.random.normal(k_x, (B, S, H), dtype=jnp.float32)
        weight = jax.random.normal(k_w, (O, H), dtype=jnp.float32)
        gate_w = jax.random.normal(k_g, (E, H), dtype=jnp.float32) * 0.02
        A_w = jax.random.normal(k_a, (E, R, H), dtype=jnp.float32) * (1.0 / np.sqrt(H))
        B_w = jax.random.normal(k_b, (E, O, R), dtype=jnp.float32) * 0.01
        return {'x': x, 'weight': weight, 'gate_w': gate_w, 'A_w': A_w, 'B_w': B_w}
    _L0_ffn_in = _L0_ffn_setup()
    _L0_c = _w((lambda *s: np.random.randn(*s).astype(np.float32) * 0.05)(1, 256))
    _L0_wmod = _w((lambda *s: np.random.randn(*s).astype(np.float32) * 0.05)(256, 6 * 256) * 256 ** (-0.5))

    def _L1_attn_setup():
        import jax, jax.numpy as jnp
        import numpy as np
        D = 256
        H = 8
        QK = D // 2
        FF = 1024
        CAP = 15.0
        EPS = 1e-06

        def _rmsnorm(x, w, eps=EPS):
            xf = x.astype(jnp.float32)
            var = jnp.mean(xf * xf, axis=-1, keepdims=True)
            return (w * xf * jax.lax.rsqrt(var + eps)).astype(x.dtype)

        def _soft_cap(x, cap=CAP):
            return cap * jnp.tanh(x / cap)

        def _mlstm_parallel(q, k, v, i_pre, f_pre):
            B, Hn, S, dqk = q.shape
            logfg = jax.nn.log_sigmoid(f_pre)
            Fcum = jnp.cumsum(logfg, axis=-1)
            Dmat = Fcum[..., :, None] - Fcum[..., None, :] + i_pre[..., None, :]
            causal = jnp.tril(jnp.ones((S, S), dtype=bool))
            Dmat = jnp.where(causal, Dmat, -jnp.inf)
            m = jnp.max(Dmat, axis=-1, keepdims=True)
            Smat = jnp.exp(Dmat - m)
            qk = jnp.einsum('bhsd,bhtd->bhst', q, k) / jnp.sqrt(jnp.float32(dqk))
            C = qk * Smat
            n = jnp.maximum(jnp.abs(jnp.sum(C, axis=-1, keepdims=True)), jnp.exp(-m))
            h = jnp.einsum('bhst,bhtd->bhsd', C / n, v)
            return h
        key = jax.random.key(seed)
        ks = jax.random.split(key, 17)
        sc = 0.02
        inp = {'x': jax.random.normal(ks[0], (2, 256, D), jnp.float32), 'norm1_w': jnp.ones((D,), jnp.float32), 'wq': jax.random.normal(ks[1], (D, QK), jnp.float32) * sc, 'wk': jax.random.normal(ks[2], (D, QK), jnp.float32) * sc, 'wv': jax.random.normal(ks[3], (D, D), jnp.float32) * sc, 'w_ig': jax.random.normal(ks[4], (D, H), jnp.float32) * sc, 'b_ig': jnp.zeros((H,), jnp.float32), 'w_fg': jax.random.normal(ks[5], (D, H), jnp.float32) * sc, 'b_fg': jnp.linspace(3.0, 6.0, H).astype(jnp.float32), 'w_og': jax.random.normal(ks[6], (D, D), jnp.float32) * sc, 'mh_w': jnp.ones((D,), jnp.float32), 'w_out': jax.random.normal(ks[7], (D, D), jnp.float32) * sc, 'norm2_w': jnp.ones((D,), jnp.float32), 'w_gate': jax.random.normal(ks[8], (D, FF), jnp.float32) * sc, 'w_up': jax.random.normal(ks[9], (D, FF), jnp.float32) * sc, 'w_down': jax.random.normal(ks[10], (FF, D), jnp.float32) * sc}
        return inp
    _L1_attn_in = _L1_attn_setup()

    def _L1_ffn_setup():
        import jax, jax.numpy as jnp
        import numpy as np
        TOPK = 2

        def _mlp(x, w1, w2, w3):
            a = jnp.dot(x, w1.T).astype(jnp.float32)
            b = jnp.dot(x, w3.T).astype(jnp.float32)
            h = (jax.nn.silu(a) * b).astype(x.dtype)
            return jnp.dot(h, w2.T)
        key = jax.random.key(seed)
        ks = jax.random.split(key, 8)
        B, S, D, I, E = (4, 256, 256, 176, 16)
        SI = I * 2
        sc = 0.02
        return {'x': jax.random.normal(ks[0], (B, S, D), jnp.bfloat16), 'gate_w': jax.random.normal(ks[1], (E, D), jnp.float32) * sc, 'w1': jax.random.normal(ks[2], (E, I, D), jnp.bfloat16) * sc, 'w2': jax.random.normal(ks[3], (E, D, I), jnp.bfloat16) * sc, 'w3': jax.random.normal(ks[4], (E, I, D), jnp.bfloat16) * sc, 'sw1': jax.random.normal(ks[5], (SI, D), jnp.bfloat16) * sc, 'sw2': jax.random.normal(ks[6], (D, SI), jnp.bfloat16) * sc, 'sw3': jax.random.normal(ks[7], (SI, D), jnp.bfloat16) * sc}
    _L1_ffn_in = _L1_ffn_setup()
    _L1_c = _w((lambda *s: np.random.randn(*s).astype(np.float32) * 0.05)(1, 256))
    _L1_wmod = _w((lambda *s: np.random.randn(*s).astype(np.float32) * 0.05)(256, 6 * 256) * 256 ** (-0.5))
    _d = {'L0_attn_hidden_states': _L0_attn_in['hidden_states'], 'L0_attn_in_proj_w': _L0_attn_in['in_proj_w'], 'L0_attn_conv_w': _L0_attn_in['conv_w'], 'L0_attn_conv_b': _L0_attn_in['conv_b'], 'L0_attn_x_proj_w': _L0_attn_in['x_proj_w'], 'L0_attn_dt_proj_w': _L0_attn_in['dt_proj_w'], 'L0_attn_dt_proj_b': _L0_attn_in['dt_proj_b'], 'L0_attn_A_log': _L0_attn_in['A_log'], 'L0_attn_D': _L0_attn_in['D'], 'L0_attn_out_proj_w': _L0_attn_in['out_proj_w'], 'L0_ffn_weight': _L0_ffn_in['weight'], 'L0_ffn_gate_w': _L0_ffn_in['gate_w'], 'L0_ffn_A_w': _L0_ffn_in['A_w'], 'L0_ffn_B_w': _L0_ffn_in['B_w'], 'L0_c': _L0_c, 'L0_wmod': _L0_wmod, 'L1_attn_norm1_w': _L1_attn_in['norm1_w'], 'L1_attn_wq': _L1_attn_in['wq'], 'L1_attn_wk': _L1_attn_in['wk'], 'L1_attn_wv': _L1_attn_in['wv'], 'L1_attn_w_ig': _L1_attn_in['w_ig'], 'L1_attn_b_ig': _L1_attn_in['b_ig'], 'L1_attn_w_fg': _L1_attn_in['w_fg'], 'L1_attn_b_fg': _L1_attn_in['b_fg'], 'L1_attn_w_og': _L1_attn_in['w_og'], 'L1_attn_mh_w': _L1_attn_in['mh_w'], 'L1_attn_w_out': _L1_attn_in['w_out'], 'L1_attn_norm2_w': _L1_attn_in['norm2_w'], 'L1_attn_w_gate': _L1_attn_in['w_gate'], 'L1_attn_w_up': _L1_attn_in['w_up'], 'L1_attn_w_down': _L1_attn_in['w_down'], 'L1_ffn_gate_w': _L1_ffn_in['gate_w'], 'L1_ffn_w1': _L1_ffn_in['w1'], 'L1_ffn_w2': _L1_ffn_in['w2'], 'L1_ffn_w3': _L1_ffn_in['w3'], 'L1_ffn_sw1': _L1_ffn_in['sw1'], 'L1_ffn_sw2': _L1_ffn_in['sw2'], 'L1_ffn_sw3': _L1_ffn_in['sw3'], 'L1_c': _L1_c, 'L1_wmod': _L1_wmod}
    _x0 = _d['L0_attn_hidden_states']
    _d['L0_attn_hidden_states'] = jax.random.normal(jax.random.fold_in(jax.random.key(seed), 1), (1, 1024, 256), dtype=_x0.dtype)
    del _x0
    return _d

def reference(L0_attn_hidden_states, L0_attn_in_proj_w, L0_attn_conv_w, L0_attn_conv_b, L0_attn_x_proj_w, L0_attn_dt_proj_w, L0_attn_dt_proj_b, L0_attn_A_log, L0_attn_D, L0_attn_out_proj_w, L0_ffn_weight, L0_ffn_gate_w, L0_ffn_A_w, L0_ffn_B_w, L0_c, L0_wmod, L1_attn_norm1_w, L1_attn_wq, L1_attn_wk, L1_attn_wv, L1_attn_w_ig, L1_attn_b_ig, L1_attn_w_fg, L1_attn_b_fg, L1_attn_w_og, L1_attn_mh_w, L1_attn_w_out, L1_attn_norm2_w, L1_attn_w_gate, L1_attn_w_up, L1_attn_w_down, L1_ffn_gate_w, L1_ffn_w1, L1_ffn_w2, L1_ffn_w3, L1_ffn_sw1, L1_ffn_sw2, L1_ffn_sw3, L1_c, L1_wmod):

    def _L0_attn_ref(hidden_states, in_proj_w, conv_w, conv_b, x_proj_w, dt_proj_w, dt_proj_b, A_log, D, out_proj_w):
        import jax, jax.numpy as jnp
        import numpy as np
        B, L, H = (1, 256, 256)
        E, N, K, R = (512, 16, 4, 128)

        def _mamba_mixer(hidden_states, in_proj_w, conv_w, conv_b, x_proj_w, dt_proj_w, dt_proj_b, A_log, D, out_proj_w):
            proj = jnp.einsum('blh,eh->ble', hidden_states, in_proj_w)
            h, gate = jnp.split(proj, 2, axis=-1)
            h_c = h.transpose(0, 2, 1)
            h_c = jax.lax.conv_general_dilated(h_c, conv_w, window_strides=(1,), padding=[(K - 1, 0)], feature_group_count=E, dimension_numbers=('NCH', 'OIH', 'NCH'))
            h_c = h_c + conv_b[None, :, None]
            h = jax.nn.silu(h_c).transpose(0, 2, 1)
            ssm = jnp.einsum('ble,pe->blp', h, x_proj_w)
            dt, Bp, Cp = jnp.split(ssm, [R, R + N], axis=-1)
            dt = jax.nn.softplus(jnp.einsum('blr,er->ble', dt, dt_proj_w) + dt_proj_b)
            A = -jnp.exp(A_log)
            dA = jnp.exp(dt[..., None] * A)
            dBu = (dt * h)[..., None] * Bp[:, :, None, :]

            def step(s, xs):
                dA_t, dBu_t = xs
                s = s * dA_t + dBu_t
                return (s, s)
            s0 = jnp.zeros((h.shape[0], E, N), h.dtype)
            _, states = jax.lax.scan(step, s0, (dA.transpose(1, 0, 2, 3), dBu.transpose(1, 0, 2, 3)))
            y = jnp.einsum('lben,bln->ble', states, Cp)
            y = y + h * D
            y = y * jax.nn.silu(gate)
            return jnp.einsum('ble,he->blh', y, out_proj_w)
        return _mamba_mixer(hidden_states, in_proj_w, conv_w, conv_b, x_proj_w, dt_proj_w, dt_proj_b, A_log, D, out_proj_w)

    def _L0_ffn_ref(x, weight, gate_w, A_w, B_w):
        import jax, jax.numpy as jnp
        import numpy as np
        LORA_ALPHA = 16.0
        TOP_K = 2
        E = gate_w.shape[0]
        out = jnp.einsum('bsh,oh->bso', x, weight)
        logits = jnp.einsum('bsh,eh->bse', x, gate_w)
        probs = jax.nn.softmax(logits, axis=-1)
        topk_w, topk_idx = jax.lax.top_k(probs, TOP_K)
        topk_w = topk_w / jnp.sum(topk_w, axis=-1, keepdims=True)
        onehot = jax.nn.one_hot(topk_idx, E, dtype=x.dtype)
        cw = jnp.einsum('bsk,bske->bse', topk_w, onehot)
        t = jnp.einsum('bsh,erh->bser', x, A_w)
        t = t * cw[..., None]
        lora = jnp.einsum('bser,eor->bso', t, B_w)
        return out + LORA_ALPHA * lora

    def _L1_attn_ref(x, norm1_w, wq, wk, wv, w_ig, b_ig, w_fg, b_fg, w_og, mh_w, w_out, norm2_w, w_gate, w_up, w_down):
        import jax, jax.numpy as jnp
        import numpy as np
        D = 256
        H = 8
        QK = D // 2
        FF = 1024
        CAP = 15.0
        EPS = 1e-06

        def _rmsnorm(x, w, eps=EPS):
            xf = x.astype(jnp.float32)
            var = jnp.mean(xf * xf, axis=-1, keepdims=True)
            return (w * xf * jax.lax.rsqrt(var + eps)).astype(x.dtype)

        def _soft_cap(x, cap=CAP):
            return cap * jnp.tanh(x / cap)

        def _mlstm_parallel(q, k, v, i_pre, f_pre):
            B, Hn, S, dqk = q.shape
            logfg = jax.nn.log_sigmoid(f_pre)
            Fcum = jnp.cumsum(logfg, axis=-1)
            Dmat = Fcum[..., :, None] - Fcum[..., None, :] + i_pre[..., None, :]
            causal = jnp.tril(jnp.ones((S, S), dtype=bool))
            Dmat = jnp.where(causal, Dmat, -jnp.inf)
            m = jnp.max(Dmat, axis=-1, keepdims=True)
            Smat = jnp.exp(Dmat - m)
            qk = jnp.einsum('bhsd,bhtd->bhst', q, k) / jnp.sqrt(jnp.float32(dqk))
            C = qk * Smat
            n = jnp.maximum(jnp.abs(jnp.sum(C, axis=-1, keepdims=True)), jnp.exp(-m))
            h = jnp.einsum('bhst,bhtd->bhsd', C / n, v)
            return h
        B, S, _ = x.shape
        dqk, dv = (QK // H, D // H)
        h_in = _rmsnorm(x, norm1_w)
        q = (h_in @ wq).reshape(B, S, H, dqk).transpose(0, 2, 1, 3)
        k = (h_in @ wk).reshape(B, S, H, dqk).transpose(0, 2, 1, 3)
        v = (h_in @ wv).reshape(B, S, H, dv).transpose(0, 2, 1, 3)
        o_pre = h_in @ w_og
        i_pre = _soft_cap(h_in @ w_ig + b_ig).transpose(0, 2, 1)
        f_pre = _soft_cap(h_in @ w_fg + b_fg).transpose(0, 2, 1)
        h = _mlstm_parallel(q, k, v, i_pre, f_pre)
        h = h.transpose(0, 2, 1, 3)
        hf = h.astype(jnp.float32)
        var = jnp.mean(hf * hf, axis=-1, keepdims=True)
        h_norm = hf * jax.lax.rsqrt(var + EPS) * mh_w.reshape(H, dv)
        h_norm = h_norm.reshape(B, S, D)
        h_out = jax.nn.sigmoid(o_pre) * h_norm
        x1 = x + h_out @ w_out
        h2 = _rmsnorm(x1, norm2_w)
        mlp = jax.nn.silu(h2 @ w_gate) * (h2 @ w_up) @ w_down
        return x1 + mlp

    def _L1_ffn_ref(x, gate_w, w1, w2, w3, sw1, sw2, sw3):
        import jax, jax.numpy as jnp
        import numpy as np
        TOPK = 2

        def _mlp(x, w1, w2, w3):
            a = jnp.dot(x, w1.T).astype(jnp.float32)
            b = jnp.dot(x, w3.T).astype(jnp.float32)
            h = (jax.nn.silu(a) * b).astype(x.dtype)
            return jnp.dot(h, w2.T)
        B, S, D = x.shape
        E = gate_w.shape[0]
        xf = x.reshape(-1, D)
        T = xf.shape[0]
        scores = jax.nn.sigmoid(jnp.dot(xf.astype(jnp.float32), gate_w.T))
        topv, topi = jax.lax.top_k(scores, TOPK)
        topv = topv / topv.sum(axis=-1, keepdims=True)
        dw = jnp.zeros((T, E), jnp.float32).at[jnp.arange(T)[:, None], topi].add(topv)
        y0 = _mlp(xf, sw1, sw2, sw3).astype(jnp.float32)

        def step(y, ws):
            e1, e2, e3, we = ws
            out = _mlp(xf, e1, e2, e3).astype(jnp.float32)
            return (y + out * we[:, None], None)
        y, _ = jax.lax.scan(step, y0, (w1, w2, w3, dw.T))
        return y.astype(x.dtype).reshape(B, S, D)
    x = L0_attn_hidden_states
    mod = (_silu(L0_c) @ L0_wmod).reshape(L0_c.shape[0], 6, 1, -1)
    sa, ca, ga, sb, cb, gb = (mod[:, 0], mod[:, 1], mod[:, 2], mod[:, 3], mod[:, 4], mod[:, 5])
    ga = (2 * (ga >= 0) - 1) * jnp.maximum(jnp.abs(ga), 0.25)
    gb = (2 * (gb >= 0) - 1) * jnp.maximum(jnp.abs(gb), 0.25)
    h = _layernorm(x, axis=-1) * (1 + ca) + sa
    x = x + ga * _L0_attn_ref(h, L0_attn_in_proj_w, L0_attn_conv_w, L0_attn_conv_b, L0_attn_x_proj_w, L0_attn_dt_proj_w, L0_attn_dt_proj_b, L0_attn_A_log, L0_attn_D, L0_attn_out_proj_w)
    h = _layernorm(x, axis=-1) * (1 + cb) + sb
    x = x + gb * _L0_ffn_ref(h, L0_ffn_weight, L0_ffn_gate_w, L0_ffn_A_w, L0_ffn_B_w)
    mod = (_silu(L1_c) @ L1_wmod).reshape(L1_c.shape[0], 6, 1, -1)
    sa, ca, ga, sb, cb, gb = (mod[:, 0], mod[:, 1], mod[:, 2], mod[:, 3], mod[:, 4], mod[:, 5])
    ga = (2 * (ga >= 0) - 1) * jnp.maximum(jnp.abs(ga), 0.25)
    gb = (2 * (gb >= 0) - 1) * jnp.maximum(jnp.abs(gb), 0.25)
    h = _layernorm(x, axis=-1) * (1 + ca) + sa
    x = x + ga * _L1_attn_ref(h, L1_attn_norm1_w, L1_attn_wq, L1_attn_wk, L1_attn_wv, L1_attn_w_ig, L1_attn_b_ig, L1_attn_w_fg, L1_attn_b_fg, L1_attn_w_og, L1_attn_mh_w, L1_attn_w_out, L1_attn_norm2_w, L1_attn_w_gate, L1_attn_w_up, L1_attn_w_down)
    h = _layernorm(x, axis=-1) * (1 + cb) + sb
    x = x + gb * _L1_ffn_ref(h, L1_ffn_gate_w, L1_ffn_w1, L1_ffn_w2, L1_ffn_w3, L1_ffn_sw1, L1_ffn_sw2, L1_ffn_sw3)
    return x

_drawn_inputs = setup_inputs


def setup_inputs(seed=0):
    import zlib

    import numpy as np

    out = dict(_drawn_inputs(seed))
    spreads = {'L0_attn_D': (1.0, 0.6),
     'L1_attn_norm1_w': (1.0, 0.6),
     'L1_attn_b_ig': (0.0, 2.0),
     'L1_attn_mh_w': (1.0, 0.6),
     'L1_attn_norm2_w': (1.0, 0.6)}
    factors = {'L0_attn_in_proj_w': 8.0,
     'L0_attn_conv_w': 8.0,
     'L0_attn_conv_b': 8.0,
     'L0_attn_x_proj_w': 8.0,
     'L0_attn_dt_proj_w': 8.0,
     'L0_attn_dt_proj_b': 8.0,
     'L0_attn_A_log': 8.0,
     'L0_attn_out_proj_w': 8.0,
     'L1_attn_wq': 6.294,
     'L1_attn_wk': 6.322,
     'L1_attn_wv': 6.313,
     'L1_attn_w_ig': 8.0,
     'L1_attn_w_fg': 200.0,
     'L1_attn_b_fg': 200.0,
     'L1_attn_w_og': 8.0,
     'L1_attn_w_out': 6.296,
     'L1_attn_w_gate': 8.0,
     'L1_attn_w_up': 8.0,
     'L1_attn_w_down': 8.0,
     'L1_ffn_gate_w': 35.587,
     'L1_ffn_w1': 37.57,
     'L1_ffn_w2': 32.783,
     'L1_ffn_w3': 32.839,
     'L1_ffn_sw1': 28.18,
     'L1_ffn_sw2': 24.811,
     'L1_ffn_sw3': 24.648,
     'L0_ffn_gate_w': 8.0,
     'L0_ffn_A_w': 8.0,
     'L0_ffn_B_w': 8.0}
    for name, (base, spread) in spreads.items():
        noise = np.random.default_rng([zlib.crc32(name.encode()), seed]).standard_normal(out[name].shape)
        drawn = base * np.exp(spread * noise) if base else spread * noise
        out[name] = jnp.asarray(drawn.astype(out[name].dtype))
    for name, factor in factors.items():
        out[name] = (out[name] * factor).astype(out[name].dtype)
    return out
```

```python
from contextlib import ExitStack

import concourse.bass as bass
from concourse import mybir

P = 128
T = 1024
D = 256
KC = D // P
TC = T // P
HT = 512
NH = T // HT
HC = HT // P
E = 512
EC = E // P
NS = 16
TAPS = 4
R0 = 128
E0, RL = 8, 16
H, DV = 8, 32
QR = 32
HG = 2
VE = DV + 1
FF = 1024
FC = FF // P
E1 = 16
IC = 25
QD = 32
WS = 64.0
LN_EPS, RMS_EPS = 1e-5, 1e-6
CAP = 15.0

ALU = mybir.AluOpType
ACT = mybir.ActivationFunctionType
AX_X = mybir.AxisListType.X
F32 = mybir.dt.float32
BF16 = mybir.dt.bfloat16
F16 = mybir.dt.float16


def adaln_two_layers(nc, d, out):
    ctx = ExitStack()
    with ctx:
        def sem(name):
            return ctx.enter_context(nc.semaphore(name))

        def sbt(stack, name, shape, dt=F32):
            return stack.enter_context(nc.sbuf_tensor(name, shape, dt))

        x = sbt(ctx, "x", [P, TC, D])
        xn = sbt(ctx, "xn", [P, TC, D])
        hT = sbt(ctx, "hT", [P, KC, T])
        tmpx = sbt(ctx, "tmpx", [P, 2, D])
        ident = sbt(ctx, "ident", [P, P])
        ones = sbt(ctx, "ones", [P, P])
        sel = sbt(ctx, "sel", [P, 2 * NS, P], BF16)
        zero16 = sbt(ctx, "zero16", [P, HT], BF16)
        st = sbt(ctx, "st", [P, TC, 6])
        mv = sbt(ctx, "mv", [P, TC, 2])
        ve = sbt(ctx, "ve", [P, TC])
        sd = sbt(ctx, "sd", [P, TC])
        rs = sbt(ctx, "rs", [P, TC])
        eps = sbt(ctx, "eps", [P, 2])
        cs = sbt(ctx, "cs", [P, 2, KC])
        scs = sbt(ctx, "scs", [P, 2, KC])
        scb = sbt(ctx, "scb", [P, 2, KC, P])
        modc = sbt(ctx, "modc", [P, 2, 4, KC])
        gbc = sbt(ctx, "gbc", [P, 2, 2, D])
        gt1 = sbt(ctx, "gt1", [P, 2, D])
        gt2 = sbt(ctx, "gt2", [P, 2, D])
        small0 = sbt(ctx, "small0", [P, EC, TAPS + 3])
        alog = sbt(ctx, "alog", [P, NS, EC])
        aneg = sbt(ctx, "aneg", [P, NS, EC])
        carry = sbt(ctx, "carry", [P, NS, EC])
        rev = sbt(ctx, "rev", [P, E1])
        small1 = sbt(ctx, "small1", [P, 2, KC])
        wf0 = sbt(ctx, "wf0", [P, KC, D + E0 + P])
        wlb = sbt(ctx, "wlb", [P, D])
        wo0 = sbt(ctx, "wo0", [P, EC, D])
        ffn0_t = xn[:, 0:HC, :].rearrange("p c d -> p (c d)").rearrange("p (c r) -> p c r", r=P)
        ffn0_tT = xn[:, HC:TC, :].rearrange("p c d -> p (c d)")
        sq = xn[:, :, :].rearrange("p c d -> p (c d)").rearrange("p (k t) -> p k t", k=KC)
        hoT = sq
        ffn0_t = xn[:, 0:HC, :].rearrange("p c d -> p (c d)").rearrange("p (c r) -> p c r", r=P)
        ffn0_tT = xn[:, HC:TC, :].rearrange("p c d -> p (c d)")
        sq = xn[:, :, :].rearrange("p c d -> p (c d)").rearrange("p (k t) -> p k t", k=KC)
        hoT = sq
        ffn0_t = xn[:, 0:HC, :].rearrange("p c d -> p (c d)").rearrange("p (c r) -> p c r", r=P)
        ffn0_tT = xn[:, HC:TC, :].rearrange("p c d -> p (c d)")
        sq = xn[:, :, :].rearrange("p c d -> p (c d)").rearrange("p (k t) -> p k t", k=KC)
        hoT = sq
        ffn0_t = xn[:, 0:HC, :].rearrange("p c d -> p (c d)").rearrange("p (c r) -> p c r", r=P)
        ffn0_tT = xn[:, HC:TC, :].rearrange("p c d -> p (c d)")
        sq = xn[:, :, :].rearrange("p c d -> p (c d)").rearrange("p (k t) -> p k t", k=KC)
        hoT = sq
        ffn0_t = xn[:, 0:HC, :].rearrange("p c d -> p (c d)").rearrange("p (c r) -> p c r", r=P)
        ffn0_tT = xn[:, HC:TC, :].rearrange("p c d -> p (c d)")
        sq = xn[:, :, :].rearrange("p c d -> p (c d)").rearrange("p (k t) -> p k t", k=KC)
        hoT = sq
        ffn0_t = xn[:, 0:HC, :].rearrange("p c d -> p (c d)").rearrange("p (c r) -> p c r", r=P)
        ffn0_tT = xn[:, HC:TC, :].rearrange("p c d -> p (c d)")
        sq = xn[:, :, :].rearrange("p c d -> p (c d)").rearrange("p (k t) -> p k t", k=KC)
        hoT = sq
        ffn0_t = xn[:, 0:HC, :].rearrange("p c d -> p (c d)").rearrange("p (c r) -> p c r", r=P)
        ffn0_tT = xn[:, HC:TC, :].rearrange("p c d -> p (c d)")
        sq = xn[:, :, :].rearrange("p c d -> p (c d)").rearrange("p (k t) -> p k t", k=KC)
        hoT = sq
        ffn0_t = xn[:, 0:HC, :].rearrange("p c d -> p (c d)").rearrange("p (c r) -> p c r", r=P)
        ffn0_tT = xn[:, HC:TC, :].rearrange("p c d -> p (c d)")
        sq = xn[:, :, :].rearrange("p c d -> p (c d)").rearrange("p (k t) -> p k t", k=KC)
        hoT = sq
        ffn0_t = xn[:, 0:HC, :].rearrange("p c d -> p (c d)").rearrange("p (c r) -> p c r", r=P)
        ffn0_tT = xn[:, HC:TC, :].rearrange("p c d -> p (c d)")
        sq = xn[:, :, :].rearrange("p c d -> p (c d)").rearrange("p (k t) -> p k t", k=KC)
        hoT = sq
        gl = sbt(ctx, "gl", [P, TC, E1])
        ga_ = sbt(ctx, "ga_", [P, TC, E1])
        gb_ = sbt(ctx, "gb_", [P, TC, E1])
        gc_ = sbt(ctx, "gc_", [P, TC, E1])
        gr = sbt(ctx, "gr", [P, 6, TC])

        mixer = ExitStack()
        win = sbt(mixer, "win", [P, KC, 2 * E])
        wx = sbt(mixer, "wx", [P, EC, R0 + 3 * QD])
        wdt = sbt(mixer, "wdt", [P, E])
        hc = sbt(mixer, "hc", [P, EC, T])
        gate = sbt(mixer, "gate", [P, EC, T])
        dt_ = sbt(mixer, "dt_", [P, EC, T])
        u = sbt(mixer, "u", [P, EC, T])
        bcp = sbt(mixer, "bcp", [P, T], BF16)
        with ExitStack() as first:
            wmod = sbt(first, "wmod", [P, 2, KC, 6 * D])
        with ExitStack() as before:
            hpad = sbt(before, "hpad", [P, EC, T + TAPS - 1])
            cv = sbt(before, "cv", [P, EC, T])
            dtr = sbt(before, "dtr", [P, T])
            bch = sbt(before, "bch", [P, T], BF16)
            bcr = sbt(before, "bcr", [P, T])
        with ExitStack() as during:
            pb = sbt(during, "pb", [P, 4, EC, HT])
            dA = sbt(during, "dA", [P, 2, EC, HT])
            bsb = sbt(during, "bsb", [P, 2, HT])
            csb = sbt(during, "csb", [P, 2, HT])
        mixer.close()

        layer1 = ExitStack()
        w1 = sbt(layer1, "w1", [P, KC, IC * P], BF16)
        w3 = sbt(layer1, "w3", [P, KC, IC * P], BF16)
        w2 = sbt(layer1, "w2", [P, IC, D], BF16)
        selx = sbt(layer1, "selx", [P, IC, P], BF16)
        wg1 = sbt(layer1, "wg1", [P, KC, E1])
        wout1 = sbt(layer1, "wout1", [P, KC, D])
        wg = sbt(layer1, "wg", [P, KC, FF])
        wu = sbt(layer1, "wu", [P, KC, FF])
        sg = sbt(layer1, "sg", [P, TC, D])
        with ExitStack() as attn:
            selr = sbt(attn, "selr", [P, HG, P], BF16)
            bif = sbt(attn, "bif", [P, 2 * H])
            mhw = sbt(attn, "mhw", [P, D])
            qT = sbt(attn, "qT", [P, HG, T])
            kT = sbt(attn, "kT", [P, HG, T])
            vext = sbt(attn, "vext", [P, TC, H, VE])
            zif = sbt(attn, "zif", [P, TC, 2 * H])
            zt = sbt(attn, "zt", [P, TC, 2 * H])
            lw = sbt(attn, "lw", [P, 4, TC, H])
            gp = sbt(attn, "gp", [P, T], BF16)
            agt = sbt(attn, "agt", [P, 3, TC, H])
            rbc = sbt(attn, "rbc", [P, H, TC])
            rrow = sbt(attn, "rrow", [P, HG, TC])
            dec = sbt(attn, "dec", [P, HG, TC])
            wkt = sbt(attn, "wkt", [P, TC, H])
            wqt = sbt(attn, "wqt", [P, TC, H])
            ks = sbt(attn, "ks", [P, TC, H, QR])
            states = sbt(attn, "states", [P, TC, HG, VE])
            nden = sbt(attn, "nden", [P, 3, TC, H])
            with ExitStack() as proj:
                wq = sbt(proj, "wq", [P, KC, HG * P])
                wk = sbt(proj, "wk", [P, KC, HG * P])
                wvif = sbt(proj, "wvif", [P, KC, D + 2 * H])
                wog = sbt(proj, "wog", [P, KC, D])
                hin = sbt(proj, "hin", [P, KC, T])
            with ExitStack() as rows:
                lif = sbt(rows, "lif", [P, 2, TC, 3 * QD])
                rowF = sbt(rows, "rowF", [P, T])
                rowA = sbt(rows, "rowA", [P, T])
                rowG = sbt(rows, "rowG", [P, T])
                rowM = sbt(rows, "rowM", [P, T])
                gh = sbt(rows, "gh", [P, T], BF16)
            with ExitStack() as chunks:
                arg = sbt(chunks, "arg", [P, 2, 4, HG, P])
                pr = sbt(chunks, "pr", [P, 4, HG, P])
                num = sbt(chunks, "num", [P, TC, H, VE])
        with ExitStack() as mlp:
            wd = sbt(mlp, "wd", [P, FC, D])
            x1T = sbt(mlp, "x1T", [P, KC, T])
            h2T = sbt(mlp, "h2T", [P, KC, T])
            sil = sbt(mlp, "sil", [P, 2, T])
            gg = sbt(mlp, "gg", [P, FC, T])
        with ExitStack() as moe:
            h16 = sbt(moe, "h16", [P, 2, KC, T], F16)
            dwx = sbt(moe, "dwx", [P, TC, 3 * QD])
            dwp = sbt(moe, "dwp", [P, T], BF16)
            dwh = sbt(moe, "dwh", [P, T], BF16)
            dwr = sbt(moe, "dwr", [P, T])
            sa_ = sbt(moe, "sa_", [P, 2, HT])
            gh1 = sbt(moe, "gh1", [P, 2, HT])
            g16 = sbt(moe, "g16", [P, 2, 2, HT], F16)
            xo = sbt(moe, "xo", [P, 2, D])
        layer1.close()
        ps = ctx.enter_context(nc.psum_tensor("ps", [P, 8, HT], F32))

        def banks(b, n, rows=P):
            return ps[0:rows, b:b + n, :].rearrange("p b f -> p (b f)")

        def over(ap, shape):
            return ap.broadcast_to(shape)

        ho_head = ks[:].rearrange("p c h n -> p (c h) n")
        ho_tok = ks[:].rearrange("p c h n -> p c (h n)")
        sq_tok = xn[:, :, :].rearrange("p c d -> p (c d)").rearrange("p (a n) -> p a n", n=DV)

        names = """ld_mod ld_x0 ld_x1 ld_const ld_win ld_mix ld_ffn0 ld_attn ld_gateup ld_moe ld_down
            c_silu c_wide mod_mm mod_col gate_vec
            zeroed ones_ready
            ln_var ln_sd ln_norm ln_T ln_h
            in_mm in_evac conv_done hc_ready
            x_mm dtr_ready bc_parts dt_mm sp_exp dt_ready u_ready aexp aneg_ready
            y_zero bcast_ready bsb_ready dA_ready dbu_done scan_done carry_saved cmul_dve cmul_pool sum_done
            y_evac y_gated
            out_mm x_mixed
            f0_mm f0_out soft_arg soft_exp f0_t f0_T f0_tT f0_lora x_ffn0
            sq_ready ss_mm rms_sd hin_ready q_mm k_mm q_sb k_sb v_mm v_sb o_sb z_in z_tanh z_exp z_ln lif_ready lif_T
            sp_rest sp_ln abs_done inter_used z_w v_ones rows_zero sg_ready enm_ready y_gated_a y_gated_b var_ready dwx_zero moe_prod row_parts row_tok tok_T agt_ready rr_mm rr_sb w_arg w_exp kT_T ks_ready state_mm state_done
            s_mm g_mm arg_ready arg_masked e_ready pr_ready inter_mm intra_mm num_ready
            den_ready num_sq var_sd ho_ready ho_T hoT_ready
            wo_mm x1_ready sq2_ready ss2_mm rms2_sd h2_ready gu_mm sil_ready gg_ready down_mm x_attn
            h_hi h_split z1_mm z1_exp dw_ready dw_T dw_parts acc_zero up_mm moe_sil g_ready ghi_ready glo_ready acc_mm
            x_out stored act_step dve_step pool_step""".split()
        s = {n: sem(n) for n in names}

        block = ctx.enter_context(nc.Block())

        @block.sync
        def _(sp):
            def load(dst, name, signal):
                sp.dma_start(dst, d[name]).then_inc(s[signal], 16)

            xv = d["x"].rearrange("(c p) f -> p c f", p=P)
            sp.dma_start(x[:, 0:HC, :], xv[:, 0:HC, :]).then_inc(s["ld_x0"], 16)
            sp.dma_start(x[:, HC:TC, :], xv[:, HC:TC, :]).then_inc(s["ld_x1"], 16)
            load(ident[:], "ident", "ld_const")
            load(sel[:], "sel", "ld_const")
            load(rev[:], "rev", "ld_const")
            load(small1[:], "norm_w", "ld_const")
            load(win[:], "win", "ld_win")
            load(small0[:], "small0", "ld_mix")
            load(alog[:], "alog", "ld_mix")
            load(wx[:], "wx", "ld_mix")
            load(wdt[:], "wdt", "ld_mix")
            load(wo0[:], "wo0", "ld_ffn0")
            load(wf0[:], "wf0", "ld_ffn0")
            load(wlb[:], "wlb", "ld_ffn0")
            sp.wait_ge(s["out_mm"], TC)
            for dst, name in ((wq, "wq"), (wk, "wk"), (wvif, "wvif"), (wog, "wog"), (selr, "selr"), (bif, "bif"),
                              (mhw, "mhw"), (wout1, "wout1")):
                load(dst[:], name, "ld_attn")
            load(wg[:], "wg", "ld_gateup")
            load(wu[:], "wu", "ld_gateup")
            for dst, name in ((w1, "w1"), (w3, "w3"), (w2, "w2"), (selx, "selx"), (wg1, "wg1")):
                load(dst[:], name, "ld_moe")
            sp.wait_ge(s["hoT_ready"], 4)
            load(wd[:], "wd", "ld_down")
            ov = out.rearrange("(c p) f -> p c f", p=P)
            for th in range(NH):
                sp.wait_ge(s["x_out"], th + 1)
                sp.dma_start(ov[:, th * HC:(th + 1) * HC, :], x[:, th * HC:(th + 1) * HC, :]).then_inc(s["stored"], 16)
            sp.wait_ge(s["stored"], 16 * NH)

        @block.tensor
        def _(pe):
            mm = nc.tensor.matmul

            def clear(b):
                return mm(ps[:, b, :], zero16[:, 0:P], zero16[:, :], start=True, stop=False)

            pe.wait_ge(s["ld_mod"], 48)
            pe.wait_ge(s["c_silu"], 1)
            for l in range(2):
                for n, part in enumerate((0, 1, 3, 4)):
                    for f in range(KC):
                        col = (l * 4 + n) * KC + f
                        for k in range(KC):
                            lo = part * D + f * P
                            mm(ps[:, 0, col:col + 1], wmod[:, l, k, lo:lo + P], scs[:, l, k:k + 1],
                               start=k == 0, stop=k == KC - 1)
            pe.wait_ge(s["c_wide"], 1)
            for l in range(2):
                for k in range(KC):
                    gates = wmod[:, l, k, :].rearrange("p (a b f) -> p a b f", a=2, b=3)[:, :, 2, :]
                    last = mm(ps[:, 1 + l, :], scb[:, l, k, :], gates, start=k == 0, stop=k == KC - 1)
            last.then_inc(s["mod_mm"], 1)

            def ln_transposes(n):
                for th in range(NH):
                    pe.wait_ge(s["ln_norm"], TC * n + HC * (th + 1))
                    for k in range(KC):
                        for c in range(HC):
                            last = nc.tensor.transpose(ps[:, 2 * k + th, c * P:(c + 1) * P],
                                                       xn[:, th * HC + c, k * P:(k + 1) * P], ident[:])
                    last.then_inc(s["ln_T"], 1)

            pe.wait_ge(s["ld_const"], 64)
            pe.wait_ge(s["ones_ready"], 3)
            pe.wait_ge(s["gate_vec"], 1)
            ln_transposes(0)

            pe.wait_ge(s["ln_h"], 4)
            pe.wait_ge(s["ld_win"], 16)
            for g in range(2 * EC):
                b = 2 * ((g + 2) % 4)
                if g >= 4:
                    pe.wait_ge(s["in_evac"], g - 3)
                for th in range(NH):
                    for k in range(KC):
                        last = mm(ps[:, b + th, :], win[:, k, g * P:(g + 1) * P], hT[:, k, th * HT:(th + 1) * HT],
                                  start=k == 0, stop=k == KC - 1)
                last.then_inc(s["in_mm"], 1)

            pe.wait_ge(s["in_evac"], 2 * EC)
            pe.wait_ge(s["ld_mix"], 64)
            for j in range(EC):
                pe.wait_ge(s["hc_ready"], j + 1)
                for th in range(NH):
                    rhs = hc[:, j, th * HT:(th + 1) * HT]
                    mm(ps[:, th, :], wx[:, j, 0:R0], rhs, start=j == 0, stop=j == EC - 1)
                    last = mm(ps[0:3 * QD, 2 + th, :], wx[:, j, R0:R0 + 3 * QD], rhs, start=j == 0, stop=j == EC - 1)
            last.then_inc(s["x_mm"], 1)

            pe.wait_ge(s["dtr_ready"], 1)
            for j, b in enumerate((4, 6, 0, 2)):
                if b == 2:
                    pe.wait_ge(s["bc_parts"], 1)
                for th in range(NH):
                    last = mm(ps[:, b + th, :], wdt[:, j * P:(j + 1) * P], dtr[:, th * HT:(th + 1) * HT],
                              start=True, stop=True)
                last.then_inc(s["dt_mm"], 1)

            pe.wait_ge(s["bc_parts"], 1)
            for th in range(NH):
                half = bcp[:, th * HT:(th + 1) * HT]
                if th == 0:
                    pe.wait_ge(s["dt_ready"], EC)
                else:
                    pe.wait_ge(s["y_evac"], th)
                for j in range(EC):
                    clear(j)

                def bcast(n, r):
                    mm(ps[:, 4 + r % 2, :], sel[:, n, :], half, start=True, stop=True)
                    mm(ps[:, 6 + r % 2, :], sel[:, n + NS, :], half, start=True, stop=True)\
                        .then_inc(s["bcast_ready"], 1)

                def sums(it, r, last_one):
                    pe.wait_ge(s["cmul_dve"], it + 1)
                    pe.wait_ge(s["cmul_pool"], it + 1)
                    for j in range(EC):
                        last = mm(ps[:, j, :], ident[:], pb[:, r, j, :], start=False, stop=last_one)
                    last.then_inc(s["sum_done"], 1)

                for n in range(2):
                    if th:
                        pe.wait_ge(s["bsb_ready"], NS * th + n - 1)
                        pe.wait_ge(s["cmul_dve"], NS * th + n - 1)
                    bcast(n, n)

                def group(i, last_group):
                    for r in range(4):
                        n = 4 * i + r
                        it = NS * th + n
                        if not (last_group and r >= 2):
                            pe.wait_ge(s["bsb_ready"], it + 1)
                            pe.wait_ge(s["cmul_dve"], it + 1)
                            bcast(n + 2, r)
                        sums(it, r, last_group and r == 3)

                with pe.Fori(0, NS // 4 - 1) as i:
                    group(i, False)
                group(NS // 4 - 1, True)

            pe.wait_ge(s["ld_ffn0"], 48)
            for c in range(TC):
                if c == 0:
                    pe.wait_ge(s["y_gated_a"], 1)
                if c == HC:
                    pe.wait_ge(s["y_gated_b"], 1)
                for j in range(EC):
                    last = mm(ps[:, (4 + c) % 8, 0:D], hc[:, j, c * P:(c + 1) * P], wo0[:, j, :],
                              start=j == 0, stop=j == EC - 1)
                last.then_inc(s["out_mm"], 1)

            ln_transposes(1)
            pe.wait_ge(s["ln_h"], 8)
            for c in range(TC):
                for k in range(KC):
                    last = mm(ps[:, 4 + c // 2, (c % 2) * 136:(c % 2) * 136 + 136], hT[:, k, c * P:(c + 1) * P],
                              wf0[:, k, D:D + E0 + P], start=k == 0, stop=k == KC - 1)
            last.then_inc(s["f0_mm"], 1)
            for c in range(TC):
                if c % 2 == 0:
                    clear(c // 2)
                for k in range(KC):
                    mm(ps[:, c // 2, (c % 2) * D:(c % 2 + 1) * D], hT[:, k, c * P:(c + 1) * P], wf0[:, k, 0:D],
                       start=False, stop=False)
            pe.wait_ge(s["f0_t"], 1)
            for c in range(TC):
                last = nc.tensor.transpose(ps[:, 4 + c // HC, (c % HC) * P:(c % HC + 1) * P], ffn0_t[:, c, :], ident[:])
            last.then_inc(s["f0_T"], 1)
            pe.wait_ge(s["f0_tT"], 1)
            for c in range(TC):
                last = mm(ps[:, c // 2, (c % 2) * D:(c % 2 + 1) * D], ffn0_tT[:, c * P:(c + 1) * P], wlb[:, :],
                          start=False, stop=c % 2 == 1)
            last.then_inc(s["f0_lora"], 1)

            ln_transposes(2)

            def feature_sums(b):
                for th in range(NH):
                    for k in range(KC):
                        last = mm(ps[:, b + th, :], ones[:], sq[:, k, th * HT:(th + 1) * HT],
                                  start=k == 0, stop=k == KC - 1)
                return last

            pe.wait_ge(s["sq_ready"], KC)
            feature_sums(4).then_inc(s["ss_mm"], 1)
            pe.wait_ge(s["hin_ready"], KC)
            pe.wait_ge(s["ld_attn"], 8 * 16)
            for w, b, done in ((wq, 0, s["q_mm"]), (wk, 4, s["k_mm"])):
                for g in range(HG):
                    for th in range(NH):
                        for k in range(KC):
                            last = mm(ps[:, b + 2 * g + th, :], w[:, k, g * P:(g + 1) * P],
                                      hin[:, k, th * HT:(th + 1) * HT], start=k == 0, stop=k == KC - 1)
                    last.then_inc(done, 1)
            for c in range(TC):
                b = 2 * (c % 4)
                if c == 0:
                    pe.wait_ge(s["q_sb"], HG)
                elif c == 2:
                    pe.wait_ge(s["k_sb"], HG)
                elif c >= 4:
                    pe.wait_ge(s["v_sb"], c - 3)
                    pe.wait_ge(s["o_sb"], c - 3)
                for k in range(KC):
                    mm(ps[:, b, 0:D + 2 * H], hin[:, k, c * P:(c + 1) * P], wvif[:, k, :], start=k == 0, stop=k == KC - 1)
                for k in range(KC):
                    last = mm(ps[:, b + 1, 0:D], hin[:, k, c * P:(c + 1) * P], wog[:, k, :], start=k == 0, stop=k == KC - 1)
                last.then_inc(s["v_mm"], 1)
            pe.wait_ge(s["lif_ready"], 1)
            pe.wait_ge(s["o_sb"], TC)
            for a in range(2):
                for c in range(TC):
                    last = nc.tensor.transpose(ps[0:3 * QD, 2 * a + c // HC, (c % HC) * P:(c % HC + 1) * P],
                                               lif[:, a, c, :], ident[:])
            last.then_inc(s["lif_T"], 1)
            pe.wait_ge(s["row_tok"], 1)
            for a, row in enumerate((rowA, rowG, rowM)):
                for c in range(TC):
                    col = (a * TC + c) * H
                    last = nc.tensor.transpose(ps[:, 4, col:col + H], row[0:H, c * P:(c + 1) * P], ident[0:H, 0:H])
            last.then_inc(s["tok_T"], 1)
            pe.wait_ge(s["row_parts"], 1)
            ends = gp[:, P - 1:T:P]
            for h in range(H):
                mm(ps[:, 5, h * TC:(h + 1) * TC], sel[:, h, :], ends, start=True, stop=True)
            for g in range(HG):
                last = mm(ps[:, 5, (H + g) * TC:(H + g + 1) * TC], selr[:, g, :], ends, start=True, stop=True)
            last.then_inc(s["rr_mm"], 1)
            for c in range(TC):
                for g in range(HG):
                    col = (c % 2) * D + g * P
                    last = nc.tensor.transpose(ps[:, c // 2, col:col + P], kT[:, g, c * P:(c + 1) * P], ident[:])
            last.then_inc(s["kT_T"], 1)
            for c in range(TC):
                if c % 2 == 0:
                    pe.wait_ge(s["ks_ready"], c // 2 + 1)
                for h in range(H):
                    g, r = h // 4, h % 4
                    col = (c % 4) * HG * VE + g * VE
                    last = mm(ps[QD * r:QD * (r + 1), 6 + c // 4, col:col + VE], ks[:, c, h, :], vext[:, c, h, :],
                              start=True, stop=True)
                last.then_inc(s["state_mm"], 1)

            def g_rows(c):
                if c:
                    pe.wait_ge(s["arg_ready"], c)
                for r in range(4):
                    for g in range(HG):
                        col = (r % 2) * D + g * P
                        last = mm(ps[:, 4 + r // 2, col:col + P], sel[:, 4 * g + r, :], gp[:, c * P:(c + 1) * P],
                                  start=True, stop=True)
                last.then_inc(s["g_mm"], 1)

            def scores(c):
                if c:
                    pe.wait_ge(s["inter_used"], c)
                    pe.wait_ge(s["state_done"], c)
                for g in range(HG):
                    for r in range(4):
                        rows = slice(QD * r, QD * (r + 1))
                        last = mm(ps[:, r, g * P:(g + 1) * P], kT[rows, g, c * P:(c + 1) * P],
                                  qT[rows, g, c * P:(c + 1) * P], start=True, stop=True)
                if c:
                    for g in range(HG):
                        for r in range(4):
                            rows = slice(QD * r, QD * (r + 1))
                            col = D + g * VE
                            last = mm(ps[:, r, col:col + VE], qT[rows, g, c * P:(c + 1) * P],
                                      states[rows, c - 1, g, :], start=True, stop=True)
                last.then_inc(s["s_mm"], 1)

            def intra(c):
                pe.wait_ge(s["pr_ready"], c + 1)
                if c == 0:
                    pe.wait_ge(s["state_done"], TC - 1)
                if c >= 2:
                    pe.wait_ge(s["num_ready"], c - 1)
                for h in range(H):
                    last = mm(ps[:, 6 + c % 2, h * VE:(h + 1) * VE], pr[:, h % 4, h // 4, :], vext[:, c, h, :],
                              start=True, stop=True)
                last.then_inc(s["intra_mm"], 1)

            pe.wait_ge(s["ks_ready"], 4)
            pe.wait_ge(s["w_exp"], 1)
            g_rows(0)
            for c in range(TC):
                scores(c)
                if c + 1 < TC:
                    g_rows(c + 1)
                intra(c)

            for th in range(NH):
                pe.wait_ge(s["ho_ready"], th + 1)
                for k in range(KC):
                    for c in range(HC):
                        last = nc.tensor.transpose(ps[:, 2 * k + th, c * P:(c + 1) * P],
                                                   ho_tok[:, th * HC + c, k * P:(k + 1) * P], ident[:])
                last.then_inc(s["ho_T"], 1)
            pe.wait_ge(s["hoT_ready"], 4)
            for m in range(KC):
                for th in range(NH):
                    for k in range(KC):
                        last = mm(ps[:, 4 + 2 * m + th, :], wout1[:, k, m * P:(m + 1) * P],
                                  hoT[:, k, th * HT:(th + 1) * HT], start=k == 0, stop=k == KC - 1)
                last.then_inc(s["wo_mm"], 1)
            pe.wait_ge(s["sq2_ready"], KC)
            feature_sums(0).then_inc(s["ss2_mm"], 1)

            pe.wait_ge(s["h2_ready"], KC)
            pe.wait_ge(s["ld_gateup"], 32)
            for f in range(FC):
                b = 4 * (f % 2)
                if f >= 2:
                    pe.wait_ge(s["gg_ready"], f - 1)
                for w, o in ((wg, 0), (wu, 2)):
                    for th in range(NH):
                        for k in range(KC):
                            last = mm(ps[:, b + o + th, :], w[:, k, f * P:(f + 1) * P], h2T[:, k, th * HT:(th + 1) * HT],
                                      start=k == 0, stop=k == KC - 1)
                last.then_inc(s["gu_mm"], 1)
            pe.wait_ge(s["ld_down"], 16)
            pe.wait_ge(s["gg_ready"], FC)
            for c in range(TC):
                clear(c)
                for k in range(KC):
                    mm(ps[:, c, k * P:(k + 1) * P], x1T[:, k, c * P:(c + 1) * P], ident[:], start=False, stop=False)
                for f in range(FC):
                    last = mm(ps[:, c, 0:D], gg[:, f, c * P:(c + 1) * P], wd[:, f, :], start=False, stop=f == FC - 1)
                last.then_inc(s["down_mm"], 1)

            ln_transposes(3)
            pe.wait_ge(s["ln_h"], 16)
            pe.wait_ge(s["ld_moe"], 80)
            for c in range(TC):
                for k in range(KC):
                    last = mm(ps[:, 4, c * E1:(c + 1) * E1], hT[:, k, c * P:(c + 1) * P], wg1[:, k, :],
                              start=k == 0, stop=k == KC - 1)
            last.then_inc(s["z1_mm"], 1)
            pe.wait_ge(s["dw_ready"], 1)
            for c in range(TC):
                last = nc.tensor.transpose(ps[0:3 * QD, 6 + c // HC, (c % HC) * P:(c % HC + 1) * P], dwx[:, c, :], ident[:])
            last.then_inc(s["dw_T"], 1)
            pe.wait_ge(s["dw_parts"], 1)
            pe.wait_ge(s["h_split"], 1)
            for th in range(NH):
                half = slice(th * HT, (th + 1) * HT)

                def up(ic, r):
                    for w, b in ((w1, 2), (w3, 4)):
                        for k in range(KC):
                            for part in range(2):
                                mm(ps[:, b + r, :], w[:, k, bass.ts(ic, P)], h16[:, part, k, half],
                                   start=(k == 0 and part == 0), stop=(k == KC - 1 and part == 1))
                    mm(ps[:, 6 + r, :], selx[:, ic, :], dwp[:, half], start=True, stop=True).then_inc(s["up_mm"], 1)

                def down(ic, r, last_one):
                    pe.wait_ge(s["glo_ready"], IC * th + ic + 1)
                    for c in range(HC):
                        for part in range(2):
                            last = mm(ps[:, c // 2, (c % 2) * D:(c % 2 + 1) * D], g16[:, r, part, c * P:(c + 1) * P],
                                      w2[:, ic, :], start=False,
                                      stop=last_one and c % 2 == 1 and part == 1)
                    last.then_inc(s["acc_mm"], 1)

                if th:
                    pe.wait_ge(s["g_ready"], IC * th)
                    pe.wait_ge(s["x_out"], th)
                for b in range(2):
                    clear(b)
                def pair(i, first):
                    for r in range(2):
                        if not (first and r == 0):
                            pe.wait_ge(s["g_ready"], IC * th + 2 * i + r)
                        up(2 * i + r + 1, 1 - r)
                        down(2 * i + r, r, False)

                up(0, 0)
                if th == 0:
                    pair(0, True)
                with pe.Fori(1 if th == 0 else 0, IC // 2) as i:
                    pair(i, False)
                down(IC - 1, 0, True)

        @block.scalar
        def _(act):
            A = nc.scalar.activation
            step = [0]

            def then(ins):
                step[0] += 1
                ins.then_inc(s["act_step"], 1)
                act.wait_ge(s["act_step"], step[0])

            act.dma_start(cs[:], d["c"]).then_inc(s["ld_mod"], 16)
            for l in range(2):
                act.dma_start(wmod[:, l], d["wmod"][l]).then_inc(s["ld_mod"], 16)
            act.wait_ge(s["ld_mod"], 48)
            A(scs[:], cs[:], ACT.Silu).then_inc(s["c_silu"], 1)

            def layernorm(n, layer, shift, scale):
                act.wait_ge(s["ln_var"], n + 1)
                A(sd[:], ve[:], ACT.Sqrt).then_inc(s["ln_sd"], 1)
                for th in range(NH):
                    act.wait_ge(s["ln_T"], NH * n + th + 1)
                    for k in range(KC):
                        A(hT[:, k, th * HT:(th + 1) * HT], ps[:, 2 * k + th, :], ACT.Identity,
                          bias=modc[:, layer, shift, k:k + 1], scale=modc[:, layer, scale, k:k + 1])\
                            .then_inc(s["ln_h"], 1)

            act.wait_ge(s["mod_col"], 1)
            layernorm(0, 0, 0, 1)
            act.wait_ge(s["zeroed"], 3)
            for g in range(EC):
                act.wait_ge(s["in_mm"], g + 1)
                A(hpad[:, g, TAPS - 1:], banks(2 * ((g + 2) % 4), 2), ACT.Copy).then_inc(s["in_evac"], 1)
            for g in range(EC, 2 * EC):
                act.wait_ge(s["in_mm"], g + 1)
                A(gate[:, g - EC, :], banks(2 * ((g + 2) % 4), 2), ACT.Silu).then_inc(s["in_evac"], 1)
            for j in range(EC):
                act.wait_ge(s["conv_done"], j + 1)
                A(hc[:, j, :], cv[:, j, :], ACT.Silu).then_inc(s["hc_ready"], 1)
            act.wait_ge(s["ld_mix"], 64)
            then(A(alog[:], alog[:], ACT.Exp))
            nc.scalar.mul(aneg[:], alog[:], -1.0).then_inc(s["aneg_ready"], 1)
            act.wait_ge(s["x_mm"], 1)
            A(dtr[:], banks(0, 2), ACT.Copy).then_inc(s["dtr_ready"], 1)
            for j, b in enumerate((4, 6, 0, 2)):
                act.wait_ge(s["dt_mm"], j + 1)
                A(cv[:, j, :], banks(b, 2), ACT.Abs, bias=small0[:, j, 5:6]).then_inc(s["abs_done"], 1)
            act.wait_ge(s["abs_done"], EC)
            for j in range(EC):
                A(cv[:, j, :], cv[:, j, :], ACT.Exp, scale=-1.0).then_inc(s["sp_exp"], 1)
            for j in range(EC):
                act.wait_ge(s["sp_rest"], j + 1)
                A(hpad[:, j, 0:T], hpad[:, j, 0:T], ACT.Ln).then_inc(s["sp_ln"], 1)

            act.wait_ge(s["dt_ready"], EC)
            act.wait_ge(s["u_ready"], EC)
            act.wait_ge(s["aneg_ready"], 1)
            for th in range(NH):
                half = slice(th * HT, (th + 1) * HT)

                def group(i, first):
                    for r in range(4):
                        it = NS * th + 4 * i + r
                        free = not (first and r < 2)
                        if free:
                            act.wait_ge(s["scan_done"], it - 1)
                        for j in range(EC):
                            last = A(dA[:, r % 2, j, :], dt_[:, j, half], ACT.Exp, scale=aneg[:, 4 * i + r, j:j + 1])
                        last.then_inc(s["dA_ready"], 1)
                        act.wait_ge(s["bcast_ready"], it + 1)
                        if free:
                            act.wait_ge(s["dbu_done"], it - 1)
                        A(bsb[:, r % 2, :], ps[:, 4 + r % 2, :], ACT.Copy)
                        if free:
                            act.wait_ge(s["cmul_pool"], it - 1)
                        A(csb[:, r % 2, :], ps[:, 6 + r % 2, :], ACT.Copy).then_inc(s["bsb_ready"], 1)

                if th == 0:
                    group(0, True)
                with act.Fori(1 if th == 0 else 0, NS // 4) as i:
                    group(i, False)

            layernorm(1, 0, 2, 3)
            act.wait_ge(s["soft_arg"], 1)
            A(ga_[:, :, 0:E0], gl[:, :, 0:E0], ACT.Exp).then_inc(s["soft_exp"], 1)
            act.wait_ge(s["f0_T"], 1)
            A(ffn0_tT, banks(4, 2), ACT.Copy).then_inc(s["f0_tT"], 1)

            layernorm(2, 1, 0, 1)
            act.wait_ge(s["ln_h"], 12)
            for k in range(KC):
                A(sq[:, k, :], hT[:, k, :], ACT.Square).then_inc(s["sq_ready"], 1)
            act.wait_ge(s["ss_mm"], 1)
            A(kT[:, 0, :], banks(4, 2), ACT.Sqrt, scale=1.0 / D, bias=eps[:, 0:1]).then_inc(s["rms_sd"], 1)
            for g in range(HG):
                act.wait_ge(s["q_mm"], g + 1)
                nc.scalar.mul(qT[:, g, :], banks(2 * g, 2), 0.25).then_inc(s["q_sb"], 1)
            for c in range(TC):
                act.wait_ge(s["v_mm"], c + 1)
                A(sg[:, c, :], ps[:, 2 * (c % 4) + 1, 0:D], ACT.Sigmoid).then_inc(s["o_sb"], 1)
            act.wait_ge(s["z_in"], TC)
            A(zt[:], zif[:], ACT.Tanh, scale=1.0 / CAP).then_inc(s["z_tanh"], 1)
            act.wait_ge(s["z_tanh"], 1)
            A(lw[:, 0], zt[:, :, H:2 * H], ACT.Exp, scale=-CAP).then_inc(s["z_exp"], 1)
            act.wait_ge(s["z_w"], 1)
            A(lw[:, 2], lw[:, 1], ACT.Ln).then_inc(s["z_ln"], 1)
            act.wait_ge(s["tok_T"], 1)
            A(agt[:, 2].rearrange("p c h -> p (c h)"), ps[:, 4, 2 * TC * H:3 * TC * H], ACT.Exp, scale=-1.0)\
                .then_inc(s["enm_ready"], 1)
            act.wait_ge(s["w_arg"], 1)
            A(wkt[:], wkt[:], ACT.Exp)
            A(wqt[:, 1:], wqt[:, 1:], ACT.Exp)
            A(dec[:, :, 1:], dec[:, :, 1:], ACT.Exp).then_inc(s["w_exp"], 1)
            for c in range(TC):
                act.wait_ge(s["arg_masked"], c + 1)
                A(arg[:, c % 2], arg[:, c % 2], ACT.Exp).then_inc(s["e_ready"], 1)
            act.wait_ge(s["den_ready"], 1)
            A(sq_tok, ho_head, ACT.Square).then_inc(s["num_sq"], 1)
            act.wait_ge(s["var_ready"], 1)
            A(nden[:, 2], nden[:, 1], ACT.Sqrt, scale=1.0 / DV, bias=eps[:, 0:1]).then_inc(s["var_sd"], 1)
            for th in range(NH):
                act.wait_ge(s["ho_T"], th + 1)
                for k in range(KC):
                    A(hoT[:, k, th * HT:(th + 1) * HT], ps[:, 2 * k + th, :], ACT.Copy).then_inc(s["hoT_ready"], 1)
            for k in range(KC):
                act.wait_ge(s["x1_ready"], k + 1)
                if k == 0:
                    act.wait_ge(s["wo_mm"], KC)
                A(sq[:, k, :], x1T[:, k, :], ACT.Square).then_inc(s["sq2_ready"], 1)
            act.wait_ge(s["ss2_mm"], 1)
            A(sil[:, 0, :], banks(0, 2), ACT.Sqrt, scale=1.0 / D, bias=eps[:, 0:1]).then_inc(s["rms2_sd"], 1)
            act.wait_ge(s["h2_ready"], KC)
            for f in range(FC):
                act.wait_ge(s["gu_mm"], f + 1)
                if f >= 2:
                    act.wait_ge(s["gg_ready"], f - 1)
                A(sil[:, f % 2, :], banks(4 * (f % 2), 2), ACT.Silu).then_inc(s["sil_ready"], 1)

            layernorm(3, 1, 2, 3)
            act.wait_ge(s["z1_mm"], 1)
            A(ga_[:].rearrange("p c e -> p (c e)"), ps[:, 4, 0:TC * E1], ACT.Exp, scale=-1.0).then_inc(s["z1_exp"], 1)
            for th in range(NH):
                def silu(ic, r, first):
                    m = IC * th + ic
                    act.wait_ge(s["up_mm"], m + 1)
                    if not first:
                        act.wait_ge(s["g_ready"], m - 1)
                    A(sa_[:, r, :], ps[:, 2 + r, :], ACT.Silu).then_inc(s["moe_sil"], 1)

                silu(0, 0, th == 0)
                if th == 0:
                    silu(1, 1, True)
                    silu(2, 0, False)
                with act.Fori(1 if th == 0 else 0, IC // 2) as i:
                    silu(2 * i + 1, 1, False)
                    silu(2 * i + 2, 0, False)

        @block.gpsimd
        def _(pool):
            tt = nc.gpsimd.tensor_tensor
            nc.gpsimd.memset(ones[:], 1.0).then_inc(s["ones_ready"], 1)
            nc.gpsimd.memset(zero16[:], 0.0).then_inc(s["ones_ready"], 1)
            nc.gpsimd.memset(eps[:], RMS_EPS).then_inc(s["ones_ready"], 1)
            pool.wait_ge(s["mod_mm"], 1)
            nc.gpsimd.memset(hpad[:, :, 0:TAPS - 1], 0.0).then_inc(s["zeroed"], 1)
            pool.wait_ge(s["zeroed"], 1)
            nc.gpsimd.memset(bcp[3 * QD:P, :], 0.0).then_inc(s["zeroed"], 1)
            pool.wait_ge(s["zeroed"], 2)
            nc.gpsimd.memset(carry[:], 0.0).then_inc(s["zeroed"], 1)
            pool.wait_ge(s["zeroed"], 3)
            for j in range(EC):
                pool.wait_ge(s["dt_ready"], j + 1)
                tt(u[:, j, :], dt_[:, j, :], hc[:, j, :], ALU.mult).then_inc(s["u_ready"], 1)
            pool.wait_ge(s["u_ready"], EC)

            for th in range(NH):
                half = slice(th * HT, (th + 1) * HT)

                def dbu(it, r, first):
                    pool.wait_ge(s["bsb_ready"], it + 1)
                    if not first:
                        pool.wait_ge(s["sum_done"], it - 3)
                    tt(pb[:, r], u[:, :, half], over(bsb[:, r % 2, :].unsqueeze(1), [P, EC, HT]), ALU.mult)\
                        .then_inc(s["dbu_done"], 1)

                def cmul(it, r):
                    if th == 0:
                        pool.wait_ge(s["carry_saved"], it + 1)
                    else:
                        pool.wait_ge(s["scan_done"], it + 1)
                    tt(pb[:, r, EC - 1, :], pb[:, r, EC - 1, :], csb[:, r % 2, :], ALU.mult).then_inc(s["cmul_pool"], 1)

                def group(i, first, last_group):
                    for r in range(4):
                        it = NS * th + 4 * i + r
                        if not (last_group and r == 3):
                            dbu(it + 1, (r + 1) % 4, first and r < 3)
                        cmul(it, r)

                dbu(NS * th, 0, th == 0)
                if th == 0:
                    group(0, True, False)
                with pool.Fori(1 if th == 0 else 0, NS // 4 - 1) as i:
                    group(i, False, False)
                group(NS // 4 - 1, False, True)
            pool.wait_ge(s["y_evac"], 1)
            tt(hc[:, :, 0:HT], hc[:, :, 0:HT], gate[:, :, 0:HT], ALU.mult).then_inc(s["y_gated_a"], 1)

            pool.wait_ge(s["out_mm"], TC)
            nc.gpsimd.memset(vext[:, :, :, DV:VE], 1.0).then_inc(s["v_ones"], 1)
            pool.wait_ge(s["v_ones"], 1)
            nc.gpsimd.memset(gp[3 * QD:P, :], 0.0).then_inc(s["v_ones"], 1)
            pool.wait_ge(s["v_ones"], 2)
            pool.wait_ge(s["v_mm"], TC)
            nc.gpsimd.memset(lif[:], 0.0).then_inc(s["rows_zero"], 1)
            pool.wait_ge(s["rows_zero"], 1)
            nc.gpsimd.memset(rowM[0:3 * QD, :], 0.0).then_inc(s["rows_zero"], 1)
            pool.wait_ge(s["rows_zero"], 2)
            pool.wait_ge(s["o_sb"], TC)
            pool.wait_ge(s["ld_attn"], 8 * 16)
            tt(sg[:], sg[:], over(mhw[:].unsqueeze(1), [P, TC, D]), ALU.mult).then_inc(s["sg_ready"], 1)
            for c in range(TC):
                pool.wait_ge(s["arg_ready"], c + 1)
                a = arg[:, c % 2]
                nc.gpsimd.affine_select(out=a, in_=a, compare_op=ALU.is_ge, fill=-1e30, base=0,
                                        pattern=[[0, 4], [0, HG], [1, P]], channel_multiplier=-1)\
                    .then_inc(s["arg_masked"], 1)
            pool.wait_ge(s["down_mm"], TC)
            nc.gpsimd.memset(dwx[:], 0.0).then_inc(s["dwx_zero"], 1)
            pool.wait_ge(s["dwx_zero"], 1)
            nc.gpsimd.memset(dwp[3 * QD:P, :], 0.0).then_inc(s["dwx_zero"], 1)
            pool.wait_ge(s["dwx_zero"], 2)
            wide = dwx[:].rearrange("p c (q e) -> p c q e", q=3)
            for q in range(3):
                nc.gpsimd.memset(wide[:, :, q, E1:E1 + 1], 1.0).then_inc(s["dwx_zero"], 1)
            for th in range(NH):
                def low_part(ic, r):
                    m = IC * th + ic
                    pool.wait_ge(s["ghi_ready"], m + 1)
                    tt(g16[:, r, 1, :], gh1[:, r, :], g16[:, r, 0, :], ALU.subtract).then_inc(s["glo_ready"], 1)

                low_part(0, 0)
                with pool.Fori(0, IC // 2) as i:
                    low_part(2 * i + 1, 1)
                    low_part(2 * i + 2, 0)

        @block.vector
        def _(dve):
            V = nc.vector
            step = [0]

            def then(ins):
                step[0] += 1
                ins.then_inc(s["dve_step"], 1)
                dve.wait_ge(s["dve_step"], step[0])

            dve.wait_ge(s["c_silu"], 1)
            V.tensor_copy(scb[:], over(scs[:].unsqueeze(3), [P, 2, KC, P])).then_inc(s["c_wide"], 1)

            def layernorm(n):
                for c in range(TC):
                    if n == 0:
                        dve.wait_ge(s["ld_x0" if c < HC else "ld_x1"], 16)
                    last = V.bn_stats(st[:, c, :], x[:, c, :])
                then(last)
                for c in range(TC):
                    last = V.bn_aggr(mv[:, c, :], st[:, c, :])
                then(last)
                V.tensor_scalar(ve[:], mv[:, :, 1], LN_EPS, None, ALU.add).then_inc(s["ln_var"], 1)
                dve.wait_ge(s["ln_sd"], n + 1)
                then(V.reciprocal(rs[:], sd[:]))
                for c in range(TC):
                    V.tensor_scalar(xn[:, c, :], x[:, c, :], mv[:, c, 0:1], rs[:, c:c + 1], ALU.subtract, ALU.mult)\
                        .then_inc(s["ln_norm"], 1)

            dve.wait_ge(s["mod_mm"], 1)
            then(V.tensor_copy(modc[:].rearrange("p l n f -> p (l n f)"), ps[:, 0, 0:8 * KC]))
            scales = modc[:].rearrange("p l (a b) f -> p l a b f", b=2)
            for l in range(2):
                last = V.tensor_scalar(scales[:, l, :, 1, :], scales[:, l, :, 1, :], 1.0, None, ALU.add)
            last.then_inc(s["mod_col"], 1)
            for l in range(2):
                g2 = ps[:, 1 + l, :].rearrange("p (a f) -> p a f", a=2)
                then(V.tensor_copy(gt2[:], g2))
                then(V.scalar_tensor_tensor(gt1[:], gt2[:], -1.0, gt2[:], ALU.mult, ALU.max))
                V.tensor_scalar(gt1[:], gt1[:], 0.25, None, ALU.max)
                then(V.tensor_scalar(gt2[:], gt2[:], 0.0, 2.0, ALU.is_ge, ALU.mult))
                then(V.scalar_tensor_tensor(gbc[:, l], gt2[:], -1.0, gt1[:], ALU.add, ALU.mult))
            V.tensor_scalar(gt2[:, 0, :], gbc[:, 1, 1, :], WS, None, ALU.mult).then_inc(s["gate_vec"], 1)
            layernorm(0)

            dve.wait_ge(s["ld_mix"], 64)
            dve.wait_ge(s["zeroed"], 3)
            for j in range(EC):
                dve.wait_ge(s["in_evac"], j + 1)
                w = small0[:, j, :]
                then(V.tensor_scalar(cv[:, j, :], hpad[:, j, 0:T], w[:, 0:1], w[:, 4:5], ALU.mult, ALU.add))
                for k in range(1, TAPS):
                    last = V.scalar_tensor_tensor(cv[:, j, :], hpad[:, j, k:k + T], w[:, k:k + 1], cv[:, j, :],
                                                  ALU.mult, ALU.add)
                    if k < TAPS - 1:
                        then(last)
                last.then_inc(s["conv_done"], 1)

            def three_parts(dst, src, high, rest, done):
                a, b, c = (slice(QD * q, QD * (q + 1)) for q in range(3))
                then(V.tensor_copy(high[0:3 * QD], src))
                V.tensor_copy(dst[a], high[a])
                then(V.tensor_tensor(rest[0:3 * QD], src, high[0:3 * QD], ALU.subtract))
                V.tensor_copy(dst[b], rest[b])
                then(V.tensor_copy(high[c], rest[c]))
                V.tensor_tensor(dst[c], rest[c], high[c], ALU.subtract).then_inc(done, 1)

            dve.wait_ge(s["x_mm"], 1)
            three_parts(bcp, banks(2, 2, 3 * QD), bch, bcr, s["bc_parts"])
            for j, b in enumerate((4, 6, 0, 2)):
                dve.wait_ge(s["abs_done"], j + 1)
                then(V.tensor_scalar(dt_[:, j, :], banks(b, 2), small0[:, j, 5:6], 0.0, ALU.add, ALU.max))
            for j in range(EC):
                dve.wait_ge(s["sp_exp"], j + 1)
                then(V.tensor_scalar(hpad[:, j, 0:T], cv[:, j, :], 1.0, None, ALU.add))
                V.scalar_tensor_tensor(cv[:, j, :], hpad[:, j, 0:T], -1.0, cv[:, j, :], ALU.add, ALU.subtract)\
                    .then_inc(s["sp_rest"], 1)
            for j in range(EC):
                dve.wait_ge(s["sp_rest"], j + 1)
                then(V.tensor_tensor(dt_[:, j, :], dt_[:, j, :], cv[:, j, :], ALU.subtract))
                dve.wait_ge(s["sp_ln"], j + 1)
                V.tensor_tensor(dt_[:, j, :], dt_[:, j, :], hpad[:, j, 0:T], ALU.add).then_inc(s["dt_ready"], 1)

            for th in range(NH):
                half = slice(th * HT, (th + 1) * HT)

                def group(i):
                    for r in range(4):
                        n = 4 * i + r
                        it = NS * th + n
                        dve.wait_ge(s["dA_ready"], it + 1)
                        dve.wait_ge(s["dbu_done"], it + 1)
                        for j in range(EC):
                            start = 0.0 if th == 0 else carry[:, n, j:j + 1]
                            last = V.tensor_tensor_scan(pb[:, r, j, :], dA[:, r % 2, j, :], pb[:, r, j, :], start,
                                                        ALU.mult, ALU.add)
                        last.then_inc(s["scan_done"], 1)
                        dve.wait_ge(s["scan_done"], it + 1)
                        if th == 0:
                            V.tensor_copy(carry[:, n, :], pb[:, r, :, HT - 1]).then_inc(s["carry_saved"], 1)
                            dve.wait_ge(s["carry_saved"], it + 1)
                        dve.wait_ge(s["bsb_ready"], it + 1)
                        V.tensor_tensor(pb[:, r, 0:EC - 1, :], pb[:, r, 0:EC - 1, :],
                                        over(ps[:, 6 + r % 2, :].unsqueeze(1), [P, EC - 1, HT]), ALU.mult)\
                            .then_inc(s["cmul_dve"], 1)

                with dve.Fori(0, NS // 4) as i:
                    group(i)
                dve.wait_ge(s["sum_done"], NS * (th + 1))
                for j in range(EC):
                    last = V.scalar_tensor_tensor(hc[:, j, half], hc[:, j, half], small0[:, j, 6:7], ps[:, j, :],
                                                  ALU.mult, ALU.add)
                last.then_inc(s["y_evac"], 1)
            dve.wait_ge(s["y_evac"], NH)
            V.tensor_tensor(hc[:, :, HT:T], hc[:, :, HT:T], gate[:, :, HT:T], ALU.mult).then_inc(s["y_gated_b"], 1)

            def add_to_x(c, psum, g):
                then(V.tensor_tensor(tmpx[:], psum, over(g.unsqueeze(1), [P, 2, D]), ALU.mult))
                then(V.tensor_tensor(x[:, c:c + 2, :], x[:, c:c + 2, :], tmpx[:], ALU.add))

            for c in range(0, TC, 2):
                dve.wait_ge(s["out_mm"], c + 2)
                add_to_x(c, ps[:, (4 + c) % 8:(4 + c) % 8 + 2, 0:D], gbc[:, 0, 0, :])
            layernorm(1)

            def top2(v, e, scale):
                r_ = over(rev[:, E1 - e:E1].unsqueeze(1), [P, TC, e])
                one, key, v2 = ga_[:, :, 0:e], gb_[:, :, 0:e], gc_[:, :, 0:e]

                def wide(a):
                    return over(a.unsqueeze(2), [P, TC, e])

                then(V.tensor_reduce(gr[:, 0], v, AX_X, ALU.max))
                then(V.tensor_tensor(key, v, wide(gr[:, 0]), ALU.is_equal))
                then(V.tensor_tensor(key, key, r_, ALU.mult))
                then(V.tensor_reduce(gr[:, 1], key, AX_X, ALU.max))
                then(V.tensor_tensor(one, key, wide(gr[:, 1]), ALU.is_equal))
                then(V.scalar_tensor_tensor(v2, one, -4.0, v, ALU.mult, ALU.add))
                then(V.tensor_reduce(gr[:, 2], v2, AX_X, ALU.max))
                then(V.tensor_tensor(key, v2, wide(gr[:, 2]), ALU.is_equal))
                then(V.tensor_tensor(key, key, r_, ALU.mult))
                then(V.tensor_reduce(gr[:, 3], key, AX_X, ALU.max))
                then(V.tensor_tensor(key, key, wide(gr[:, 3]), ALU.is_equal))
                then(V.tensor_tensor(one, one, key, ALU.add))
                then(V.tensor_tensor(gr[:, 4], gr[:, 0], gr[:, 2], ALU.add))
                then(V.reciprocal(gr[:, 5], gr[:, 4]))
                then(V.tensor_tensor(key, v, one, ALU.mult))
                then(V.scalar_tensor_tensor(key, key, scale, wide(gr[:, 5]), ALU.mult, ALU.mult))

            dve.wait_ge(s["f0_mm"], 1)
            pair = ps[:, 4:8, 0:272].rearrange("p b (c n) -> p b c n", c=2)
            v = gl[:, :, 0:E0]
            then(V.tensor_copy(v.rearrange("p (b c) e -> p b c e", c=2), pair[:, :, :, 0:E0]))
            then(V.tensor_reduce(gr[:, 0], v, AX_X, ALU.max))
            V.tensor_tensor(v, v, over(gr[:, 0].unsqueeze(2), [P, TC, E0]), ALU.subtract).then_inc(s["soft_arg"], 1)
            dve.wait_ge(s["soft_exp"], 1)
            then(V.tensor_reduce(gr[:, 1], ga_[:, :, 0:E0], AX_X, ALU.add))
            then(V.reciprocal(gr[:, 2], gr[:, 1]))
            then(V.tensor_tensor(v, ga_[:, :, 0:E0], over(gr[:, 2].unsqueeze(2), [P, TC, E0]), ALU.mult))
            top2(v, E0, 16.0)
            cw = gb_[:, :, 0:E0].rearrange("p (b c) e -> p b c e", c=2)
            tw = ffn0_t.rearrange("p (b c) n -> p b c n", c=2)
            for c in range(2):
                last = V.tensor_tensor(tw[:, :, c, :].rearrange("p b (e r) -> p b e r", r=RL),
                                       pair[:, :, c, E0:136].rearrange("p b (e r) -> p b e r", r=RL),
                                       over(cw[:, :, c, :].unsqueeze(3), [P, 4, E0, RL]), ALU.mult)
            last.then_inc(s["f0_t"], 1)
            dve.wait_ge(s["f0_lora"], 1)
            for b in range(4):
                add_to_x(2 * b, ps[:, b, :].rearrange("p (c f) -> p c f", c=2), gbc[:, 0, 1, :])
            layernorm(2)

            def rmsnorm(dst, src, which, sd_, inv, ready):
                then(V.reciprocal(inv, sd_))
                for k in range(KC):
                    V.scalar_tensor_tensor(dst[:, k, :], src[:, k, :], small1[:, which, k:k + 1], inv,
                                           ALU.mult, ALU.mult).then_inc(ready, 1)

            dve.wait_ge(s["ln_h"], 12)
            dve.wait_ge(s["rms_sd"], 1)
            rmsnorm(hin, hT, 0, kT[:, 0, :], kT[:, 1, :], s["hin_ready"])
            dve.wait_ge(s["hin_ready"], KC)
            for g in range(HG):
                dve.wait_ge(s["k_mm"], g + 1)
                V.tensor_copy(kT[:, g, :], banks(4 + 2 * g, 2)).then_inc(s["k_sb"], 1)
            dve.wait_ge(s["ld_attn"], 8 * 16)
            for c in range(TC):
                dve.wait_ge(s["v_mm"], c + 1)
                b = 2 * (c % 4)
                V.tensor_tensor(zif[:, c, :], ps[:, b, D:D + 2 * H], bif[:], ALU.add).then_inc(s["z_in"], 1)
                V.tensor_copy(vext[:, c, :, 0:DV], ps[:, b, 0:D].rearrange("p (h v) -> p h v", h=H))\
                    .then_inc(s["v_sb"], 1)

            dve.wait_ge(s["rows_zero"], 2)
            dve.wait_ge(s["z_tanh"], 1)
            for q in range(3):
                V.tensor_scalar(lif[:, 1, :, QD * q:QD * q + H], zt[:, :, 0:H], CAP, None, ALU.mult)
            dve.wait_ge(s["z_exp"], 1)
            V.tensor_scalar(lw[:, 1], lw[:, 0], 1.0, None, ALU.add).then_inc(s["z_w"], 1)
            dve.wait_ge(s["z_w"], 1)
            then(V.tensor_scalar(lw[:, 3], lw[:, 1], -1.0, None, ALU.add))
            then(V.tensor_tensor(lw[:, 3], lw[:, 0], lw[:, 3], ALU.subtract))
            then(V.reciprocal(lw[:, 0], lw[:, 1]))
            then(V.tensor_tensor(lw[:, 3], lw[:, 3], lw[:, 0], ALU.mult))
            dve.wait_ge(s["z_ln"], 1)
            then(V.tensor_tensor(lw[:, 3], lw[:, 3], lw[:, 2], ALU.add))
            for q in range(3):
                last = V.tensor_scalar(lif[:, 0, :, QD * q:QD * q + H], lw[:, 3], -1.0, None, ALU.mult)
            last.then_inc(s["lif_ready"], 1)
            dve.wait_ge(s["lif_T"], 1)
            R3 = slice(0, 3 * QD)
            then(V.tensor_tensor_scan(rowF[R3, :], banks(0, 2, 3 * QD), rowM[R3, :], 0.0, ALU.add, ALU.add))
            then(V.tensor_tensor(rowA[R3, :], banks(2, 2, 3 * QD), rowF[R3, :], ALU.subtract))
            then(V.tensor_tensor_scan(rowG[R3, :], rowA[R3, :], rowA[R3, :], -1e30, ALU.max, ALU.max))
            V.tensor_tensor(rowM[R3, :], rowF[R3, :], rowG[R3, :], ALU.add).then_inc(s["row_tok"], 1)
            dve.wait_ge(s["row_tok"], 1)
            three_parts(gp, rowG[R3, :], gh, rowF, s["row_parts"])
            dve.wait_ge(s["tok_T"], 1)
            dve.wait_ge(s["enm_ready"], 1)
            V.tensor_copy(agt[:, 0:2].rearrange("p a c h -> p (a c h)"), ps[:, 4, 0:2 * TC * H])
            dve.wait_ge(s["rr_mm"], 1)
            V.tensor_copy(rbc[:].rearrange("p h c -> p (h c)"), ps[:, 5, 0:H * TC])
            then(V.tensor_copy(rrow[:].rearrange("p g c -> p (g c)"), ps[:, 5, H * TC:(H + HG) * TC]))
            ends = rbc[:].rearrange("p h c -> p c h")
            V.tensor_tensor(wkt[:], agt[:, 0], ends, ALU.subtract)
            V.tensor_tensor(wqt[:, 1:], ends[:, 0:TC - 1], agt[:, 1, 1:], ALU.subtract)
            V.tensor_tensor(dec[:, :, 1:], rrow[:, :, 0:TC - 1], rrow[:, :, 1:], ALU.subtract).then_inc(s["w_arg"], 1)
            dve.wait_ge(s["w_exp"], 1)
            dve.wait_ge(s["kT_T"], 1)
            for b in range(4):
                V.tensor_tensor(ks[:, 2 * b:2 * b + 2].rearrange("p c h n -> p (c h) n"),
                                ps[:, b, :].rearrange("p (ch n) -> p ch n", n=QR),
                                over(wkt[:, 2 * b:2 * b + 2].rearrange("p c h -> p (c h)").unsqueeze(2),
                                     [P, 2 * H, QR]), ALU.mult).then_inc(s["ks_ready"], 1)
            dve.wait_ge(s["v_ones"], 2)
            for c in range(TC - 1):
                dve.wait_ge(s["state_mm"], 4 * (c // 4) + 4)
                for g in range(HG):
                    col = (c % 4) * HG * VE + g * VE
                    add = ps[:, 6 + c // 4, col:col + VE]
                    if c == 0:
                        last = V.tensor_copy(states[:, c, g, :], add)
                    else:
                        last = V.scalar_tensor_tensor(states[:, c, g, :], states[:, c - 1, g, :], dec[:, g, c:c + 1], add,
                                                      ALU.mult, ALU.add)
                last.then_inc(s["state_done"], 1)
                dve.wait_ge(s["state_done"], c + 1)

            def heads(a):
                return a.rearrange("p (g r) -> p r g", g=HG)

            def exponent(c):
                dve.wait_ge(s["g_mm"], c + 1)
                V.tensor_tensor(arg[:, c % 2], over(heads(agt[:, 0, c, :]).unsqueeze(3), [P, 4, HG, P]),
                                banks(4, 2).rearrange("p (r g t) -> p r g t", r=4, g=HG), ALU.subtract)\
                    .then_inc(s["arg_ready"], 1)

            def gather(c):
                dve.wait_ge(s["intra_mm"], c + 1)
                own = ps[:, 6 + c % 2, 0:H * VE].rearrange("p (h v) -> p h v", h=H)
                if c == 0:
                    V.tensor_copy(num[:, c], own).then_inc(s["num_ready"], 1)
                else:
                    V.tensor_tensor(num[:, c], num[:, c], own, ALU.add).then_inc(s["num_ready"], 1)

            exponent(0)
            for c in range(TC):
                if c + 1 < TC:
                    exponent(c + 1)
                dve.wait_ge(s["e_ready"], c + 1)
                dve.wait_ge(s["s_mm"], c + 1)
                if c:
                    dve.wait_ge(s["intra_mm"], c)
                last = V.tensor_tensor(pr[:], ps[:, 0:4, 0:D].rearrange("p r (g t) -> p r g t", g=HG), arg[:, c % 2],
                                       ALU.mult)
                last.then_inc(s["pr_ready"], 1)
                if c:
                    V.tensor_tensor(num[:, c].rearrange("p (g r) v -> p r g v", g=HG),
                                    ps[:, 0:4, D:D + HG * VE].rearrange("p r (g v) -> p r g v", g=HG),
                                    over(heads(wqt[:, c, :]).unsqueeze(3), [P, 4, HG, VE]), ALU.mult)\
                        .then_inc(s["inter_used"], 1)
                    gather(c - 1)
                else:
                    dve.wait_ge(s["pr_ready"], 1)
                    dve.sem_inc(s["inter_used"], 1)
            dve.wait_ge(s["inter_used"], TC)
            gather(TC - 1)

            dve.wait_ge(s["num_ready"], TC)
            dve.wait_ge(s["enm_ready"], 1)
            nv = num[:].rearrange("p c h v -> p (c h) v")
            flat = [nden[:, a].rearrange("p c h -> p (c h)") for a in range(3)]
            then(V.scalar_tensor_tensor(nden[:, 0], num[:, :, :, DV], -1.0, num[:, :, :, DV], ALU.mult, ALU.max))
            then(V.tensor_tensor(nden[:, 0], nden[:, 0], agt[:, 2], ALU.max))
            then(V.reciprocal(nden[:, 1], nden[:, 0]))
            V.tensor_tensor(ho_head, nv[:, :, 0:DV], over(flat[1].unsqueeze(2), [P, TC * H, DV]), ALU.mult)\
                .then_inc(s["den_ready"], 1)
            dve.wait_ge(s["num_sq"], 1)
            V.tensor_reduce(flat[1], sq_tok, AX_X, ALU.add).then_inc(s["var_ready"], 1)
            dve.wait_ge(s["var_sd"], 1)
            then(V.reciprocal(nden[:, 0], nden[:, 2]))
            dve.wait_ge(s["sg_ready"], 1)
            for th in range(NH):
                rows = slice(th * HC * H, (th + 1) * HC * H)
                then(V.tensor_tensor(ho_head[:, rows], ho_head[:, rows],
                                     over(flat[0][:, rows].unsqueeze(2), [P, HC * H, DV]), ALU.mult))
                toks = slice(th * HC, (th + 1) * HC)
                V.tensor_tensor(ho_tok[:, toks], ho_tok[:, toks], sg[:, toks], ALU.mult).then_inc(s["ho_ready"], 1)
            for m in range(KC):
                dve.wait_ge(s["wo_mm"], m + 1)
                V.tensor_tensor(x1T[:, m, :], hT[:, m, :], banks(4 + 2 * m, 2), ALU.add).then_inc(s["x1_ready"], 1)
            dve.wait_ge(s["x1_ready"], KC)
            dve.wait_ge(s["rms2_sd"], 1)
            rmsnorm(h2T, x1T, 1, sil[:, 0, :], sil[:, 1, :], s["h2_ready"])
            for f in range(FC):
                dve.wait_ge(s["sil_ready"], f + 1)
                V.tensor_tensor(gg[:, f, :], sil[:, f % 2, :], banks(4 * (f % 2) + 2, 2), ALU.mult)\
                    .then_inc(s["gg_ready"], 1)
            for c in range(0, TC, 2):
                dve.wait_ge(s["down_mm"], c + 2)
                add_to_x(c, ps[:, c:c + 2, 0:D], gbc[:, 1, 0, :])
            layernorm(3)

            dve.wait_ge(s["ln_h"], 16)
            dve.wait_ge(s["down_mm"], TC)
            V.tensor_copy(h16[:, 0], hT[:]).then_inc(s["h_hi"], 1)
            dve.wait_ge(s["h_hi"], 1)
            V.tensor_tensor(h16[:, 1], hT[:], h16[:, 0], ALU.subtract).then_inc(s["h_split"], 1)
            dve.wait_ge(s["z1_exp"], 1)
            then(V.tensor_scalar(gl[:], ga_[:], 1.0, None, ALU.add))
            then(V.reciprocal(gl[:], gl[:]))
            top2(gl[:], E1, 1.0)
            dve.wait_ge(s["dwx_zero"], 5)
            wide = dwx[:].rearrange("p c (q e) -> p c q e", q=3)
            for q in range(3):
                last = V.tensor_copy(wide[:, :, q, 0:E1], gb_[:])
            last.then_inc(s["dw_ready"], 1)
            dve.wait_ge(s["dw_T"], 1)
            three_parts(dwp, banks(6, 2, 3 * QD), dwh, dwr, s["dw_parts"])
            for th in range(NH):
                def gated(ic, r, first):
                    m = IC * th + ic
                    dve.wait_ge(s["moe_sil"], m + 1)
                    V.tensor_tensor(sa_[:, r, :], sa_[:, r, :], ps[:, 4 + r, :], ALU.mult).then_inc(s["moe_prod"], 1)
                    dve.wait_ge(s["moe_prod"], m + 1)
                    if not first:
                        dve.wait_ge(s["glo_ready"], m - 1)
                    V.tensor_tensor(gh1[:, r, :], sa_[:, r, :], ps[:, 6 + r, :], ALU.mult).then_inc(s["g_ready"], 1)
                    dve.wait_ge(s["g_ready"], m + 1)
                    if not first:
                        dve.wait_ge(s["acc_mm"], m - 1)
                    V.tensor_copy(g16[:, r, 0, :], gh1[:, r, :]).then_inc(s["ghi_ready"], 1)

                gated(0, 0, th == 0)
                if th == 0:
                    gated(1, 1, True)
                    gated(2, 0, False)
                with dve.Fori(1 if th == 0 else 0, IC // 2) as i:
                    gated(2 * i + 1, 1, False)
                    gated(2 * i + 2, 0, False)
                dve.wait_ge(s["acc_mm"], IC * (th + 1))
                for b in range(2):
                    c = th * HC + 2 * b
                    then(V.tensor_tensor(tmpx[:], ps[:, b, :].rearrange("p (c f) -> p c f", c=2),
                                         over(gt2[:, 0, :].unsqueeze(1), [P, 2, D]), ALU.mult))
                    last = V.tensor_tensor(x[:, c:c + 2, :], x[:, c:c + 2, :], tmpx[:], ALU.add)
                    if b == 0:
                        then(last)
                last.then_inc(s["x_out"], 1)


def program(nc, arrays):
    d = {}
    for name, a in arrays.items():
        t = nc.dram_tensor(f"in_{name}_dram", a.shape, mybir.dt.from_np(a.dtype), kind="ExternalInput").ap()
        d[name] = t
    out = nc.dram_tensor("out_0_dram", (T, D), F32, kind="ExternalOutput").ap()
    adaln_two_layers(nc, d, out)


def _rows(w):
    import numpy as np
    return np.ascontiguousarray(w.reshape(-1, 128, w.shape[1]).transpose(1, 0, 2))


def _heads_apart(w):
    import numpy as np
    o = np.zeros((w.shape[0], 8, 32), w.dtype)
    o[:, :, :16] = w.reshape(w.shape[0], 8, 16)
    return o.reshape(w.shape[0], 256)


def kernel(**inputs):
    import numpy as np
    import concourse.bacc as _bacc
    from concourse.bass_utils import run_bass_kernel_spmd as _run

    i = {k: np.asarray(v) for k, v in inputs.items()}
    cat, tile = np.concatenate, np.tile
    bf = i["L1_ffn_w1"].dtype
    cols = lambda v: v.reshape(-1, 128).T
    ar = {}
    ar["x"] = i["L0_attn_hidden_states"].reshape(T, D)
    ar["c"] = np.stack([cols(i["L0_c"].ravel()), cols(i["L1_c"].ravel())], 1)
    ar["wmod"] = np.stack([_rows(i["L0_wmod"]), _rows(i["L1_wmod"])])
    ar["win"] = _rows(i["L0_attn_in_proj_w"].T)
    conv = i["L0_attn_conv_w"].reshape(EC, P, TAPS).transpose(1, 0, 2)
    vecs = [cols(i[n]) for n in ("L0_attn_conv_b", "L0_attn_dt_proj_b", "L0_attn_D")]
    ar["small0"] = cat([conv] + [v[:, :, None] for v in vecs], 2)
    ar["alog"] = i["L0_attn_A_log"].reshape(EC, P, NS).transpose(1, 2, 0)
    xp = i["L0_attn_x_proj_w"].T
    ar["wx"] = _rows(cat([xp[:, :R0]] + [xp[:, R0:]] * 3, 1))
    ar["wdt"] = i["L0_attn_dt_proj_w"].T
    ar["wo0"] = _rows(i["L0_attn_out_proj_w"].T)
    ar["wf0"] = _rows(cat([i["L0_ffn_weight"].T, i["L0_ffn_gate_w"].T, i["L0_ffn_A_w"].reshape(P, D).T], 1))
    ar["wlb"] = i["L0_ffn_B_w"].transpose(0, 2, 1).reshape(P, D)
    ar["norm_w"] = np.stack([cols(i["L1_attn_norm1_w"]), cols(i["L1_attn_norm2_w"])], 1)
    ar["wq"] = _rows(_heads_apart(i["L1_attn_wq"]))
    ar["wk"] = _rows(_heads_apart(i["L1_attn_wk"]))
    ar["wvif"] = _rows(cat([i["L1_attn_wv"], i["L1_attn_w_ig"], i["L1_attn_w_fg"]], 1))
    ar["wog"] = _rows(i["L1_attn_w_og"])
    ar["bif"] = tile(cat([i["L1_attn_b_ig"], i["L1_attn_b_fg"]])[None], (P, 1))
    ar["mhw"] = tile(i["L1_attn_mh_w"][None], (P, 1))
    ar["wout1"] = _rows(i["L1_attn_w_out"])
    ar["wg"] = _rows(i["L1_attn_w_gate"])
    ar["wu"] = _rows(i["L1_attn_w_up"])
    ar["wd"] = _rows(i["L1_attn_w_down"])
    ar["wg1"] = _rows(i["L1_ffn_gate_w"].T)
    inner = i["L1_ffn_w1"].shape[1]

    def all_rows(routed, shared):
        m = cat([routed.reshape(-1, D), shared], 0)
        return cat([m, np.zeros((IC * P - m.shape[0], D), m.dtype)], 0)

    ar["w1"] = _rows(all_rows(i["L1_ffn_w1"], i["L1_ffn_sw1"]).T)
    ar["w3"] = _rows(all_rows(i["L1_ffn_w3"], i["L1_ffn_sw3"]).T)
    ar["w2"] = _rows(all_rows(i["L1_ffn_w2"].transpose(0, 2, 1), i["L1_ffn_sw2"].T))
    row = np.arange(P)
    ar["ident"] = np.eye(P, dtype=np.float32)
    inside = (row < 3 * QD)[:, None, None]
    ar["sel"] = (inside & (row[:, None, None] % QD == np.arange(2 * NS)[None, :, None]) & np.ones((1, 1, P), bool)).astype(bf)
    head = 4 * np.arange(HG)[:, None] + row[None, :] // QD
    ar["selr"] = (inside & (row[:, None, None] % QD == head[None])).astype(bf)
    expert = np.minimum(np.arange(IC * P).reshape(IC, P) // inner, E1)
    ar["selx"] = ((inside & (row[:, None, None] % QD == expert[None])) * np.float32(1 / WS)).astype(bf)
    ar["rev"] = tile(np.arange(E1, 0, -1, dtype=np.float32)[None], (P, 1))

    nc = _bacc.Bacc("TRN2", target_bir_lowering=False, num_devices=1)
    ar = {k: np.ascontiguousarray(v) for k, v in ar.items()}
    program(nc, ar)
    r = _run(nc, [{f"in_{k}_dram": v for k, v in ar.items()}], core_ids=[0])
    return r.results[0]["out_0_dram"].reshape(1, T, D)
```

```python
from contextlib import ExitStack

import concourse.bass as bass
from concourse import mybir

P = 128
T = 1024
D = 256
KC = D // P
TC = T // P
HT = 512
NH = T // HT
HC = HT // P
E = 512
EC = E // P
NS = 16
TAPS = 4
R0 = 128
E0, RL = 8, 16
H, DV = 8, 32
QR = 32
HG = 2
VE = DV + 1
FF = 1024
FC = FF // P
E1 = 16
IC = 25
QD = 32
WS = 64.0
LN_EPS, RMS_EPS = 1e-5, 1e-6
CAP = 15.0

ALU = mybir.AluOpType
ACT = mybir.ActivationFunctionType
AX_X = mybir.AxisListType.X
F32 = mybir.dt.float32
BF16 = mybir.dt.bfloat16
F16 = mybir.dt.float16


def adaln_two_layers(nc, d, out):
    ctx = ExitStack()
    with ctx:
        def sem(name):
            return ctx.enter_context(nc.semaphore(name))

        def sbt(stack, name, shape, dt=F32):
            return stack.enter_context(nc.sbuf_tensor(name, shape, dt))

        x = sbt(ctx, "x", [P, TC, D])
        xn = sbt(ctx, "xn", [P, TC, D])
        hT = sbt(ctx, "hT", [P, KC, T])
        tmpx = sbt(ctx, "tmpx", [P, 2, D])
        ident = sbt(ctx, "ident", [P, P])
        ones = sbt(ctx, "ones", [P, P])
        sel = sbt(ctx, "sel", [P, 2 * NS, P], BF16)
        zero16 = sbt(ctx, "zero16", [P, HT], BF16)
        st = sbt(ctx, "st", [P, TC, 6])
        mv = sbt(ctx, "mv", [P, TC, 2])
        ve = sbt(ctx, "ve", [P, TC])
        sd = sbt(ctx, "sd", [P, TC])
        rs = sbt(ctx, "rs", [P, TC])
        eps = sbt(ctx, "eps", [P, 2])
        cs = sbt(ctx, "cs", [P, 2, KC])
        scs = sbt(ctx, "scs", [P, 2, KC])
        scb = sbt(ctx, "scb", [P, 2, KC, P])
        modc = sbt(ctx, "modc", [P, 2, 4, KC])
        gbc = sbt(ctx, "gbc", [P, 2, 2, D])
        gt1 = sbt(ctx, "gt1", [P, 2, D])
        gt2 = sbt(ctx, "gt2", [P, 2, D])
        small0 = sbt(ctx, "small0", [P, EC, TAPS + 3])
        alog = sbt(ctx, "alog", [P, NS, EC])
        aneg = sbt(ctx, "aneg", [P, NS, EC])
        carry = sbt(ctx, "carry", [P, NS, EC])
        rev = sbt(ctx, "rev", [P, E1])
        small1 = sbt(ctx, "small1", [P, 2, KC])
        wf0 = sbt(ctx, "wf0", [P, KC, D + E0 + P])
        wlb = sbt(ctx, "wlb", [P, D])
        wo0 = sbt(ctx, "wo0", [P, EC, D])
        ffn0_t = xn[:, 0:HC, :].rearrange("p c d -> p (c d)").rearrange("p (c r) -> p c r", r=P)
        ffn0_tT = xn[:, HC:TC, :].rearrange("p c d -> p (c d)")
        sq = xn[:, :, :].rearrange("p c d -> p (c d)").rearrange("p (k t) -> p k t", k=KC)
        qw = sq
        hoT = sq
        gl = sbt(ctx, "gl", [P, TC, E1])
        ga_ = sbt(ctx, "ga_", [P, TC, E1])
        gb_ = sbt(ctx, "gb_", [P, TC, E1])
        gc_ = sbt(ctx, "gc_", [P, TC, E1])
        gr = sbt(ctx, "gr", [P, 6, TC])

        mixer = ExitStack()
        win = sbt(mixer, "win", [P, KC, 2 * E])
        wx = sbt(mixer, "wx", [P, EC, R0 + 3 * QD])
        wdt = sbt(mixer, "wdt", [P, E])
        hc = sbt(mixer, "hc", [P, EC, T])
        gate = sbt(mixer, "gate", [P, EC, T])
        dt_ = sbt(mixer, "dt_", [P, EC, T])
        u = sbt(mixer, "u", [P, EC, T])
        bcp = sbt(mixer, "bcp", [P, T], BF16)
        with ExitStack() as first:
            wmod = sbt(first, "wmod", [P, 2, KC, 6 * D])
        with ExitStack() as before:
            hpad = sbt(before, "hpad", [P, EC, T + TAPS - 1])
            cv = sbt(before, "cv", [P, EC, T])
            dtr = sbt(before, "dtr", [P, T])
            bch = sbt(before, "bch", [P, T], BF16)
            bcr = sbt(before, "bcr", [P, T])
        with ExitStack() as during:
            pb = sbt(during, "pb", [P, 4, EC, HT])
            dA = sbt(during, "dA", [P, 4, EC, HT])
            bsb = xn[:, :, :].rearrange("p c d -> p (c d)").rearrange("p (n t) -> p n t", t=HT)
            csb = hT[:, :, :].rearrange("p k t -> p (k t)").rearrange("p (n t) -> p n t", t=HT)
        mixer.close()

        layer1 = ExitStack()
        wout1 = sbt(layer1, "wout1", [P, KC, D])
        wg = sbt(layer1, "wg", [P, KC, FF])
        wu = sbt(layer1, "wu", [P, KC, FF])
        sg = sbt(layer1, "sg", [P, TC, D])
        with ExitStack() as attn:
            selr = sbt(attn, "selr", [P, HG, P], BF16)
            bif = sbt(attn, "bif", [P, 2 * H])
            mhw = sbt(attn, "mhw", [P, D])
            qT = sbt(attn, "qT", [P, HG, T])
            kT = sbt(attn, "kT", [P, HG, T])
            vext = sbt(attn, "vext", [P, TC, H, VE])
            zif = sbt(attn, "zif", [P, TC, 2 * H])
            zt = sbt(attn, "zt", [P, TC, 2 * H])
            lw = sbt(attn, "lw", [P, 4, TC, H])
            gp = sbt(attn, "gp", [P, T], BF16)
            agt = sbt(attn, "agt", [P, 3, TC, H])
            rbc = sbt(attn, "rbc", [P, H, TC])
            rrow = sbt(attn, "rrow", [P, HG, TC])
            dec = sbt(attn, "dec", [P, HG, TC])
            wkt = sbt(attn, "wkt", [P, TC, H])
            qbd = sbt(attn, "qbd", [P, HG, TC, 4, P])
            rinv = sbt(attn, "rinv", [P, 3, TC])
            states = sbt(attn, "states", [P, TC - 1, HG, VE])
            sbd = sbt(attn, "sbd", [P, TC - 1, HG, 4, VE])
            nden = sbt(attn, "nden", [P, 3, TC, H])
            wq = sbt(attn, "wq", [P, KC, HG * P])
            wk = sbt(attn, "wk", [P, KC, HG * P])
            wvif = sbt(attn, "wvif", [P, KC, D + 2 * H])
            wog = sbt(attn, "wog", [P, KC, D])
            with ExitStack() as rows:
                rowF = sbt(rows, "rowF", [P, T])
                rowA = sbt(rows, "rowA", [P, T])
                rowG = sbt(rows, "rowG", [P, T])
                rowM = sbt(rows, "rowM", [P, T])
                lif = sbt(rows, "lif", [P, 2, TC, 3 * QD])
                gh = sbt(rows, "gh", [P, T], BF16)
            with ExitStack() as chunks:
                ks = sbt(chunks, "ks", [P, TC, H, QR])
                arg = sbt(chunks, "arg", [P, 2, H, P])
                pr = sbt(chunks, "pr", [P, 2, H, P])
                num = sbt(chunks, "num", [P, TC, H, VE])
        w1 = sbt(layer1, "w1", [P, KC, IC * P], BF16)
        w3 = sbt(layer1, "w3", [P, KC, IC * P], BF16)
        w2 = sbt(layer1, "w2", [P, IC, D], BF16)
        selx = sbt(layer1, "selx", [P, IC, P], BF16)
        wg1 = sbt(layer1, "wg1", [P, KC, E1])
        with ExitStack() as mlp:
            wd = sbt(mlp, "wd", [P, FC, D])
            x1T = sbt(mlp, "x1T", [P, KC, T])
            sd2 = sbt(mlp, "sd2", [P, 2, T])
            sil = sbt(mlp, "sil", [P, 2, T])
            gg = sbt(mlp, "gg", [P, FC, T])
        with ExitStack() as moe:
            h16 = sbt(moe, "h16", [P, 2, KC, T], F16)
            dwx = sbt(moe, "dwx", [P, TC, 3 * QD])
            dwp = sbt(moe, "dwp", [P, T], BF16)
            dwh = sbt(moe, "dwh", [P, T], BF16)
            dwr = sbt(moe, "dwr", [P, T])
            sa_ = sbt(moe, "sa_", [P, 2, HT])
            gh1 = sbt(moe, "gh1", [P, 2, HT])
            g16 = sbt(moe, "g16", [P, 2, 2, HT], F16)
            xo = sbt(moe, "xo", [P, 2, D])
        layer1.close()
        ps = ctx.enter_context(nc.psum_tensor("ps", [P, 8, HT], F32))

        def banks(b, n, rows=P):
            return ps[0:rows, b:b + n, :].rearrange("p b f -> p (b f)")

        def over(ap, shape):
            return ap.broadcast_to(shape)

        ho_head = ks[:].rearrange("p c h n -> p (c h) n")
        ho_tok = ks[:].rearrange("p c h n -> p c (h n)")
        sq_tok = xn[:, :, :].rearrange("p c d -> p (c d)").rearrange("p (a n) -> p a n", n=DV)

        names = """ld_mod ld_x0 ld_x1 ld_const ld_win ld_mix ld_ffn0 ld_attn ld_gateup ld_moe ld_down
            c_silu c_wide mod_mm mod_col gate_vec
            zeroed ones_ready
            ln_var ln_sd ln_norm ln_T ln_h
            in_mm in_evac conv_done hc_ready
            x_mm dtr_ready bc_parts dt_mm sp_exp dt_ready u_ready aexp aneg_ready
            y_zero bc_bcast bc_copied dA_ready dbu_done scan_done carry_saved cmul_dve sum_done
            y_evac y_gated
            out_mm x_mixed
            f0_mm f0_out soft_arg soft_exp f0_t f0_T f0_tT f0_lora x_ffn0
            sq_ready ss_mm rms_sd w_scaled z_mm vo_sb g_scaled gu_used qbd_act qbd_dve qbd_pool q_mm k_mm q_sb k_sb v_mm z_in z_tanh z_exp z_ln lif_ready lif_T
            sp_rest sp_ln abs_done z_w v_ones rows_zero sg_ready enm_ready y_gated_a y_gated_b var_ready dwx_zero moe_prod row_parts row_tok tok_T agt_ready rr_mm rr_sb w_arg w_exp kT_T ks_ready state_mm state_done
            qg_mm qw_arg qw_exp qw_ready sbd_ready s_mm g_mm arg_ready arg_masked e_ready pr_ready intra_mm num_ready
            den_ready num_sq var_sd ho_ready ho_T hoT_ready
            wo_mm x1_ready sq2_ready ss2_mm rms2_sd gu_mm sil_ready gg_ready down_mm x_attn
            h_hi h_split z1_mm z1_exp dw_ready dw_T dw_parts acc_zero up_mm moe_sil g_ready ghi_ready glo_ready acc_mm
            x_out stored act_step dve_step pool_step""".split()
        s = {n: sem(n) for n in names}

        block = ctx.enter_context(nc.Block())

        @block.sync
        def _(sp):
            def load(dst, name, signal):
                sp.dma_start(dst, d[name]).then_inc(s[signal], 16)

            xv = d["x"].rearrange("(c p) f -> p c f", p=P)
            sp.dma_start(x[:, 0:HC, :], xv[:, 0:HC, :]).then_inc(s["ld_x0"], 16)
            sp.dma_start(x[:, HC:TC, :], xv[:, HC:TC, :]).then_inc(s["ld_x1"], 16)
            load(ident[:], "ident", "ld_const")
            load(sel[:], "sel", "ld_const")
            load(rev[:], "rev", "ld_const")
            load(small1[:], "norm_w", "ld_const")
            load(win[:], "win", "ld_win")
            load(small0[:], "small0", "ld_mix")
            load(alog[:], "alog", "ld_mix")
            load(wx[:], "wx", "ld_mix")
            load(wdt[:], "wdt", "ld_mix")
            load(wo0[:], "wo0", "ld_ffn0")
            load(wf0[:], "wf0", "ld_ffn0")
            load(wlb[:], "wlb", "ld_ffn0")
            sp.wait_ge(s["out_mm"], TC)
            for dst, name in ((wq, "wq"), (wk, "wk"), (wvif, "wvif"), (wog, "wog"), (selr, "selr"), (bif, "bif"),
                              (mhw, "mhw"), (wout1, "wout1")):
                load(dst[:], name, "ld_attn")
            load(wg[:], "wg", "ld_gateup")
            load(wu[:], "wu", "ld_gateup")
            sp.wait_ge(s["hoT_ready"], 4)
            load(wd[:], "wd", "ld_down")
            for dst, name in ((wg1, "wg1"), (w1, "w1"), (w3, "w3"), (w2, "w2"), (selx, "selx")):
                load(dst[:], name, "ld_moe")
            ov = out.rearrange("(c p) f -> p c f", p=P)
            for th in range(NH):
                sp.wait_ge(s["x_out"], th + 1)
                sp.dma_start(ov[:, th * HC:(th + 1) * HC, :], x[:, th * HC:(th + 1) * HC, :]).then_inc(s["stored"], 16)
            sp.wait_ge(s["stored"], 16 * NH)

        @block.tensor
        def _(pe):
            mm = nc.tensor.matmul

            def clear(b):
                return mm(ps[:, b, :], zero16[:, 0:P], zero16[:, :], start=True, stop=False)

            pe.wait_ge(s["ld_mod"], 48)
            pe.wait_ge(s["c_silu"], 1)
            for l in range(2):
                for n, part in enumerate((0, 1, 3, 4)):
                    for f in range(KC):
                        col = (l * 4 + n) * KC + f
                        for k in range(KC):
                            lo = part * D + f * P
                            mm(ps[:, 0, col:col + 1], wmod[:, l, k, lo:lo + P], scs[:, l, k:k + 1],
                               start=k == 0, stop=k == KC - 1)
            pe.wait_ge(s["c_wide"], 1)
            for l in range(2):
                for k in range(KC):
                    gates = wmod[:, l, k, :].rearrange("p (a b f) -> p a b f", a=2, b=3)[:, :, 2, :]
                    last = mm(ps[:, 1 + l, :], scb[:, l, k, :], gates, start=k == 0, stop=k == KC - 1)
            last.then_inc(s["mod_mm"], 1)

            def ln_transposes(n):
                for th in range(NH):
                    pe.wait_ge(s["ln_norm"], TC * n + HC * (th + 1))
                    for k in range(KC):
                        for c in range(HC):
                            last = nc.tensor.transpose(ps[:, 2 * k + th, c * P:(c + 1) * P],
                                                       xn[:, th * HC + c, k * P:(k + 1) * P], ident[:])
                    last.then_inc(s["ln_T"], 1)

            pe.wait_ge(s["ld_const"], 64)
            pe.wait_ge(s["ones_ready"], 3)
            pe.wait_ge(s["gate_vec"], 1)
            ln_transposes(0)

            pe.wait_ge(s["ln_h"], 4)
            pe.wait_ge(s["ld_win"], 16)
            for g in range(2 * EC):
                b = 2 * ((g + 2) % 4)
                if g >= 4:
                    pe.wait_ge(s["in_evac"], g - 3)
                for th in range(NH):
                    for k in range(KC):
                        last = mm(ps[:, b + th, :], win[:, k, g * P:(g + 1) * P], hT[:, k, th * HT:(th + 1) * HT],
                                  start=k == 0, stop=k == KC - 1)
                last.then_inc(s["in_mm"], 1)

            pe.wait_ge(s["in_evac"], 2 * EC)
            pe.wait_ge(s["ld_mix"], 64)
            for j in range(EC):
                pe.wait_ge(s["hc_ready"], j + 1)
                for th in range(NH):
                    rhs = hc[:, j, th * HT:(th + 1) * HT]
                    mm(ps[:, th, :], wx[:, j, 0:R0], rhs, start=j == 0, stop=j == EC - 1)
                    last = mm(ps[0:3 * QD, 2 + th, :], wx[:, j, R0:R0 + 3 * QD], rhs, start=j == 0, stop=j == EC - 1)
            last.then_inc(s["x_mm"], 1)

            pe.wait_ge(s["dtr_ready"], 1)
            for j, b in enumerate((4, 6, 0, 2)):
                if b == 2:
                    pe.wait_ge(s["bc_parts"], 1)
                for th in range(NH):
                    last = mm(ps[:, b + th, :], wdt[:, j * P:(j + 1) * P], dtr[:, th * HT:(th + 1) * HT],
                              start=True, stop=True)
                last.then_inc(s["dt_mm"], 1)

            pe.wait_ge(s["bc_parts"], 1)
            pe.wait_ge(s["dt_ready"], EC)
            for th in range(NH):
                def bcast(n, r, h):
                    toks = bcp[:, h * HT:(h + 1) * HT]
                    mm(ps[:, 4 + r % 2, :], sel[:, n, :], toks, start=True, stop=True)
                    mm(ps[:, 6 + r % 2, :], sel[:, n + NS, :], toks, start=True, stop=True)\
                        .then_inc(s["bc_bcast"], 1)

                def group(i, last_group):
                    for r in range(4):
                        n = 4 * i + r
                        it = NS * th + n
                        if not (last_group and r and th == NH - 1):
                            pe.wait_ge(s["bc_copied"], it + 2)
                            if last_group and r:
                                bcast(r - 1, r + 1, th + 1)
                            else:
                                bcast(n + 3, r + 1, th)
                        pe.wait_ge(s["cmul_dve"], it + 1)
                        for j in range(EC):
                            last = mm(ps[:, j, :], ident[:], pb[:, r, j, :], start=False, stop=last_group and r == 3)
                        last.then_inc(s["sum_done"], 1)

                if th == 0:
                    for n in range(3):
                        if n == 2:
                            pe.wait_ge(s["bc_copied"], 1)
                        bcast(n, n, 0)
                else:
                    pe.wait_ge(s["y_evac"], th)
                for j in range(EC):
                    clear(j)
                with pe.Fori(0, NS // 4 - 1) as i:
                    group(i, False)
                group(NS // 4 - 1, True)

            pe.wait_ge(s["ld_ffn0"], 48)
            for c in range(TC):
                if c == 0:
                    pe.wait_ge(s["y_gated_a"], 1)
                if c == HC:
                    pe.wait_ge(s["y_gated_b"], 1)
                for j in range(EC):
                    last = mm(ps[:, (4 + c) % 8, 0:D], hc[:, j, c * P:(c + 1) * P], wo0[:, j, :],
                              start=j == 0, stop=j == EC - 1)
                last.then_inc(s["out_mm"], 1)

            ln_transposes(1)
            pe.wait_ge(s["ln_h"], 8)
            for c in range(TC):
                for k in range(KC):
                    last = mm(ps[:, 4 + c // 2, (c % 2) * 136:(c % 2) * 136 + 136], hT[:, k, c * P:(c + 1) * P],
                              wf0[:, k, D:D + E0 + P], start=k == 0, stop=k == KC - 1)
            last.then_inc(s["f0_mm"], 1)
            for c in range(TC):
                if c % 2 == 0:
                    clear(c // 2)
                for k in range(KC):
                    mm(ps[:, c // 2, (c % 2) * D:(c % 2 + 1) * D], hT[:, k, c * P:(c + 1) * P], wf0[:, k, 0:D],
                       start=False, stop=False)
            pe.wait_ge(s["f0_t"], 1)
            for c in range(TC):
                last = nc.tensor.transpose(ps[:, 4 + c // HC, (c % HC) * P:(c % HC + 1) * P], ffn0_t[:, c, :], ident[:])
            last.then_inc(s["f0_T"], 1)
            pe.wait_ge(s["f0_tT"], 1)
            for c in range(TC):
                last = mm(ps[:, c // 2, (c % 2) * D:(c % 2 + 1) * D], ffn0_tT[:, c * P:(c + 1) * P], wlb[:, :],
                          start=False, stop=c % 2 == 1)
            last.then_inc(s["f0_lora"], 1)

            ln_transposes(2)

            pe.wait_ge(s["ln_h"], 12)
            pe.wait_ge(s["w_scaled"], 1)
            for c in range(TC):
                for k in range(KC):
                    last = mm(ps[:, 4, c * 2 * H:(c + 1) * 2 * H], hT[:, k, c * P:(c + 1) * P], wvif[:, k, D:D + 2 * H],
                              start=k == 0, stop=k == KC - 1)
            last.then_inc(s["z_mm"], 1)
            pe.wait_ge(s["sq_ready"], KC)
            for c in range(TC):
                for k in range(KC):
                    last = mm(ps[:, 5, c:c + 1], sq[:, k, c * P:(c + 1) * P], ones[:, 0:1], start=k == 0, stop=k == KC - 1)
            last.then_inc(s["ss_mm"], 1)

            def project(w, g, b):
                for th in range(NH):
                    for k in range(KC):
                        last = mm(ps[:, b + th, :], w[:, k, g * P:(g + 1) * P],
                                  hT[:, k, th * HT:(th + 1) * HT], start=k == 0, stop=k == KC - 1)
                return last

            project(wk, 0, 6).then_inc(s["k_mm"], 1)
            project(wk, 1, 0).then_inc(s["k_mm"], 1)
            for c in range(TC):
                b = 6 * (1 - c % 2)
                if c == 2:
                    pe.wait_ge(s["lif_ready"], 1)
                    for a in range(2):
                        for t in range(TC):
                            last = nc.tensor.transpose(ps[0:3 * QD, 2 + 2 * a + t // HC, (t % HC) * P:(t % HC + 1) * P],
                                                       lif[:, a, t, :], ident[:])
                    last.then_inc(s["lif_T"], 1)
                if c < 2:
                    pe.wait_ge(s["k_sb"], c + 1)
                else:
                    pe.wait_ge(s["vo_sb"], c - 1)
                for k in range(KC):
                    mm(ps[:, b, 0:D], hT[:, k, c * P:(c + 1) * P], wvif[:, k, 0:D], start=k == 0, stop=k == KC - 1)
                for k in range(KC):
                    last = mm(ps[:, b + 1, 0:D], hT[:, k, c * P:(c + 1) * P], wog[:, k, :], start=k == 0, stop=k == KC - 1)
                last.then_inc(s["v_mm"], 1)
            pe.wait_ge(s["vo_sb"], TC - 1)
            project(wq, 0, 6).then_inc(s["q_mm"], 1)
            pe.wait_ge(s["vo_sb"], TC)
            project(wq, 1, 0).then_inc(s["q_mm"], 1)
            pe.wait_ge(s["row_tok"], 1)
            for a, row in enumerate((rowA, rowG, rowM)):
                for c in range(TC):
                    col = (a * TC + c) * H
                    last = nc.tensor.transpose(ps[:, 2, col:col + H], row[0:H, c * P:(c + 1) * P], ident[0:H, 0:H])
            last.then_inc(s["tok_T"], 1)
            for c in range(TC):
                if c == HC:
                    pe.wait_ge(s["q_sb"], 1)
                for g in range(HG):
                    col = (c % 2) * D + g * P
                    last = nc.tensor.transpose(ps[:, 4 + c // 2, col:col + P], kT[:, g, c * P:(c + 1) * P], ident[:])
            last.then_inc(s["kT_T"], 1)
            pe.wait_ge(s["row_parts"], 1)
            ends = gp[:, P - 1:T:P]
            for h in range(H):
                mm(ps[:, 3, h * TC:(h + 1) * TC], sel[:, h, :], ends, start=True, stop=True)
            for g in range(HG):
                last = mm(ps[:, 3, (H + g) * TC:(H + g + 1) * TC], selr[:, g, :], ends, start=True, stop=True)
            last.then_inc(s["rr_mm"], 1)
            pe.wait_ge(s["q_sb"], HG)
            for g in range(HG):
                if g:
                    pe.wait_ge(s["qw_arg"], g)
                for th in range(NH):
                    last = mm(ps[:, th, :], selr[:, g, :], gp[:, th * HT:(th + 1) * HT], start=True, stop=True)
                last.then_inc(s["qg_mm"], 1)
            pe.wait_ge(s["w_arg"], 1)
            pe.wait_ge(s["w_exp"], 1)
            for c in range(TC):
                if c % 2 == 0:
                    pe.wait_ge(s["ks_ready"], c // 2 + 1)
                for h in range(H):
                    g, r = h // 4, h % 4
                    col = (c % 4) * HG * VE + g * VE
                    last = mm(ps[QD * r:QD * (r + 1), 2 + c // 4, col:col + VE], ks[:, c, h, :], vext[:, c, h, :],
                              start=True, stop=True)
                last.then_inc(s["state_mm"], 1)

            def g_rows(c):
                if c:
                    pe.wait_ge(s["arg_ready"], c)
                for h in range(H):
                    last = mm(ps[:, 4 + h // 4, (h % 4) * P:(h % 4 + 1) * P], sel[:, h, :], gp[:, c * P:(c + 1) * P],
                              start=True, stop=True)
                last.then_inc(s["g_mm"], 1)

            def scores(c):
                if c >= 2:
                    pe.wait_ge(s["pr_ready"], c - 1)
                for g in range(HG):
                    last = mm(ps[:, 2 * (c % 2) + g, :], kT[:, g, c * P:(c + 1) * P],
                              qbd[:, g, c].rearrange("p r t -> p (r t)"), start=True, stop=True)
                last.then_inc(s["s_mm"], 1)

            def outputs(c):
                b = 6 + c % 2
                if c >= 2:
                    pe.wait_ge(s["num_ready"], c - 1)
                clear(b)
                for g in range(HG if c else 0):
                    mm(ps[:, b, g * 4 * VE:(g + 1) * 4 * VE], qw[:, g, c * P:(c + 1) * P],
                       sbd[:, c - 1, g].rearrange("p r v -> p (r v)"), start=False, stop=False)
                if c + 2 < TC:
                    g_rows(c + 2)
                pe.wait_ge(s["pr_ready"], c + 1)
                for h in range(H):
                    last = mm(ps[:, b, h * VE:(h + 1) * VE], pr[:, c % 2, h, :], vext[:, c, h, :],
                              start=False, stop=h == H - 1)
                last.then_inc(s["intra_mm"], 1)

            pe.wait_ge(s["ks_ready"], 4)
            g_rows(0)
            pe.wait_ge(s["qbd_act"], 4)
            pe.wait_ge(s["qbd_dve"], 2)
            pe.wait_ge(s["qbd_pool"], 2)
            pe.wait_ge(s["qw_arg"], HG)
            scores(0)
            pe.wait_ge(s["state_done"], TC - 1)
            scores(1)
            g_rows(1)
            pe.wait_ge(s["sbd_ready"], 1)
            pe.wait_ge(s["qw_ready"], 1)
            for c in range(TC):
                outputs(c)
                if c + 2 < TC:
                    scores(c + 2)

            for th in range(NH):
                pe.wait_ge(s["ho_ready"], th + 1)
                for k in range(KC):
                    for c in range(HC):
                        last = nc.tensor.transpose(ps[:, 2 * k + th, c * P:(c + 1) * P],
                                                   ho_tok[:, th * HC + c, k * P:(k + 1) * P], ident[:])
                last.then_inc(s["ho_T"], 1)
            pe.wait_ge(s["hoT_ready"], 4)
            for m in range(KC):
                for th in range(NH):
                    for k in range(KC):
                        last = mm(ps[:, 4 + 2 * m + th, :], wout1[:, k, m * P:(m + 1) * P],
                                  hoT[:, k, th * HT:(th + 1) * HT], start=k == 0, stop=k == KC - 1)
                last.then_inc(s["wo_mm"], 1)

            pe.wait_ge(s["x1_ready"], KC)
            pe.wait_ge(s["w_scaled"], 2)
            for f in range(FC):
                b = 4 * (f % 2)
                if f == 1:
                    pe.wait_ge(s["sq2_ready"], KC)
                    for th in range(NH):
                        for k in range(KC):
                            last = mm(ps[:, 4 + th, :], ones[:], sq[:, k, th * HT:(th + 1) * HT],
                                      start=k == 0, stop=k == KC - 1)
                    last.then_inc(s["ss2_mm"], 1)
                    pe.wait_ge(s["rms2_sd"], 1)
                if f >= 2:
                    pe.wait_ge(s["gu_used"], f - 1)
                for w, o in ((wg, 0), (wu, 2)):
                    for th in range(NH):
                        for k in range(KC):
                            last = mm(ps[:, b + o + th, :], w[:, k, f * P:(f + 1) * P], x1T[:, k, th * HT:(th + 1) * HT],
                                      start=k == 0, stop=k == KC - 1)
                last.then_inc(s["gu_mm"], 1)
            pe.wait_ge(s["ld_down"], 16)

            def down_first(c):
                clear(c)
                for k in range(KC):
                    mm(ps[:, c, k * P:(k + 1) * P], x1T[:, k, c * P:(c + 1) * P], ident[:], start=False, stop=False)
                for f in range(FC - 1):
                    mm(ps[:, c, 0:D], gg[:, f, c * P:(c + 1) * P], wd[:, f, :], start=False, stop=False)

            def down_last(c):
                mm(ps[:, c, 0:D], gg[:, FC - 1, c * P:(c + 1) * P], wd[:, FC - 1, :], start=False, stop=True)\
                    .then_inc(s["down_mm"], 1)

            pe.wait_ge(s["gg_ready"], FC - 1)
            for c in range(HC):
                down_first(c)
            pe.wait_ge(s["gg_ready"], FC)
            for c in range(HC):
                down_last(c)
            for c in range(HC, TC):
                down_first(c)
                down_last(c)

            ln_transposes(3)
            pe.wait_ge(s["ln_h"], 16)
            pe.wait_ge(s["ld_moe"], 80)
            for c in range(TC):
                for k in range(KC):
                    last = mm(ps[:, 4, c * E1:(c + 1) * E1], hT[:, k, c * P:(c + 1) * P], wg1[:, k, :],
                              start=k == 0, stop=k == KC - 1)
            last.then_inc(s["z1_mm"], 1)
            pe.wait_ge(s["dw_ready"], 1)
            for c in range(TC):
                last = nc.tensor.transpose(ps[0:3 * QD, 6 + c // HC, (c % HC) * P:(c % HC + 1) * P], dwx[:, c, :], ident[:])
            last.then_inc(s["dw_T"], 1)
            pe.wait_ge(s["dw_parts"], 1)
            pe.wait_ge(s["h_split"], 1)
            for th in range(NH):
                half = slice(th * HT, (th + 1) * HT)

                def up(ic, r):
                    for w, b in ((w1, 2), (w3, 4)):
                        for k in range(KC):
                            for part in range(2):
                                mm(ps[:, b + r, :], w[:, k, bass.ts(ic, P)], h16[:, part, k, half],
                                   start=(k == 0 and part == 0), stop=(k == KC - 1 and part == 1))
                    mm(ps[:, 6 + r, :], selx[:, ic, :], dwp[:, half], start=True, stop=True).then_inc(s["up_mm"], 1)

                def down(ic, r, last_one):
                    pe.wait_ge(s["glo_ready"], IC * th + ic + 1)
                    for c in range(HC):
                        for part in range(2):
                            last = mm(ps[:, c // 2, (c % 2) * D:(c % 2 + 1) * D], g16[:, r, part, c * P:(c + 1) * P],
                                      w2[:, ic, :], start=False,
                                      stop=last_one and c % 2 == 1 and part == 1)
                    last.then_inc(s["acc_mm"], 1)

                if th:
                    pe.wait_ge(s["g_ready"], IC * th)
                    pe.wait_ge(s["x_out"], th)
                for b in range(2):
                    clear(b)
                def pair(i, first):
                    for r in range(2):
                        if not (first and r == 0):
                            pe.wait_ge(s["g_ready"], IC * th + 2 * i + r)
                        up(2 * i + r + 1, 1 - r)
                        down(2 * i + r, r, False)

                up(0, 0)
                if th == 0:
                    pair(0, True)
                with pe.Fori(1 if th == 0 else 0, IC // 2) as i:
                    pair(i, False)
                down(IC - 1, 0, True)

        @block.scalar
        def _(act):
            A = nc.scalar.activation
            step = [0]

            def then(ins):
                step[0] += 1
                ins.then_inc(s["act_step"], 1)
                act.wait_ge(s["act_step"], step[0])

            act.dma_start(cs[:], d["c"]).then_inc(s["ld_mod"], 16)
            for l in range(2):
                act.dma_start(wmod[:, l], d["wmod"][l]).then_inc(s["ld_mod"], 16)
            act.wait_ge(s["ld_mod"], 48)
            A(scs[:], cs[:], ACT.Silu).then_inc(s["c_silu"], 1)

            def layernorm(n, layer, shift, scale):
                act.wait_ge(s["ln_var"], n + 1)
                A(sd[:], ve[:], ACT.Sqrt).then_inc(s["ln_sd"], 1)
                for th in range(NH):
                    act.wait_ge(s["ln_T"], NH * n + th + 1)
                    for k in range(KC):
                        A(hT[:, k, th * HT:(th + 1) * HT], ps[:, 2 * k + th, :], ACT.Identity,
                          bias=modc[:, layer, shift, k:k + 1], scale=modc[:, layer, scale, k:k + 1])\
                            .then_inc(s["ln_h"], 1)

            act.wait_ge(s["mod_col"], 1)
            layernorm(0, 0, 0, 1)
            act.wait_ge(s["zeroed"], 3)
            for g in range(EC):
                act.wait_ge(s["in_mm"], g + 1)
                A(hpad[:, g, TAPS - 1:], banks(2 * ((g + 2) % 4), 2), ACT.Copy).then_inc(s["in_evac"], 1)
            for g in range(EC, 2 * EC):
                act.wait_ge(s["in_mm"], g + 1)
                A(gate[:, g - EC, :], banks(2 * ((g + 2) % 4), 2), ACT.Silu).then_inc(s["in_evac"], 1)
            for j in range(EC):
                act.wait_ge(s["conv_done"], j + 1)
                A(hc[:, j, :], cv[:, j, :], ACT.Silu).then_inc(s["hc_ready"], 1)
            act.wait_ge(s["ld_mix"], 64)
            then(A(alog[:], alog[:], ACT.Exp))
            nc.scalar.mul(aneg[:], alog[:], -1.0).then_inc(s["aneg_ready"], 1)
            act.wait_ge(s["x_mm"], 1)
            A(dtr[:], banks(0, 2), ACT.Copy).then_inc(s["dtr_ready"], 1)
            for j, b in enumerate((4, 6, 0, 2)):
                act.wait_ge(s["dt_mm"], j + 1)
                A(cv[:, j, :], banks(b, 2), ACT.Abs, bias=small0[:, j, 5:6]).then_inc(s["abs_done"], 1)
            act.wait_ge(s["abs_done"], EC)
            for j in range(EC):
                A(cv[:, j, :], cv[:, j, :], ACT.Exp, scale=-1.0).then_inc(s["sp_exp"], 1)
            for j in range(EC):
                act.wait_ge(s["sp_rest"], j + 1)
                A(hpad[:, j, 0:T], hpad[:, j, 0:T], ACT.Ln).then_inc(s["sp_ln"], 1)

            act.wait_ge(s["dt_ready"], EC)
            act.wait_ge(s["u_ready"], EC)
            act.wait_ge(s["aneg_ready"], 1)
            for th in range(NH):
                half = slice(th * HT, (th + 1) * HT)

                def copy_bc(it, r, first):
                    act.wait_ge(s["bc_bcast"], it + 1)
                    if not first:
                        act.wait_ge(s["cmul_dve"], it - 3)
                    A(bsb[:, r % 4, :], ps[:, 4 + r % 2, :], ACT.Copy)
                    A(csb[:, r % 4, :], ps[:, 6 + r % 2, :], ACT.Copy).then_inc(s["bc_copied"], 1)

                def group(i, first, last_group):
                    for r in range(4):
                        it = NS * th + 4 * i + r
                        if not first:
                            act.wait_ge(s["scan_done"], it - 3)
                        for j in range(EC):
                            last = A(dA[:, r, j, :], dt_[:, j, half], ACT.Exp, scale=aneg[:, 4 * i + r, j:j + 1])
                        last.then_inc(s["dA_ready"], 1)
                        if not (last_group and r >= 2 and th == NH - 1):
                            copy_bc(it + 2, r + 2, first and r < 2)

                if th == 0:
                    for n in range(2):
                        copy_bc(n, n, True)
                    group(0, True, False)
                with act.Fori(1 if th == 0 else 0, NS // 4 - 1) as i:
                    group(i, False, False)
                group(NS // 4 - 1, False, True)

            layernorm(1, 0, 2, 3)
            act.wait_ge(s["soft_arg"], 1)
            A(ga_[:, :, 0:E0], gl[:, :, 0:E0], ACT.Exp).then_inc(s["soft_exp"], 1)
            act.wait_ge(s["f0_T"], 1)
            A(ffn0_tT, banks(4, 2), ACT.Copy).then_inc(s["f0_tT"], 1)

            layernorm(2, 1, 0, 1)
            act.wait_ge(s["ln_h"], 12)
            for k in range(KC):
                A(sq[:, k, :], hT[:, k, :], ACT.Square).then_inc(s["sq_ready"], 1)
            act.wait_ge(s["ss_mm"], 1)
            A(rinv[:, 0], ps[:, 5, 0:TC], ACT.Sqrt, scale=1.0 / D, bias=eps[:, 0:1]).then_inc(s["rms_sd"], 1)
            act.wait_ge(s["z_in"], 1)
            A(zt[:], zif[:], ACT.Tanh, scale=1.0 / CAP).then_inc(s["z_tanh"], 1)
            act.wait_ge(s["z_tanh"], 1)
            A(lw[:, 0], zt[:, :, H:2 * H], ACT.Exp, scale=-CAP).then_inc(s["z_exp"], 1)
            act.wait_ge(s["z_w"], 1)
            A(lw[:, 2], lw[:, 1], ACT.Ln).then_inc(s["z_ln"], 1)
            for c in range(TC):
                b = 6 * (1 - c % 2)
                act.wait_ge(s["v_mm"], c + 1)
                A(vext[:, c, :, 0:DV], ps[:, b, 0:D].rearrange("p (h v) -> p h v", h=H), ACT.Identity,
                  scale=rinv[:, 1, c:c + 1])
                A(sg[:, c, :], ps[:, b + 1, 0:D], ACT.Sigmoid, scale=rinv[:, 1, c:c + 1]).then_inc(s["vo_sb"], 1)
            for g in range(HG):
                act.wait_ge(s["q_mm"], g + 1)
                nc.scalar.mul(qT[:, g, :], banks(6 * (1 - g), 2), 0.25).then_inc(s["q_sb"], 1)
            act.wait_ge(s["tok_T"], 1)
            A(agt[:, 2].rearrange("p c h -> p (c h)"), ps[:, 2, 2 * TC * H:3 * TC * H], ACT.Exp, scale=-1.0)\
                .then_inc(s["enm_ready"], 1)
            act.wait_ge(s["q_sb"], HG)
            act.wait_ge(s["v_ones"], 3)
            for g, r in ((0, 2), (0, 3), (1, 2), (1, 3)):
                rows = slice(QD * r, QD * (r + 1))
                A(qbd[rows, g, :, r, :], qT[rows, g, :].rearrange("p (c t) -> p c t", t=P), ACT.Copy)\
                    .then_inc(s["qbd_act"], 1)
            act.wait_ge(s["w_arg"], 1)
            A(wkt[:], wkt[:], ACT.Exp)
            A(dec[:, :, 1:], dec[:, :, 1:], ACT.Exp).then_inc(s["w_exp"], 1)
            for g in range(HG):
                act.wait_ge(s["qw_arg"], g + 1)
                A(qw[:, g, P:], qw[:, g, P:], ACT.Exp).then_inc(s["qw_exp"], 1)

            def sums_out(c):
                act.wait_ge(s["intra_mm"], c + 1)
                A(num[:, c].rearrange("p h v -> p (h v)"), ps[:, 6 + c % 2, 0:H * VE], ACT.Copy).then_inc(s["num_ready"], 1)

            for c in range(TC):
                act.wait_ge(s["arg_masked"], c + 1)
                A(arg[:, c % 2], arg[:, c % 2], ACT.Exp).then_inc(s["e_ready"], 1)
                if c >= 2:
                    sums_out(c - 2)
            sums_out(TC - 2)
            sums_out(TC - 1)
            act.wait_ge(s["den_ready"], 1)
            A(sq_tok, ho_head, ACT.Square).then_inc(s["num_sq"], 1)
            act.wait_ge(s["var_ready"], 1)
            A(nden[:, 2], nden[:, 1], ACT.Sqrt, scale=1.0 / DV, bias=eps[:, 0:1]).then_inc(s["var_sd"], 1)
            for th in range(NH):
                act.wait_ge(s["ho_T"], th + 1)
                for k in range(KC):
                    A(hoT[:, k, th * HT:(th + 1) * HT], ps[:, 2 * k + th, :], ACT.Copy).then_inc(s["hoT_ready"], 1)
            for k in range(KC):
                act.wait_ge(s["x1_ready"], k + 1)
                if k == 0:
                    act.wait_ge(s["wo_mm"], KC)
                A(sq[:, k, :], x1T[:, k, :], ACT.Square).then_inc(s["sq2_ready"], 1)
            act.wait_ge(s["ss2_mm"], 1)
            A(sd2[:, 0, :], banks(4, 2), ACT.Sqrt, scale=1.0 / D, bias=eps[:, 0:1]).then_inc(s["rms2_sd"], 1)
            for f in range(FC):
                act.wait_ge(s["g_scaled"], f + 1)
                A(sil[:, f % 2, :], sil[:, f % 2, :], ACT.Silu).then_inc(s["sil_ready"], 1)

            layernorm(3, 1, 2, 3)
            act.wait_ge(s["z1_mm"], 1)
            A(ga_[:].rearrange("p c e -> p (c e)"), ps[:, 4, 0:TC * E1], ACT.Exp, scale=-1.0).then_inc(s["z1_exp"], 1)
            for th in range(NH):
                def silu(ic, r, first):
                    m = IC * th + ic
                    act.wait_ge(s["up_mm"], m + 1)
                    if not first:
                        act.wait_ge(s["g_ready"], m - 1)
                    A(sa_[:, r, :], ps[:, 2 + r, :], ACT.Silu).then_inc(s["moe_sil"], 1)

                silu(0, 0, th == 0)
                if th == 0:
                    silu(1, 1, True)
                    silu(2, 0, False)
                with act.Fori(1 if th == 0 else 0, IC // 2) as i:
                    silu(2 * i + 1, 1, False)
                    silu(2 * i + 2, 0, False)

        @block.gpsimd
        def _(pool):
            tt = nc.gpsimd.tensor_tensor
            nc.gpsimd.memset(ones[:], 1.0).then_inc(s["ones_ready"], 1)
            nc.gpsimd.memset(zero16[:], 0.0).then_inc(s["ones_ready"], 1)
            nc.gpsimd.memset(eps[:], RMS_EPS).then_inc(s["ones_ready"], 1)
            pool.wait_ge(s["mod_mm"], 1)
            nc.gpsimd.memset(hpad[:, :, 0:TAPS - 1], 0.0).then_inc(s["zeroed"], 1)
            pool.wait_ge(s["zeroed"], 1)
            nc.gpsimd.memset(bcp[3 * QD:P, :], 0.0).then_inc(s["zeroed"], 1)
            pool.wait_ge(s["zeroed"], 2)
            nc.gpsimd.memset(carry[:], 0.0).then_inc(s["zeroed"], 1)
            pool.wait_ge(s["zeroed"], 3)
            for j in range(EC):
                pool.wait_ge(s["dt_ready"], j + 1)
                tt(u[:, j, :], dt_[:, j, :], hc[:, j, :], ALU.mult).then_inc(s["u_ready"], 1)
            pool.wait_ge(s["u_ready"], EC)

            def dbu(it, r, th, first):
                pool.wait_ge(s["bc_copied"], it + 1)
                if not first:
                    pool.wait_ge(s["sum_done"], it - 3)
                tt(pb[:, r], u[:, :, th * HT:(th + 1) * HT], over(bsb[:, r, :].unsqueeze(1), [P, EC, HT]), ALU.mult)\
                    .then_inc(s["dbu_done"], 1)

            for r in range(4):
                dbu(r, r, 0, True)
            with pool.Fori(1, NS // 4) as i:
                for r in range(4):
                    dbu(4 * i + r, r, 0, False)
            with pool.Fori(0, NS // 4) as i:
                for r in range(4):
                    dbu(4 * i + r + NS, r, 1, False)
            pool.wait_ge(s["y_evac"], 1)
            tt(hc[:, :, 0:HT], hc[:, :, 0:HT], gate[:, :, 0:HT], ALU.mult).then_inc(s["y_gated_a"], 1)

            pool.wait_ge(s["out_mm"], TC)
            nc.gpsimd.memset(vext[:, :, :, DV:VE], 1.0).then_inc(s["v_ones"], 1)
            pool.wait_ge(s["v_ones"], 1)
            nc.gpsimd.memset(gp[3 * QD:P, :], 0.0).then_inc(s["v_ones"], 1)
            pool.wait_ge(s["v_ones"], 2)
            nc.gpsimd.memset(qbd[:], 0.0).then_inc(s["v_ones"], 1)
            pool.wait_ge(s["v_ones"], 3)
            nc.gpsimd.memset(sbd[:], 0.0).then_inc(s["v_ones"], 1)
            pool.wait_ge(s["v_ones"], 4)
            nc.gpsimd.memset(lif[:], 0.0).then_inc(s["rows_zero"], 1)
            pool.wait_ge(s["rows_zero"], 1)
            nc.gpsimd.memset(rowM[0:3 * QD, :], 0.0).then_inc(s["rows_zero"], 1)
            pool.wait_ge(s["rows_zero"], 2)
            pool.wait_ge(s["ld_attn"], 8 * 16)
            for k in range(KC):
                for w in (wvif, wk, wog, wq):
                    last = nc.gpsimd.tensor_scalar(w[:, k, :], w[:, k, :], small1[:, 0, k:k + 1], None, ALU.mult)
            last.then_inc(s["w_scaled"], 1)
            pool.wait_ge(s["ld_gateup"], 32)
            for k in range(KC):
                for w in (wg, wu):
                    last = nc.gpsimd.tensor_scalar(w[:, k, :], w[:, k, :], small1[:, 1, k:k + 1], None, ALU.mult)
            last.then_inc(s["w_scaled"], 1)
            pool.wait_ge(s["w_scaled"], 2)
            pool.wait_ge(s["q_sb"], 1)
            for r in range(2):
                rows = slice(QD * r, QD * (r + 1))
                nc.gpsimd.tensor_copy(qbd[rows, 0, :, r, :], qT[rows, 0, :].rearrange("p (c t) -> p c t", t=P))\
                    .then_inc(s["qbd_pool"], 1)
                pool.wait_ge(s["qbd_pool"], r + 1)
            pool.wait_ge(s["ld_attn"], 8 * 16)
            tt(sg[:], sg[:], over(mhw[:].unsqueeze(1), [P, TC, D]), ALU.mult).then_inc(s["sg_ready"], 1)
            for c in range(TC):
                pool.wait_ge(s["arg_ready"], c + 1)
                a = arg[:, c % 2]
                nc.gpsimd.affine_select(out=a, in_=a, compare_op=ALU.is_ge, fill=-1e30, base=0,
                                        pattern=[[0, H], [1, P]], channel_multiplier=-1)\
                    .then_inc(s["arg_masked"], 1)
            pool.wait_ge(s["down_mm"], TC)
            nc.gpsimd.memset(dwx[:], 0.0).then_inc(s["dwx_zero"], 1)
            pool.wait_ge(s["dwx_zero"], 1)
            nc.gpsimd.memset(dwp[3 * QD:P, :], 0.0).then_inc(s["dwx_zero"], 1)
            pool.wait_ge(s["dwx_zero"], 2)
            wide = dwx[:].rearrange("p c (q e) -> p c q e", q=3)
            for q in range(3):
                nc.gpsimd.memset(wide[:, :, q, E1:E1 + 1], 1.0).then_inc(s["dwx_zero"], 1)
            for th in range(NH):
                def low_part(ic, r):
                    m = IC * th + ic
                    pool.wait_ge(s["ghi_ready"], m + 1)
                    tt(g16[:, r, 1, :], gh1[:, r, :], g16[:, r, 0, :], ALU.subtract).then_inc(s["glo_ready"], 1)

                low_part(0, 0)
                with pool.Fori(0, IC // 2) as i:
                    low_part(2 * i + 1, 1)
                    low_part(2 * i + 2, 0)

        @block.vector
        def _(dve):
            V = nc.vector
            step = [0]

            def then(ins):
                step[0] += 1
                ins.then_inc(s["dve_step"], 1)
                dve.wait_ge(s["dve_step"], step[0])

            dve.wait_ge(s["c_silu"], 1)
            V.tensor_copy(scb[:], over(scs[:].unsqueeze(3), [P, 2, KC, P])).then_inc(s["c_wide"], 1)

            def layernorm(n):
                for c in range(TC):
                    if n == 0:
                        dve.wait_ge(s["ld_x0" if c < HC else "ld_x1"], 16)
                    last = V.bn_stats(st[:, c, :], x[:, c, :])
                then(last)
                for c in range(TC):
                    last = V.bn_aggr(mv[:, c, :], st[:, c, :])
                then(last)
                V.tensor_scalar(ve[:], mv[:, :, 1], LN_EPS, None, ALU.add).then_inc(s["ln_var"], 1)
                dve.wait_ge(s["ln_sd"], n + 1)
                then(V.reciprocal(rs[:], sd[:]))
                for c in range(TC):
                    V.tensor_scalar(xn[:, c, :], x[:, c, :], mv[:, c, 0:1], rs[:, c:c + 1], ALU.subtract, ALU.mult)\
                        .then_inc(s["ln_norm"], 1)

            dve.wait_ge(s["mod_mm"], 1)
            then(V.tensor_copy(modc[:].rearrange("p l n f -> p (l n f)"), ps[:, 0, 0:8 * KC]))
            scales = modc[:].rearrange("p l (a b) f -> p l a b f", b=2)
            for l in range(2):
                last = V.tensor_scalar(scales[:, l, :, 1, :], scales[:, l, :, 1, :], 1.0, None, ALU.add)
            last.then_inc(s["mod_col"], 1)
            for l in range(2):
                g2 = ps[:, 1 + l, :].rearrange("p (a f) -> p a f", a=2)
                then(V.tensor_copy(gt2[:], g2))
                then(V.scalar_tensor_tensor(gt1[:], gt2[:], -1.0, gt2[:], ALU.mult, ALU.max))
                V.tensor_scalar(gt1[:], gt1[:], 0.25, None, ALU.max)
                then(V.tensor_scalar(gt2[:], gt2[:], 0.0, 2.0, ALU.is_ge, ALU.mult))
                then(V.scalar_tensor_tensor(gbc[:, l], gt2[:], -1.0, gt1[:], ALU.add, ALU.mult))
            V.tensor_scalar(gt2[:, 0, :], gbc[:, 1, 1, :], WS, None, ALU.mult).then_inc(s["gate_vec"], 1)
            layernorm(0)

            dve.wait_ge(s["ld_mix"], 64)
            dve.wait_ge(s["zeroed"], 3)
            for j in range(EC):
                dve.wait_ge(s["in_evac"], j + 1)
                w = small0[:, j, :]
                then(V.tensor_scalar(cv[:, j, :], hpad[:, j, 0:T], w[:, 0:1], w[:, 4:5], ALU.mult, ALU.add))
                for k in range(1, TAPS):
                    last = V.scalar_tensor_tensor(cv[:, j, :], hpad[:, j, k:k + T], w[:, k:k + 1], cv[:, j, :],
                                                  ALU.mult, ALU.add)
                    if k < TAPS - 1:
                        then(last)
                last.then_inc(s["conv_done"], 1)

            def three_parts(dst, src, high, rest, done):
                a, b, c = (slice(QD * q, QD * (q + 1)) for q in range(3))
                then(V.tensor_copy(high[0:3 * QD], src))
                V.tensor_copy(dst[a], high[a])
                then(V.tensor_tensor(rest[0:3 * QD], src, high[0:3 * QD], ALU.subtract))
                V.tensor_copy(dst[b], rest[b])
                then(V.tensor_copy(high[c], rest[c]))
                V.tensor_tensor(dst[c], rest[c], high[c], ALU.subtract).then_inc(done, 1)

            dve.wait_ge(s["x_mm"], 1)
            three_parts(bcp, banks(2, 2, 3 * QD), bch, bcr, s["bc_parts"])
            for j, b in enumerate((4, 6, 0, 2)):
                dve.wait_ge(s["abs_done"], j + 1)
                then(V.tensor_scalar(dt_[:, j, :], banks(b, 2), small0[:, j, 5:6], 0.0, ALU.add, ALU.max))
            for j in range(EC):
                dve.wait_ge(s["sp_exp"], j + 1)
                then(V.tensor_scalar(hpad[:, j, 0:T], cv[:, j, :], 1.0, None, ALU.add))
                V.scalar_tensor_tensor(cv[:, j, :], hpad[:, j, 0:T], -1.0, cv[:, j, :], ALU.add, ALU.subtract)\
                    .then_inc(s["sp_rest"], 1)
            for j in range(EC):
                dve.wait_ge(s["sp_rest"], j + 1)
                then(V.tensor_tensor(dt_[:, j, :], dt_[:, j, :], cv[:, j, :], ALU.subtract))
                dve.wait_ge(s["sp_ln"], j + 1)
                V.tensor_tensor(dt_[:, j, :], dt_[:, j, :], hpad[:, j, 0:T], ALU.add).then_inc(s["dt_ready"], 1)

            def y_out(th):
                half = slice(th * HT, (th + 1) * HT)
                dve.wait_ge(s["sum_done"], NS * (th + 1))
                for j in range(EC):
                    last = V.scalar_tensor_tensor(hc[:, j, half], hc[:, j, half], small0[:, j, 6:7], ps[:, j, :],
                                                  ALU.mult, ALU.add)
                last.then_inc(s["y_evac"], 1)

            for th in range(NH):
                def group(i):
                    for r in range(4):
                        n = 4 * i + r
                        it = NS * th + n
                        dve.wait_ge(s["dA_ready"], it + 1)
                        dve.wait_ge(s["dbu_done"], it + 1)
                        for j in range(EC):
                            start = 0.0 if th == 0 else carry[:, n, j:j + 1]
                            last = V.tensor_tensor_scan(pb[:, r, j, :], dA[:, r, j, :], pb[:, r, j, :], start,
                                                        ALU.mult, ALU.add)
                        last.then_inc(s["scan_done"], 1)
                        dve.wait_ge(s["scan_done"], it + 1)
                        if th == 0:
                            V.tensor_copy(carry[:, n, :], pb[:, r, :, HT - 1]).then_inc(s["carry_saved"], 1)
                            dve.wait_ge(s["carry_saved"], it + 1)
                        dve.wait_ge(s["bc_copied"], it + 1)
                        V.tensor_tensor(pb[:, r], pb[:, r], over(csb[:, r, :].unsqueeze(1), [P, EC, HT]), ALU.mult)\
                            .then_inc(s["cmul_dve"], 1)
                        if th and isinstance(i, int) and r == 0:
                            y_out(th - 1)

                if th:
                    group(0)
                with dve.Fori(1 if th else 0, NS // 4) as i:
                    group(i)
            y_out(NH - 1)
            dve.wait_ge(s["y_evac"], NH)
            V.tensor_tensor(hc[:, :, HT:T], hc[:, :, HT:T], gate[:, :, HT:T], ALU.mult).then_inc(s["y_gated_b"], 1)

            def add_to_x(c, psum, g):
                then(V.tensor_tensor(tmpx[:], psum, over(g.unsqueeze(1), [P, 2, D]), ALU.mult))
                then(V.tensor_tensor(x[:, c:c + 2, :], x[:, c:c + 2, :], tmpx[:], ALU.add))

            for c in range(0, TC, 2):
                dve.wait_ge(s["out_mm"], c + 2)
                add_to_x(c, ps[:, (4 + c) % 8:(4 + c) % 8 + 2, 0:D], gbc[:, 0, 0, :])
            layernorm(1)

            def top2(v, e, scale):
                r_ = over(rev[:, E1 - e:E1].unsqueeze(1), [P, TC, e])
                one, key, v2 = ga_[:, :, 0:e], gb_[:, :, 0:e], gc_[:, :, 0:e]

                def wide(a):
                    return over(a.unsqueeze(2), [P, TC, e])

                then(V.tensor_reduce(gr[:, 0], v, AX_X, ALU.max))
                then(V.tensor_tensor(key, v, wide(gr[:, 0]), ALU.is_equal))
                then(V.tensor_tensor(key, key, r_, ALU.mult))
                then(V.tensor_reduce(gr[:, 1], key, AX_X, ALU.max))
                then(V.tensor_tensor(one, key, wide(gr[:, 1]), ALU.is_equal))
                then(V.scalar_tensor_tensor(v2, one, -4.0, v, ALU.mult, ALU.add))
                then(V.tensor_reduce(gr[:, 2], v2, AX_X, ALU.max))
                then(V.tensor_tensor(key, v2, wide(gr[:, 2]), ALU.is_equal))
                then(V.tensor_tensor(key, key, r_, ALU.mult))
                then(V.tensor_reduce(gr[:, 3], key, AX_X, ALU.max))
                then(V.tensor_tensor(key, key, wide(gr[:, 3]), ALU.is_equal))
                then(V.tensor_tensor(one, one, key, ALU.add))
                then(V.tensor_tensor(gr[:, 4], gr[:, 0], gr[:, 2], ALU.add))
                then(V.reciprocal(gr[:, 5], gr[:, 4]))
                then(V.tensor_tensor(key, v, one, ALU.mult))
                then(V.scalar_tensor_tensor(key, key, scale, wide(gr[:, 5]), ALU.mult, ALU.mult))

            dve.wait_ge(s["f0_mm"], 1)
            pair = ps[:, 4:8, 0:272].rearrange("p b (c n) -> p b c n", c=2)
            v = gl[:, :, 0:E0]
            then(V.tensor_copy(v.rearrange("p (b c) e -> p b c e", c=2), pair[:, :, :, 0:E0]))
            then(V.tensor_reduce(gr[:, 0], v, AX_X, ALU.max))
            V.tensor_tensor(v, v, over(gr[:, 0].unsqueeze(2), [P, TC, E0]), ALU.subtract).then_inc(s["soft_arg"], 1)
            dve.wait_ge(s["soft_exp"], 1)
            then(V.tensor_reduce(gr[:, 1], ga_[:, :, 0:E0], AX_X, ALU.add))
            then(V.reciprocal(gr[:, 2], gr[:, 1]))
            then(V.tensor_tensor(v, ga_[:, :, 0:E0], over(gr[:, 2].unsqueeze(2), [P, TC, E0]), ALU.mult))
            top2(v, E0, 16.0)
            cw = gb_[:, :, 0:E0].rearrange("p (b c) e -> p b c e", c=2)
            tw = ffn0_t.rearrange("p (b c) n -> p b c n", c=2)
            for c in range(2):
                last = V.tensor_tensor(tw[:, :, c, :].rearrange("p b (e r) -> p b e r", r=RL),
                                       pair[:, :, c, E0:136].rearrange("p b (e r) -> p b e r", r=RL),
                                       over(cw[:, :, c, :].unsqueeze(3), [P, 4, E0, RL]), ALU.mult)
            last.then_inc(s["f0_t"], 1)
            dve.wait_ge(s["f0_lora"], 1)
            for b in range(4):
                add_to_x(2 * b, ps[:, b, :].rearrange("p (c f) -> p c f", c=2), gbc[:, 0, 1, :])
            layernorm(2)

            dve.wait_ge(s["rms_sd"], 1)
            then(V.reciprocal(rinv[:, 1], rinv[:, 0]))
            dve.wait_ge(s["z_mm"], 1)
            then(V.tensor_tensor(zif[:], ps[:, 4, 0:TC * 2 * H].rearrange("p (c n) -> p c n", c=TC),
                                 over(rinv[:, 1].unsqueeze(2), [P, TC, 2 * H]), ALU.mult))
            V.tensor_tensor(zif[:], zif[:], over(bif[:].unsqueeze(1), [P, TC, 2 * H]), ALU.add).then_inc(s["z_in"], 1)
            dve.wait_ge(s["k_mm"], 1)
            V.tensor_copy(kT[:, 0, :], banks(6, 2)).then_inc(s["k_sb"], 1)

            dve.wait_ge(s["rows_zero"], 2)
            dve.wait_ge(s["z_tanh"], 1)
            for q in range(3):
                V.tensor_scalar(lif[:, 1, :, QD * q:QD * q + H], zt[:, :, 0:H], CAP, None, ALU.mult)
            dve.wait_ge(s["z_exp"], 1)
            V.tensor_scalar(lw[:, 1], lw[:, 0], 1.0, None, ALU.add).then_inc(s["z_w"], 1)
            dve.wait_ge(s["z_w"], 1)
            then(V.tensor_scalar(lw[:, 3], lw[:, 1], -1.0, None, ALU.add))
            then(V.tensor_tensor(lw[:, 3], lw[:, 0], lw[:, 3], ALU.subtract))
            then(V.reciprocal(lw[:, 0], lw[:, 1]))
            then(V.tensor_tensor(lw[:, 3], lw[:, 3], lw[:, 0], ALU.mult))
            dve.wait_ge(s["z_ln"], 1)
            then(V.tensor_tensor(lw[:, 3], lw[:, 3], lw[:, 2], ALU.add))
            for q in range(3):
                last = V.tensor_scalar(lif[:, 0, :, QD * q:QD * q + H], lw[:, 3], -1.0, None, ALU.mult)
            last.then_inc(s["lif_ready"], 1)
            dve.wait_ge(s["k_mm"], 2)
            V.tensor_copy(kT[:, 1, :], banks(0, 2)).then_inc(s["k_sb"], 1)
            dve.wait_ge(s["lif_T"], 1)
            R3 = slice(0, 3 * QD)
            then(V.tensor_tensor_scan(rowF[R3, :], banks(2, 2, 3 * QD), rowM[R3, :], 0.0, ALU.add, ALU.add))
            then(V.tensor_tensor(rowA[R3, :], banks(4, 2, 3 * QD), rowF[R3, :], ALU.subtract))
            then(V.tensor_tensor_scan(rowG[R3, :], rowA[R3, :], rowA[R3, :], -1e30, ALU.max, ALU.max))
            V.tensor_tensor(rowM[R3, :], rowF[R3, :], rowG[R3, :], ALU.add).then_inc(s["row_tok"], 1)
            dve.wait_ge(s["row_tok"], 1)
            three_parts(gp, rowG[R3, :], gh, rowF, s["row_parts"])
            dve.wait_ge(s["tok_T"], 1)
            dve.wait_ge(s["enm_ready"], 1)
            V.tensor_copy(agt[:, 0:2].rearrange("p a c h -> p (a c h)"), ps[:, 2, 0:2 * TC * H])
            dve.wait_ge(s["rr_mm"], 1)
            V.tensor_copy(rbc[:].rearrange("p h c -> p (h c)"), ps[:, 3, 0:H * TC])
            then(V.tensor_copy(rrow[:].rearrange("p g c -> p (g c)"), ps[:, 3, H * TC:(H + HG) * TC]))
            ends = rbc[:].rearrange("p h c -> p c h")
            V.tensor_tensor(wkt[:], agt[:, 0], ends, ALU.subtract)
            V.tensor_tensor(dec[:, :, 1:], rrow[:, :, 0:TC - 1], rrow[:, :, 1:], ALU.subtract).then_inc(s["w_arg"], 1)
            for g in range(HG):
                dve.wait_ge(s["qg_mm"], g + 1)
                V.tensor_tensor(qw[:, g, P:].rearrange("p (c t) -> p c t", t=P),
                                over(rrow[:, g, 0:TC - 1].unsqueeze(2), [P, TC - 1, P]),
                                banks(0, 2)[:, P:].rearrange("p (c t) -> p c t", t=P), ALU.subtract)\
                    .then_inc(s["qw_arg"], 1)
            for r in range(2):
                rows = slice(QD * r, QD * (r + 1))
                V.tensor_copy(qbd[rows, 1, :, r, :], qT[rows, 1, :].rearrange("p (c t) -> p c t", t=P))\
                    .then_inc(s["qbd_dve"], 1)
            dve.wait_ge(s["w_exp"], 1)
            then(V.tensor_tensor(wkt[:], wkt[:], over(rinv[:, 1].unsqueeze(2), [P, TC, H]), ALU.mult))
            dve.wait_ge(s["kT_T"], 1)
            for b in range(4):
                V.tensor_tensor(ks[:, 2 * b:2 * b + 2].rearrange("p c h n -> p (c h) n"),
                                ps[:, 4 + b, :].rearrange("p (ch n) -> p ch n", n=QR),
                                over(wkt[:, 2 * b:2 * b + 2].rearrange("p c h -> p (c h)").unsqueeze(2),
                                     [P, 2 * H, QR]), ALU.mult).then_inc(s["ks_ready"], 1)
            dve.wait_ge(s["qw_exp"], HG)
            V.tensor_tensor(qw[:, :, P:], qw[:, :, P:], qT[:, :, P:], ALU.mult).then_inc(s["qw_ready"], 1)
            for c in range(TC - 1):
                dve.wait_ge(s["state_mm"], 4 * (c // 4) + 4)
                for g in range(HG):
                    col = (c % 4) * HG * VE + g * VE
                    add = ps[:, 2 + c // 4, col:col + VE]
                    if c == 0:
                        last = V.tensor_copy(states[:, c, g, :], add)
                    else:
                        last = V.scalar_tensor_tensor(states[:, c, g, :], states[:, c - 1, g, :], dec[:, g, c:c + 1], add,
                                                      ALU.mult, ALU.add)
                last.then_inc(s["state_done"], 1)
                dve.wait_ge(s["state_done"], c + 1)

            dve.wait_ge(s["v_ones"], 4)
            for r in range(4):
                rows = slice(QD * r, QD * (r + 1))
                last = V.tensor_copy(sbd[rows, :, :, r, :], states[rows])
            last.then_inc(s["sbd_ready"], 1)

            def exponent(c):
                dve.wait_ge(s["g_mm"], c + 1)
                if c >= 2:
                    dve.wait_ge(s["pr_ready"], c - 1)
                V.tensor_tensor(arg[:, c % 2], over(agt[:, 0, c, :].unsqueeze(2), [P, H, P]),
                                banks(4, 2).rearrange("p (h t) -> p h t", h=H), ALU.subtract)\
                    .then_inc(s["arg_ready"], 1)

            exponent(0)
            for c in range(TC):
                if c + 1 < TC:
                    exponent(c + 1)
                dve.wait_ge(s["e_ready"], c + 1)
                dve.wait_ge(s["s_mm"], c + 1)
                if c >= 2:
                    dve.wait_ge(s["intra_mm"], c - 1)
                V.scalar_tensor_tensor(pr[:, c % 2].rearrange("p h t -> p (h t)"), banks(2 * (c % 2), 2),
                                       rinv[:, 1, c:c + 1], arg[:, c % 2].rearrange("p h t -> p (h t)"),
                                       ALU.mult, ALU.mult).then_inc(s["pr_ready"], 1)

            dve.wait_ge(s["num_ready"], TC)
            dve.wait_ge(s["enm_ready"], 1)
            nv = num[:].rearrange("p c h v -> p (c h) v")
            flat = [nden[:, a].rearrange("p c h -> p (c h)") for a in range(3)]
            then(V.scalar_tensor_tensor(nden[:, 0], num[:, :, :, DV], -1.0, num[:, :, :, DV], ALU.mult, ALU.max))
            own = over(rinv[:, 1].unsqueeze(2), [P, TC, H])
            then(V.tensor_tensor(nden[:, 0], nden[:, 0], own, ALU.mult))
            then(V.tensor_tensor(nden[:, 0], nden[:, 0], agt[:, 2], ALU.max))
            then(V.reciprocal(nden[:, 1], nden[:, 0]))
            then(V.tensor_tensor(nden[:, 1], nden[:, 1], own, ALU.mult))
            V.tensor_tensor(ho_head, nv[:, :, 0:DV], over(flat[1].unsqueeze(2), [P, TC * H, DV]), ALU.mult)\
                .then_inc(s["den_ready"], 1)
            dve.wait_ge(s["num_sq"], 1)
            V.tensor_reduce(flat[1], sq_tok, AX_X, ALU.add).then_inc(s["var_ready"], 1)
            dve.wait_ge(s["var_sd"], 1)
            then(V.reciprocal(nden[:, 0], nden[:, 2]))
            dve.wait_ge(s["sg_ready"], 1)
            for th in range(NH):
                rows = slice(th * HC * H, (th + 1) * HC * H)
                then(V.tensor_tensor(ho_head[:, rows], ho_head[:, rows],
                                     over(flat[0][:, rows].unsqueeze(2), [P, HC * H, DV]), ALU.mult))
                toks = slice(th * HC, (th + 1) * HC)
                V.tensor_tensor(ho_tok[:, toks], ho_tok[:, toks], sg[:, toks], ALU.mult).then_inc(s["ho_ready"], 1)
            for m in range(KC):
                dve.wait_ge(s["wo_mm"], m + 1)
                V.tensor_tensor(x1T[:, m, :], hT[:, m, :], banks(4 + 2 * m, 2), ALU.add).then_inc(s["x1_ready"], 1)
            dve.wait_ge(s["rms2_sd"], 1)
            then(V.reciprocal(sd2[:, 1], sd2[:, 0]))
            for f in range(FC):
                b = 4 * (f % 2)
                dve.wait_ge(s["gu_mm"], f + 1)
                V.tensor_tensor(sil[:, f % 2, :], banks(b, 2), sd2[:, 1], ALU.mult).then_inc(s["g_scaled"], 1)
                dve.wait_ge(s["sil_ready"], f + 1)
                V.tensor_tensor(gg[:, f, :], sil[:, f % 2, :], banks(b + 2, 2), ALU.mult).then_inc(s["gu_used"], 1)
                dve.wait_ge(s["gu_used"], f + 1)
                V.tensor_tensor(gg[:, f, :], gg[:, f, :], sd2[:, 1], ALU.mult).then_inc(s["gg_ready"], 1)
            for c in range(0, TC, 2):
                dve.wait_ge(s["down_mm"], c + 2)
                add_to_x(c, ps[:, c:c + 2, 0:D], gbc[:, 1, 0, :])
            layernorm(3)

            dve.wait_ge(s["ln_h"], 16)
            dve.wait_ge(s["down_mm"], TC)
            V.tensor_copy(h16[:, 0], hT[:]).then_inc(s["h_hi"], 1)
            dve.wait_ge(s["h_hi"], 1)
            V.tensor_tensor(h16[:, 1], hT[:], h16[:, 0], ALU.subtract).then_inc(s["h_split"], 1)
            dve.wait_ge(s["z1_exp"], 1)
            then(V.tensor_scalar(gl[:], ga_[:], 1.0, None, ALU.add))
            then(V.reciprocal(gl[:], gl[:]))
            top2(gl[:], E1, 1.0)
            dve.wait_ge(s["dwx_zero"], 5)
            wide = dwx[:].rearrange("p c (q e) -> p c q e", q=3)
            for q in range(3):
                last = V.tensor_copy(wide[:, :, q, 0:E1], gb_[:])
            last.then_inc(s["dw_ready"], 1)
            dve.wait_ge(s["dw_T"], 1)
            three_parts(dwp, banks(6, 2, 3 * QD), dwh, dwr, s["dw_parts"])
            for th in range(NH):
                def gated(ic, r, first):
                    m = IC * th + ic
                    dve.wait_ge(s["moe_sil"], m + 1)
                    V.tensor_tensor(sa_[:, r, :], sa_[:, r, :], ps[:, 4 + r, :], ALU.mult).then_inc(s["moe_prod"], 1)
                    dve.wait_ge(s["moe_prod"], m + 1)
                    if not first:
                        dve.wait_ge(s["glo_ready"], m - 1)
                    V.tensor_tensor(gh1[:, r, :], sa_[:, r, :], ps[:, 6 + r, :], ALU.mult).then_inc(s["g_ready"], 1)
                    dve.wait_ge(s["g_ready"], m + 1)
                    if not first:
                        dve.wait_ge(s["acc_mm"], m - 1)
                    V.tensor_copy(g16[:, r, 0, :], gh1[:, r, :]).then_inc(s["ghi_ready"], 1)

                gated(0, 0, th == 0)
                if th == 0:
                    gated(1, 1, True)
                    gated(2, 0, False)
                with dve.Fori(1 if th == 0 else 0, IC // 2) as i:
                    gated(2 * i + 1, 1, False)
                    gated(2 * i + 2, 0, False)
                dve.wait_ge(s["acc_mm"], IC * (th + 1))
                for b in range(2):
                    c = th * HC + 2 * b
                    then(V.tensor_tensor(tmpx[:], ps[:, b, :].rearrange("p (c f) -> p c f", c=2),
                                         over(gt2[:, 0, :].unsqueeze(1), [P, 2, D]), ALU.mult))
                    last = V.tensor_tensor(x[:, c:c + 2, :], x[:, c:c + 2, :], tmpx[:], ALU.add)
                    if b == 0:
                        then(last)
                last.then_inc(s["x_out"], 1)


def program(nc, arrays):
    d = {}
    for name, a in arrays.items():
        t = nc.dram_tensor(f"in_{name}_dram", a.shape, mybir.dt.from_np(a.dtype), kind="ExternalInput").ap()
        d[name] = t
    out = nc.dram_tensor("out_0_dram", (T, D), F32, kind="ExternalOutput").ap()
    adaln_two_layers(nc, d, out)


def _rows(w):
    import numpy as np
    return np.ascontiguousarray(w.reshape(-1, 128, w.shape[1]).transpose(1, 0, 2))


def _heads_apart(w):
    import numpy as np
    o = np.zeros((w.shape[0], 8, 32), w.dtype)
    o[:, :, :16] = w.reshape(w.shape[0], 8, 16)
    return o.reshape(w.shape[0], 256)


def kernel(**inputs):
    import numpy as np
    import concourse.bacc as _bacc
    from concourse.bass_utils import run_bass_kernel_spmd as _run

    i = {k: np.asarray(v) for k, v in inputs.items()}
    cat, tile = np.concatenate, np.tile
    bf = i["L1_ffn_w1"].dtype
    cols = lambda v: v.reshape(-1, 128).T
    ar = {}
    ar["x"] = i["L0_attn_hidden_states"].reshape(T, D)
    ar["c"] = np.stack([cols(i["L0_c"].ravel()), cols(i["L1_c"].ravel())], 1)
    ar["wmod"] = np.stack([_rows(i["L0_wmod"]), _rows(i["L1_wmod"])])
    ar["win"] = _rows(i["L0_attn_in_proj_w"].T)
    conv = i["L0_attn_conv_w"].reshape(EC, P, TAPS).transpose(1, 0, 2)
    vecs = [cols(i[n]) for n in ("L0_attn_conv_b", "L0_attn_dt_proj_b", "L0_attn_D")]
    ar["small0"] = cat([conv] + [v[:, :, None] for v in vecs], 2)
    ar["alog"] = i["L0_attn_A_log"].reshape(EC, P, NS).transpose(1, 2, 0)
    xp = i["L0_attn_x_proj_w"].T
    ar["wx"] = _rows(cat([xp[:, :R0]] + [xp[:, R0:]] * 3, 1))
    ar["wdt"] = i["L0_attn_dt_proj_w"].T
    ar["wo0"] = _rows(i["L0_attn_out_proj_w"].T)
    ar["wf0"] = _rows(cat([i["L0_ffn_weight"].T, i["L0_ffn_gate_w"].T, i["L0_ffn_A_w"].reshape(P, D).T], 1))
    ar["wlb"] = i["L0_ffn_B_w"].transpose(0, 2, 1).reshape(P, D)
    ar["norm_w"] = np.stack([cols(i["L1_attn_norm1_w"]), cols(i["L1_attn_norm2_w"])], 1)
    ar["wq"] = _rows(_heads_apart(i["L1_attn_wq"]))
    ar["wk"] = _rows(_heads_apart(i["L1_attn_wk"]))
    ar["wvif"] = _rows(cat([i["L1_attn_wv"], i["L1_attn_w_ig"], i["L1_attn_w_fg"]], 1))
    ar["wog"] = _rows(i["L1_attn_w_og"])
    ar["bif"] = tile(cat([i["L1_attn_b_ig"], i["L1_attn_b_fg"]])[None], (P, 1))
    ar["mhw"] = tile(i["L1_attn_mh_w"][None], (P, 1))
    ar["wout1"] = _rows(i["L1_attn_w_out"])
    ar["wg"] = _rows(i["L1_attn_w_gate"])
    ar["wu"] = _rows(i["L1_attn_w_up"])
    ar["wd"] = _rows(i["L1_attn_w_down"])
    ar["wg1"] = _rows(i["L1_ffn_gate_w"].T)
    inner = i["L1_ffn_w1"].shape[1]

    def all_rows(routed, shared):
        m = cat([routed.reshape(-1, D), shared], 0)
        return cat([m, np.zeros((IC * P - m.shape[0], D), m.dtype)], 0)

    ar["w1"] = _rows(all_rows(i["L1_ffn_w1"], i["L1_ffn_sw1"]).T)
    ar["w3"] = _rows(all_rows(i["L1_ffn_w3"], i["L1_ffn_sw3"]).T)
    ar["w2"] = _rows(all_rows(i["L1_ffn_w2"].transpose(0, 2, 1), i["L1_ffn_sw2"].T))
    row = np.arange(P)
    ar["ident"] = np.eye(P, dtype=np.float32)
    inside = (row < 3 * QD)[:, None, None]
    ar["sel"] = (inside & (row[:, None, None] % QD == np.arange(2 * NS)[None, :, None]) & np.ones((1, 1, P), bool)).astype(bf)
    head = 4 * np.arange(HG)[:, None] + row[None, :] // QD
    ar["selr"] = (inside & (row[:, None, None] % QD == head[None])).astype(bf)
    expert = np.minimum(np.arange(IC * P).reshape(IC, P) // inner, E1)
    ar["selx"] = ((inside & (row[:, None, None] % QD == expert[None])) * np.float32(1 / WS)).astype(bf)
    ar["rev"] = tile(np.arange(E1, 0, -1, dtype=np.float32)[None], (P, 1))

    nc = _bacc.Bacc("TRN2", target_bir_lowering=False, num_devices=1)
    ar = {k: np.ascontiguousarray(v) for k, v in ar.items()}
    program(nc, ar)
    r = _run(nc, [{f"in_{k}_dram": v for k, v in ar.items()}], core_ids=[0])
    return r.results[0]["out_0_dram"].reshape(1, T, D)
```

```python
from contextlib import ExitStack

import concourse.bass as bass
from concourse import mybir

P = 128
T = 1024
D = 256
KC = D // P
TC = T // P
HT = 512
NH = T // HT
HC = HT // P
E = 512
EC = E // P
NS = 16
TAPS = 4
R0 = 128
E0, RL = 8, 16
H, DV = 8, 32
QR = 32
HG = 2
VE = DV + 1
FF = 1024
FC = FF // P
E1 = 16
IC = 25
RC = 22
SC = IC - RC
QD = 32
WS = 64.0
LN_EPS, RMS_EPS = 1e-5, 1e-6
CAP = 15.0

ALU = mybir.AluOpType
ACT = mybir.ActivationFunctionType
AX_X = mybir.AxisListType.X
F32 = mybir.dt.float32
BF16 = mybir.dt.bfloat16
F16 = mybir.dt.float16


def adaln_two_layers(nc, d, out):
    ctx = ExitStack()
    with ctx:
        def sem(name):
            return ctx.enter_context(nc.semaphore(name))

        def sbt(stack, name, shape, dt=F32):
            return stack.enter_context(nc.sbuf_tensor(name, shape, dt))

        x = sbt(ctx, "x", [P, TC, D])
        xn = sbt(ctx, "xn", [P, TC, D])
        hT = sbt(ctx, "hT", [P, KC, T])
        tmpx = sbt(ctx, "tmpx", [P, 2, D])
        ident = sbt(ctx, "ident", [P, P])
        ones = sbt(ctx, "ones", [P, P])
        sel = sbt(ctx, "sel", [P, 2 * NS, P], BF16)
        zero16 = sbt(ctx, "zero16", [P, HT], BF16)
        st = sbt(ctx, "st", [P, TC, 6])
        mv = sbt(ctx, "mv", [P, TC, 2])
        sd = sbt(ctx, "sd", [P, TC])
        rs = sbt(ctx, "rs", [P, TC])
        eps = sbt(ctx, "eps", [P, 2])
        cs = sbt(ctx, "cs", [P, 2, KC])
        scs = sbt(ctx, "scs", [P, 2, KC])
        scb = sbt(ctx, "scb", [P, 2, KC, P])
        modc = sbt(ctx, "modc", [P, 2, 4, KC])
        gbc = sbt(ctx, "gbc", [P, 2, 2, D])
        gt1 = sbt(ctx, "gt1", [P, 2, D])
        gt2 = sbt(ctx, "gt2", [P, 2, D])
        small0 = sbt(ctx, "small0", [P, EC, TAPS + 3])
        alog = sbt(ctx, "alog", [P, NS, EC])
        aneg = sbt(ctx, "aneg", [P, NS, EC])
        carry = sbt(ctx, "carry", [P, NS, EC])
        rev = sbt(ctx, "rev", [P, E1])
        small1 = sbt(ctx, "small1", [P, 2, KC])
        wf0 = sbt(ctx, "wf0", [P, KC, D + E0 + P])
        wlb = sbt(ctx, "wlb", [P, D])
        wo0 = sbt(ctx, "wo0", [P, EC, D])
        ffn0_t = xn[:, 0:HC, :].rearrange("p c d -> p (c d)").rearrange("p (c r) -> p c r", r=P)
        ffn0_tT = xn[:, HC:TC, :].rearrange("p c d -> p (c d)")
        sq = xn[:, :, :].rearrange("p c d -> p (c d)").rearrange("p (k t) -> p k t", k=KC)
        qw = sq
        hoT = sq
        gl = sbt(ctx, "gl", [P, TC, E1])
        ga_ = sbt(ctx, "ga_", [P, TC, E1])
        gb_ = sbt(ctx, "gb_", [P, TC, E1])
        gc_ = sbt(ctx, "gc_", [P, TC, E1])
        gr = sbt(ctx, "gr", [P, 6, TC])

        mixer = ExitStack()
        sizes = (KC * 2 * E, EC * (R0 + 3 * QD), E)
        wmix = sbt(mixer, "wmix", [P, sum(sizes)])
        win = wmix[:, 0:sizes[0]].rearrange("p (k e) -> p k e", k=KC)
        wx = wmix[:, sizes[0]:sizes[0] + sizes[1]].rearrange("p (j r) -> p j r", j=EC)
        wdt = wmix[:, sizes[0] + sizes[1]:]
        wmod1 = wmix[:, 0:KC * 6 * D].rearrange("p (k n) -> p k n", k=KC)
        hc = sbt(mixer, "hc", [P, EC, T])
        gate = sbt(mixer, "gate", [P, EC, T])
        dt_ = sbt(mixer, "dt_", [P, EC, T])
        u = sbt(mixer, "u", [P, EC, T])
        bcp = sbt(mixer, "bcp", [P, T], BF16)
        with ExitStack() as before:
            dtr = sbt(before, "dtr", [P, T])
            bch = sbt(before, "bch", [P, T], BF16)
            bcr = sbt(before, "bcr", [P, T])
            wmod0 = sbt(before, "wmod0", [P, KC, 6 * D])
            cv = sbt(before, "cv", [P, EC, T])
            sbt(before, "unused", [P, 6 * EC * HT - (T + T // 2 + T + KC * 6 * D + EC * T)])
            hpad = sbt(before, "hpad", [P, EC, T + TAPS - 1])
        with ExitStack() as during:
            dA = sbt(during, "dA", [P, 4, EC, HT])
            pb = sbt(during, "pb", [P, 4, EC, HT])
            bsb = xn[:, :, :].rearrange("p c d -> p (c d)").rearrange("p (n t) -> p n t", t=HT)
            csb = hT[:, :, :].rearrange("p k t -> p (k t)").rearrange("p (n t) -> p n t", t=HT)
        mixer.close()

        layer1 = ExitStack()
        wout1 = sbt(layer1, "wout1", [P, KC, D])
        wg = sbt(layer1, "wg", [P, KC, FF])
        wu = sbt(layer1, "wu", [P, KC, FF])
        sg = sbt(layer1, "sg", [P, TC, D])
        with ExitStack() as attn:
            selr = sbt(attn, "selr", [P, HG, P], BF16)
            bif = sbt(attn, "bif", [P, 2 * H])
            mhw = sbt(attn, "mhw", [P, D])
            qT = sbt(attn, "qT", [P, HG, T])
            kT = sbt(attn, "kT", [P, HG, T])
            vext = sbt(attn, "vext", [P, TC, H, VE])
            zif = sbt(attn, "zif", [P, TC, 2 * H])
            zt = sbt(attn, "zt", [P, TC, 2 * H])
            lw = sbt(attn, "lw", [P, 4, TC, H])
            gp = sbt(attn, "gp", [P, T], BF16)
            agt = sbt(attn, "agt", [P, 3, TC, H])
            rbc = sbt(attn, "rbc", [P, H, TC])
            rrow = sbt(attn, "rrow", [P, HG, TC])
            dec = sbt(attn, "dec", [P, HG, TC])
            wkt = sbt(attn, "wkt", [P, TC, H])
            qbd = sbt(attn, "qbd", [P, HG, TC, 4, P])
            rinv = sbt(attn, "rinv", [P, 3, TC])
            states = sbt(attn, "states", [P, TC - 1, HG, VE])
            sbd = sbt(attn, "sbd", [P, TC - 1, HG, 4, VE])
            nden = sbt(attn, "nden", [P, 3, TC, H])
            wq = sbt(attn, "wq", [P, KC, HG * P])
            wk = sbt(attn, "wk", [P, KC, HG * P])
            wvif = sbt(attn, "wvif", [P, KC, D + 2 * H])
            wog = sbt(attn, "wog", [P, KC, D])
            with ExitStack() as rows:
                rowF = sbt(rows, "rowF", [P, T])
                rowA = sbt(rows, "rowA", [P, T])
                rowG = sbt(rows, "rowG", [P, T])
                rowM = sbt(rows, "rowM", [P, T])
                lif = sbt(rows, "lif", [P, 2, TC, 3 * QD])
                gh = sbt(rows, "gh", [P, T], BF16)
            with ExitStack() as chunks:
                ks = sbt(chunks, "ks", [P, TC, H, QR])
                arg = sbt(chunks, "arg", [P, 2, H, P])
                pr = sbt(chunks, "pr", [P, 2, H, P])
                num = sbt(chunks, "num", [P, TC, H, VE])
        w1 = sbt(layer1, "w1", [P, KC, IC * P], BF16)
        w3 = sbt(layer1, "w3", [P, KC, IC * P], BF16)
        w2 = sbt(layer1, "w2", [P, IC, D], BF16)
        selx = sbt(layer1, "selx", [P, RC, P], BF16)
        wg1 = sbt(layer1, "wg1", [P, KC, E1])
        with ExitStack() as mlp:
            wd = sbt(mlp, "wd", [P, FC, D])
            x1T = sbt(mlp, "x1T", [P, KC, T])
            sd2 = sbt(mlp, "sd2", [P, 2, T])
            sil = sbt(mlp, "sil", [P, 2, T])
            gg = sbt(mlp, "gg", [P, FC, T])
        with ExitStack() as moe:
            h16 = sbt(moe, "h16", [P, 2, KC, T], F16)
            dwx = sbt(moe, "dwx", [P, TC, 3 * QD])
            dwp = sbt(moe, "dwp", [P, T], BF16)
            dwh = sbt(moe, "dwh", [P, T], BF16)
            dwr = sbt(moe, "dwr", [P, T])
            sa_ = sbt(moe, "sa_", [P, 2, HT])
            gh1 = sbt(moe, "gh1", [P, 2, HT])
            g16 = sbt(moe, "g16", [P, 2, 2, HT], F16)
        layer1.close()
        ps = ctx.enter_context(nc.psum_tensor("ps", [P, 8, HT], F32))

        def banks(b, n, rows=P):
            return ps[0:rows, b:b + n, :].rearrange("p b f -> p (b f)")

        def bc_banks(r, h):
            return (4 + r % 2, 6 + r % 2) if h == 0 else (4, 5)

        DT_BANKS = (4, 6, 0, 4)
        GATE_BANKS = ((1, 6), (2, 4), (3, 2))
        Z1_BANKS = (4, 7)

        def over(ap, shape):
            return ap.broadcast_to(shape)

        ho_head = ks[:].rearrange("p c h n -> p (c h) n")
        ho_tok = ks[:].rearrange("p c h n -> p c (h n)")
        sq_tok = qT[:].rearrange("p g t -> p (g t)").rearrange("p (a n) -> p a n", n=DV)

        names = """ld_c ld_mod0 ld_mod ln_stat ld_x0 ld_x1 ld_const ld_win ld_mix ld_ffn0 ld_attn ld_gateup ld_moe
            ld_down c_silu c_wide mod_mm mod_col gate_raw tap0_done ld_mod1 zeroed ones_ready mod_raw sp_sub
            ln_var ln_sd ln_norm acc_first
            ln_T ln_h in_mm in_evac conv_done hc_ready x_mm dtr_ready bc_parts dt_mm sp_exp dt_ready u_rest u_ready
            aneg_ready bc_bcast bc_copied dA_ready dbu_done scan_done cmul_dve sum_done y_evac
            out_mm f0_mm soft_arg soft_exp f0_t f0_T f0_tT f0_lora sq_ready ss_mm rms_sd w_scaled v_sb o_sb rinv_ready
            g_scaled gu_used qbd_act qbd_dve qbd_pool q_mm k_mm q_sb k_sb v_mm z_in z_tanh z_exp z_ln lif_ready
            lif_T sp_rest sp_ln sp_last y_read relu_done abs_done bc_mm sp_w z_w v_ones rows_zero sg_ready enm_ready
            y_gated_a y_gated_b y_sum
            var_ready dwx_zero moe_prod row_parts row_tok tok_T rr_mm w_arg w_exp kT_T ks_ready state_mm
            state_done qg_mm qw_arg qw_exp qw_ready sbd_ready s_mm g_mm arg_ready arg_masked e_ready pr_ready
            intra_mm num_ready den_ready num_sq var_sd ho_ready ho_T hoT_ready wo_mm x1_ready sq2_ready ss2_mm
            rms2_sd gu_mm sil_ready gg_ready down_mm h_hi h_split z1_mm z1_exp dw_ready dw_T dw_parts up_mm
            moe_sil g_ready ghi_ready glo_ready acc_mm x_out stored act_step dve_step""".split()
        s = {n: sem(n) for n in names}

        block = ctx.enter_context(nc.Block())

        @block.sync
        def _(sp):
            def load(dst, name, signal):
                sp.dma_start(dst, d[name]).then_inc(s[signal], 16)

            xv = d["x"].rearrange("(c p) f -> p c f", p=P)
            sp.dma_start(x[:, 0:HC, :], xv[:, 0:HC, :]).then_inc(s["ld_x0"], 16)
            sp.dma_start(x[:, HC:TC, :], xv[:, HC:TC, :]).then_inc(s["ld_x1"], 16)
            load(ident[:], "ident", "ld_const")
            load(sel[:], "sel", "ld_const")
            load(rev[:], "rev", "ld_const")
            load(small1[:], "norm_w", "ld_const")
            load(win, "win", "ld_win")
            load(small0[:], "small0", "ld_mix")
            load(alog[:], "alog", "ld_mix")
            load(wx, "wx", "ld_mix")
            load(wdt, "wdt", "ld_mix")
            sp.dma_start(wmod0[:, :, 2 * D:], d["wmod"][0][:, :, 2 * D:]).then_inc(s["ld_mod"], 16)
            load(wo0[:], "wo0", "ld_ffn0")
            load(wf0[:], "wf0", "ld_ffn0")
            load(wlb[:], "wlb", "ld_ffn0")
            sp.wait_ge(s["in_mm"], 2 * EC)
            sp.dma_start(wmod1, d["wmod"][1]).then_inc(s["ld_mod1"], 16)
            sp.wait_ge(s["out_mm"], TC)
            for dst, name in ((wq, "wq"), (wk, "wk"), (wvif, "wvif"), (wog, "wog"), (selr, "selr"), (bif, "bif"),
                              (mhw, "mhw")):
                load(dst[:], name, "ld_attn")
            sp.wait_ge(s["mod_mm"], 3)
            load(wout1[:], "wout1", "ld_gateup")
            load(wg[:], "wg", "ld_gateup")
            load(wu[:], "wu", "ld_gateup")
            sp.wait_ge(s["hoT_ready"], 4)
            load(wd[:], "wd", "ld_down")
            for dst, name in ((wg1, "wg1"), (w1, "w1"), (w3, "w3"), (w2, "w2"), (selx, "selx")):
                load(dst[:], name, "ld_moe")
            ov = out.rearrange("(c p) f -> p c f", p=P)
            stores = (slice(0, HC), slice(HC, HC + 2), slice(HC + 2, TC))
            for n, chunks in enumerate(stores):
                sp.wait_ge(s["x_out"], n + 1)
                sp.dma_start(ov[:, chunks, :], x[:, chunks, :]).then_inc(s["stored"], 16)
            sp.wait_ge(s["stored"], 16 * len(stores))

        @block.tensor
        def _(pe):
            mm = nc.tensor.matmul

            def clear(b):
                return mm(ps[:, b, :], zero16[:, 0:P], zero16[:, :], start=True, stop=False)

            wmods = (wmod0, wmod1)

            def mod_columns(l, parts, b):
                for n in parts:
                    for f in range(KC):
                        for k in range(KC):
                            lo = (0, 1, 3, 4)[n] * D + f * P
                            last = mm(ps[:, b, n * KC + f:n * KC + f + 1], wmods[l][:, k, lo:lo + P],
                                      scs[:, l, k:k + 1], start=k == 0, stop=k == KC - 1)
                return last

            def mod_gates(l, b):
                for k in range(KC):
                    gates = wmods[l][:, k, :].rearrange("p (a b f) -> p a b f", a=2, b=3)[:, :, 2, :]
                    last = mm(ps[:, b, :], scb[:, l, k, :], gates, start=k == 0, stop=k == KC - 1)
                return last

            pe.wait_ge(s["ld_mod0"], 16)
            pe.wait_ge(s["c_silu"], 1)
            mod_columns(0, (0, 1), 7).then_inc(s["mod_mm"], 1)

            def ln_transpose(n, base, th):
                pe.wait_ge(s["ln_norm"], TC * n + HC * (th + 1))
                for k in range(KC):
                    for c in range(HC):
                        last = nc.tensor.transpose(ps[:, base + 2 * k + th, c * P:(c + 1) * P],
                                                   xn[:, th * HC + c, k * P:(k + 1) * P], ident[:])
                last.then_inc(s["ln_T"], 1)

            def ln_transposes(n, base):
                for th in range(NH):
                    ln_transpose(n, base, th)

            pe.wait_ge(s["ld_const"], 64)
            pe.wait_ge(s["ones_ready"], 4)
            ln_transposes(0, 0)

            pe.wait_ge(s["ln_h"], 4)
            pe.wait_ge(s["ld_win"], 16)
            pe.wait_ge(s["mod_col"], 1)

            def in_proj(g, b):
                for th in range(NH):
                    for k in range(KC):
                        last = mm(ps[:, b + th, :], win[:, k, g * P:(g + 1) * P], hT[:, k, th * HT:(th + 1) * HT],
                                  start=k == 0, stop=k == KC - 1)
                last.then_inc(s["in_mm"], 1)

            for g, b in enumerate((4, 6, 0, 2)):
                in_proj(g, b)
            pe.wait_ge(s["in_evac"], 1)
            in_proj(EC, 4)

            def x_proj(j, b, cols):
                for th in range(NH):
                    last = mm(ps[0:cols.stop - cols.start, b + th, :], wx[:, j, cols], hc[:, j, th * HT:(th + 1) * HT],
                              start=j == 0, stop=j == EC - 1)
                return last

            rank, bc = slice(0, R0), slice(R0, R0 + 3 * QD)
            pe.wait_ge(s["in_evac"], EC)
            pe.wait_ge(s["ld_mix"], 64)
            for j in range(EC):
                pe.wait_ge(s["hc_ready"], j + 1)
                last = x_proj(j, 0, rank)
                if j == 1:
                    x_proj(0, 2, bc)
            last.then_inc(s["x_mm"], 1)
            x_proj(1, 2, bc)

            pe.wait_ge(s["dtr_ready"], 1)
            pe.wait_ge(s["in_evac"], EC + 1)
            for j, b in enumerate(DT_BANKS):
                if j == 3:
                    pe.wait_ge(s["relu_done"], 1)
                for th in range(NH):
                    last = mm(ps[:, b + th, :], wdt[:, j * P:(j + 1) * P], dtr[:, th * HT:(th + 1) * HT],
                              start=True, stop=True)
                last.then_inc(s["dt_mm"], 1)
            x_proj(2, 2, bc)
            x_proj(3, 2, bc).then_inc(s["bc_mm"], 1)
            pe.wait_ge(s["ld_mod"], 16)
            pe.wait_ge(s["relu_done"], 3)
            mod_columns(0, (2, 3), 0)
            pe.wait_ge(s["c_wide"], 1)
            mod_gates(0, 1).then_inc(s["mod_mm"], 1)
            for g, b in GATE_BANKS:
                if b == 4:
                    pe.wait_ge(s["relu_done"], EC)
                if b == 2:
                    pe.wait_ge(s["bc_parts"], 1)
                in_proj(EC + g, b)

            pe.wait_ge(s["bc_parts"], 1)
            pe.wait_ge(s["in_evac"], EC + 3)
            for th in range(NH):
                def bcast(n, r, h):
                    toks = bcp[:, h * HT:(h + 1) * HT]
                    b, c = bc_banks(r, h)
                    mm(ps[:, b, :], sel[:, n, :], toks, start=True, stop=True)
                    mm(ps[:, c, :], sel[:, n + NS, :], toks, start=True, stop=True)\
                        .then_inc(s["bc_bcast"], 1)

                def out_early(c):
                    for j in range(EC):
                        last = mm(banks(6, 2)[:, c * D:(c + 1) * D], hc[:, j, c * P:(c + 1) * P], wo0[:, j, :],
                                  start=j == 0, stop=j == EC - 1)
                    last.then_inc(s["out_mm"], 1)

                def group(i, last_group, outs=False):
                    for r in range(4):
                        n = 4 * i + r
                        it = NS * th + n
                        if not (last_group and th == NH - 1):
                            one_pair = last_group or th == NH - 1
                            pe.wait_ge(s["bc_copied"], it + (4 if one_pair else 3))
                            if last_group:
                                bcast(r, r, th + 1)
                            else:
                                bcast(n + 4, r, th)
                        pe.wait_ge(s["cmul_dve"], it + 1)
                        for j in range(EC):
                            last = mm(ps[:, j, :], ident[:], dA[:, r, j, :], start=False, stop=last_group and r == 3)
                            if last_group and r == 3 and th == NH - 1 and j < EC - 1:
                                last.then_inc(s["y_sum"], 1)
                        last.then_inc(s["sum_done"], 1)
                        if outs and r % 2:
                            out_early(2 * i - 2 + r // 2)

                if th == 0:
                    for n in range(4):
                        if n >= 2:
                            pe.wait_ge(s["bc_copied"], n - 1)
                        bcast(n, n, 0)
                    pe.wait_ge(s["in_evac"], 2 * EC)
                    pe.wait_ge(s["gate_raw"], 1)
                else:
                    pe.wait_ge(s["ld_mod1"], 16)
                    mod_columns(1, (0, 1, 2, 3), 6)
                    mod_gates(1, 7).then_inc(s["mod_mm"], 1)
                    pe.wait_ge(s["y_evac"], th)
                for j in range(EC):
                    clear(j)
                if th == 0:
                    with pe.Fori(0, NS // 4 - 1) as i:
                        group(i, False)
                else:
                    group(0, False)
                    pe.wait_ge(s["ld_ffn0"], 48)
                    pe.wait_ge(s["y_gated_a"], 1)
                    pe.wait_ge(s["gate_raw"], 2)
                    for i in range(1, NS // 4 - 1):
                        group(i, False, True)
                group(NS // 4 - 1, True)

            pe.wait_ge(s["y_gated_b"], 1)
            for c in range(HC, TC):
                for j in range(EC):
                    last = mm(ps[:, c - HC, 0:D], hc[:, j, c * P:(c + 1) * P], wo0[:, j, :],
                              start=j == 0, stop=j == EC - 1)
                last.then_inc(s["out_mm"], 1)

            def ranks_and_logits(c):
                for k in range(KC):
                    last = mm(ps[:, c // 2, (c % 2) * 136:(c % 2) * 136 + 136], hT[:, k, c * P:(c + 1) * P],
                              wf0[:, k, D:D + E0 + P], start=k == 0, stop=k == KC - 1)
                return last

            def dense(c):
                if c % 2 == 0:
                    clear(4 + c // 2)
                for k in range(KC):
                    mm(ps[:, 4 + c // 2, (c % 2) * D:(c % 2 + 1) * D], hT[:, k, c * P:(c + 1) * P], wf0[:, k, 0:D],
                       start=False, stop=False)

            ln_transpose(1, 4, 0)
            pe.wait_ge(s["ln_h"], 6)
            for c in range(HC):
                ranks_and_logits(c)
            ln_transpose(1, 4, 1)
            dense(0)
            pe.wait_ge(s["ln_h"], 8)
            for c in range(HC, TC):
                last = ranks_and_logits(c)
            last.then_inc(s["f0_mm"], 1)
            for c in range(1, TC):
                dense(c)
            pe.wait_ge(s["f0_t"], 1)
            for c in range(TC):
                last = nc.tensor.transpose(ps[:, c // HC, (c % HC) * P:(c % HC + 1) * P], ffn0_t[:, c, :], ident[:])
            last.then_inc(s["f0_T"], 1)
            pe.wait_ge(s["f0_tT"], 1)
            for c in range(TC):
                mm(ps[:, 4 + c // 2, (c % 2) * D:(c % 2 + 1) * D], ffn0_tT[:, c * P:(c + 1) * P], wlb[:, :],
                   start=False, stop=c % 2 == 1).then_inc(s["f0_lora"], 1)


            def values_and_gates(c):
                b = 2 * (c % 3)
                if c >= 3:
                    pe.wait_ge(s["v_sb"], c - 2)
                    pe.wait_ge(s["o_sb"], c - 2)
                for k in range(KC):
                    mm(ps[:, b, 0:D + 2 * H], hT[:, k, c * P:(c + 1) * P], wvif[:, k, :], start=k == 0, stop=k == KC - 1)
                for k in range(KC):
                    last = mm(ps[:, b + 1, 0:D], hT[:, k, c * P:(c + 1) * P], wog[:, k, :], start=k == 0, stop=k == KC - 1)
                last.then_inc(s["v_mm"], 1)

            def project(w, g, b):
                for th in range(NH):
                    for k in range(KC):
                        last = mm(ps[:, b + th, :], w[:, k, g * P:(g + 1) * P],
                                  hT[:, k, th * HT:(th + 1) * HT], start=k == 0, stop=k == KC - 1)
                return last

            ln_transpose(2, 4, 0)
            pe.wait_ge(s["ln_h"], 10)
            pe.wait_ge(s["w_scaled"], 1)
            values_and_gates(0)
            ln_transpose(2, 4, 1)
            values_and_gates(1)
            pe.wait_ge(s["ln_h"], 12)
            values_and_gates(2)
            pe.wait_ge(s["sq_ready"], KC)
            for c in range(TC):
                for k in range(KC):
                    last = mm(ps[:, 6, c:c + 1], sq[:, k, c * P:(c + 1) * P], ones[:, 0:1], start=k == 0, stop=k == KC - 1)
            last.then_inc(s["ss_mm"], 1)
            for c in range(3, TC):
                values_and_gates(c)
            pe.wait_ge(s["v_sb"], 6)
            pe.wait_ge(s["o_sb"], 6)
            project(wk, 0, 4).then_inc(s["k_mm"], 1)
            pe.wait_ge(s["v_sb"], TC)
            pe.wait_ge(s["o_sb"], TC)
            project(wk, 1, 0).then_inc(s["k_mm"], 1)
            pe.wait_ge(s["lif_ready"], 1)
            for a in range(2):
                pe.wait_ge(s["k_sb"], a + 1)
                for t in range(TC):
                    last = nc.tensor.transpose(ps[0:3 * QD, 4 * (1 - a) + t // HC, (t % HC) * P:(t % HC + 1) * P],
                                               lif[:, a, t, :], ident[:])
                last.then_inc(s["lif_T"], 1)
            project(wq, 0, 2).then_inc(s["q_mm"], 1)
            project(wq, 1, 6).then_inc(s["q_mm"], 1)
            pe.wait_ge(s["row_tok"], 1)
            pe.wait_ge(s["q_sb"], 1)
            for a, row in enumerate((rowA, rowG, rowM)):
                for c in range(TC):
                    col = (a * TC + c) * H
                    last = nc.tensor.transpose(ps[:, 2, col:col + H], row[0:H, c * P:(c + 1) * P], ident[0:H, 0:H])
            last.then_inc(s["tok_T"], 1)
            for c in range(TC):
                if c == HC:
                    pe.wait_ge(s["q_sb"], HG)
                for g in range(HG):
                    col = (c % 2) * D + g * P
                    last = nc.tensor.transpose(ps[:, 4 + c // 2, col:col + P], kT[:, g, c * P:(c + 1) * P], ident[:])
            last.then_inc(s["kT_T"], 1)
            pe.wait_ge(s["row_parts"], 1)
            ends = gp[:, P - 1:T:P]
            for h in range(H):
                mm(ps[:, 3, h * TC:(h + 1) * TC], sel[:, h, :], ends, start=True, stop=True)
            for g in range(HG):
                last = mm(ps[:, 3, (H + g) * TC:(H + g + 1) * TC], selr[:, g, :], ends, start=True, stop=True)
            last.then_inc(s["rr_mm"], 1)
            pe.wait_ge(s["q_sb"], HG)
            for g in range(HG):
                if g:
                    pe.wait_ge(s["qw_arg"], g)
                for th in range(NH):
                    last = mm(ps[:, th, :], selr[:, g, :], gp[:, th * HT:(th + 1) * HT], start=True, stop=True)
                last.then_inc(s["qg_mm"], 1)
            pe.wait_ge(s["w_arg"], 1)
            pe.wait_ge(s["w_exp"], 1)
            for c in range(TC):
                if c % 2 == 0:
                    pe.wait_ge(s["ks_ready"], c // 2 + 1)
                for h in range(H):
                    g, r = h // 4, h % 4
                    col = (c % 4) * HG * VE + g * VE
                    last = mm(ps[QD * r:QD * (r + 1), 2 + c // 4, col:col + VE], ks[:, c, h, :], vext[:, c, h, :],
                              start=True, stop=True)
                last.then_inc(s["state_mm"], 1)

            def g_rows(c):
                if c:
                    pe.wait_ge(s["arg_ready"], c)
                for h in range(H):
                    last = mm(ps[:, 4 + h // 4, (h % 4) * P:(h % 4 + 1) * P], sel[:, h, :], gp[:, c * P:(c + 1) * P],
                              start=True, stop=True)
                last.then_inc(s["g_mm"], 1)

            def scores(c):
                if c >= 2:
                    pe.wait_ge(s["pr_ready"], c - 1)
                for g in range(HG):
                    last = mm(ps[:, 2 * (c % 2) + g, :], kT[:, g, c * P:(c + 1) * P],
                              qbd[:, g, c].rearrange("p r t -> p (r t)"), start=True, stop=True)
                last.then_inc(s["s_mm"], 1)

            def outputs(c):
                b = 6 + c % 2
                if c >= 2:
                    pe.wait_ge(s["num_ready"], c - 1)
                clear(b)
                for g in range(HG if c else 0):
                    mm(ps[:, b, g * 4 * VE:(g + 1) * 4 * VE], qw[:, g, c * P:(c + 1) * P],
                       sbd[:, c - 1, g].rearrange("p r v -> p (r v)"), start=False, stop=False)
                if c + 2 < TC:
                    g_rows(c + 2)
                pe.wait_ge(s["pr_ready"], c + 1)
                for h in range(H):
                    last = mm(ps[:, b, h * VE:(h + 1) * VE], pr[:, c % 2, h, :], vext[:, c, h, :],
                              start=False, stop=h == H - 1)
                last.then_inc(s["intra_mm"], 1)

            pe.wait_ge(s["ks_ready"], 4)
            g_rows(0)
            pe.wait_ge(s["qbd_act"], 4)
            pe.wait_ge(s["qbd_dve"], 2)
            pe.wait_ge(s["qbd_pool"], 2)
            pe.wait_ge(s["qw_arg"], HG)
            scores(0)
            g_rows(1)
            pe.wait_ge(s["state_done"], TC - 1)
            scores(1)
            pe.wait_ge(s["sbd_ready"], 1)
            pe.wait_ge(s["qw_ready"], 1)
            for c in range(TC):
                outputs(c)
                if c + 2 < TC:
                    scores(c + 2)

            def gate_up(f, w, bank, th):
                for k in range(KC):
                    last = mm(ps[:, bank + th, :], w[:, k, f * P:(f + 1) * P], x1T[:, k, th * HT:(th + 1) * HT],
                              start=k == 0, stop=k == KC - 1)
                return last

            def square_sums(th):
                pe.wait_ge(s["sq2_ready"], KC * (th + 1))
                for k in range(KC):
                    last = mm(ps[:, 4 + th, :], ones[:], sq[:, k, th * HT:(th + 1) * HT],
                              start=k == 0, stop=k == KC - 1)
                last.then_inc(s["ss2_mm"], 1)

            pe.wait_ge(s["ld_gateup"], 48)
            for th in range(NH):
                if th == 1:
                    pe.wait_ge(s["x1_ready"], KC)
                    pe.wait_ge(s["w_scaled"], 2)
                    gate_up(0, wg, 0, 0)
                    gate_up(0, wu, 2, 0)
                pe.wait_ge(s["ho_ready"], th + 1)
                for k in range(KC):
                    for c in range(HC):
                        last = nc.tensor.transpose(ps[:, 2 * k + th, c * P:(c + 1) * P],
                                                   ho_tok[:, th * HC + c, k * P:(k + 1) * P], ident[:])
                last.then_inc(s["ho_T"], 1)
                if th == 1:
                    square_sums(0)
                pe.wait_ge(s["hoT_ready"], KC * (th + 1))
                if th == 0:
                    pe.wait_ge(s["num_ready"], TC)
                for m in range(KC):
                    for k in range(KC):
                        last = mm(ps[:, 4 + 2 * m + th, :], wout1[:, k, m * P:(m + 1) * P],
                                  hoT[:, k, th * HT:(th + 1) * HT], start=k == 0, stop=k == KC - 1)
                    last.then_inc(s["wo_mm"], 1)

            pe.wait_ge(s["x1_ready"], KC * NH)
            gate_up(0, wg, 0, 1)
            square_sums(1)
            gate_up(0, wu, 2, 1).then_inc(s["gu_mm"], 1)
            for f in range(1, FC):
                b = 4 * (f % 2)
                if f == 1:
                    pe.wait_ge(s["rms2_sd"], NH)
                else:
                    pe.wait_ge(s["gu_used"], f - 1)
                for w, o in ((wg, 0), (wu, 2)):
                    for th in range(NH):
                        last = gate_up(f, w, b + o, th)
                last.then_inc(s["gu_mm"], 1)
            pe.wait_ge(s["ld_down"], 16)

            def down_first(c):
                clear(c)
                for k in range(KC):
                    mm(ps[:, c, k * P:(k + 1) * P], x1T[:, k, c * P:(c + 1) * P], ident[:], start=False, stop=False)
                for f in range(FC - 1):
                    mm(ps[:, c, 0:D], gg[:, f, c * P:(c + 1) * P], wd[:, f, :], start=False, stop=False)

            def down_last(c):
                mm(ps[:, c, 0:D], gg[:, FC - 1, c * P:(c + 1) * P], wd[:, FC - 1, :], start=False, stop=True)\
                    .then_inc(s["down_mm"], 1)

            pe.wait_ge(s["gg_ready"], FC - 1)
            for c in range(HC):
                down_first(c)
            pe.wait_ge(s["gg_ready"], FC)
            for c in range(HC):
                down_last(c)
            for c in range(HC, TC):
                down_first(c)
                down_last(c)

            def router1(th, b):
                pe.wait_ge(s["ln_h"], 12 + KC * (th + 1))
                for c in range(HC):
                    for k in range(KC):
                        last = mm(ps[:, b, c * E1:(c + 1) * E1], hT[:, k, (th * HC + c) * P:(th * HC + c + 1) * P],
                                  wg1[:, k, :], start=k == 0, stop=k == KC - 1)
                last.then_inc(s["z1_mm"], 1)

            def weights_transpose(th):
                pe.wait_ge(s["dw_ready"], th + 1)
                for c in range(HC):
                    last = nc.tensor.transpose(ps[0:3 * QD, 6 + th, c * P:(c + 1) * P], dwx[:, th * HC + c, :], ident[:])
                last.then_inc(s["dw_T"], 1)

            ln_transpose(3, 0, 0)
            pe.wait_ge(s["ld_moe"], 5 * 16)
            router1(0, Z1_BANKS[0])
            ln_transpose(3, 0, 1)

            def up(ic, r, th, shared):
                half = slice(th * HT, (th + 1) * HT)
                for w, b in ((w1, 2), (w3, 4)):
                    for k in range(KC):
                        for part in range(2):
                            last = mm(ps[:, b + r, :], w[:, k, bass.ts(ic, P)], h16[:, part, k, half],
                                      start=(k == 0 and part == 0), stop=(k == KC - 1 and part == 1))
                if not shared:
                    last = mm(ps[:, 6 + r, :], selx[:, ic, :], dwp[:, half], start=True, stop=True)
                last.then_inc(s["up_mm"], 1)

            def down(m, ic, r, last_one):
                pe.wait_ge(s["glo_ready"], m + 1)
                for c in range(HC):
                    for part in range(2):
                        last = mm(ps[:, c // 2, (c % 2) * D:(c % 2 + 1) * D], g16[:, r, part, c * P:(c + 1) * P],
                                  w2[:, ic, :], start=False, stop=last_one and c % 2 == 1 and part == 1)
                last.then_inc(s["acc_mm"], 1)

            pe.wait_ge(s["h_split"], 1)
            pe.wait_ge(s["z1_exp"], 1)
            up(RC, 0, 0, True)
            pe.wait_ge(s["ln_h"], 16)
            up(RC + 1, 1, 0, True)
            router1(1, Z1_BANKS[1])
            weights_transpose(0)
            for th in range(NH):
                if th:
                    pe.wait_ge(s["y_read"], th)
                for b in range(2):
                    clear(b)
                for p in range(SC):
                    m = IC * th + p
                    pe.wait_ge(s["g_ready"], m + 1)
                    if p + 2 < SC:
                        up(RC + p + 2, m % 2, th, True)
                    else:
                        if p + 2 == SC:
                            pe.wait_ge(s["dw_parts"], th + 1)
                            if th == 0:
                                pe.wait_ge(s["z1_exp"], NH)
                        up(p + 2 - SC, m % 2, th, False)
                    down(m, RC + p, m % 2, False)
                with pe.Fori(0, RC // 2 - 1) as i:
                    for j in range(2):
                        m = 2 * i + IC * th + SC + j
                        r = (th + SC + j) % 2
                        pe.wait_ge(s["g_ready"], m + 1)
                        up(2 * i + j + 2, r, th, False)
                        down(m, 2 * i + j, r, False)
                for ic in range(RC - 2, RC):
                    m = IC * th + SC + ic
                    if th + 1 < NH:
                        pe.wait_ge(s["g_ready"], m + 1)
                        if ic == RC - 2:
                            pe.wait_ge(s["h_split"], NH)
                            weights_transpose(1)
                        up(ic + 2, m % 2, th + 1, True)
                    if th + 1 < NH or ic < RC - 1:
                        down(m, ic, m % 2, ic == RC - 1)
            g = g16[:, (2 * IC - 1) % 2]
            pe.wait_ge(s["ghi_ready"], 2 * IC)
            for part in range(2):
                if part:
                    pe.wait_ge(s["glo_ready"], 2 * IC)
                for c in range(HC):
                    last = mm(ps[:, c // 2, (c % 2) * D:(c % 2 + 1) * D], g[:, part, c * P:(c + 1) * P], w2[:, RC - 1, :],
                              start=False, stop=c % 2 == 1 and part == 1)
                    if part == 1 and c == 1:
                        last.then_inc(s["acc_first"], 1)
            last.then_inc(s["acc_mm"], 1)

        @block.scalar
        def _(act):
            A = nc.scalar.activation
            step = [0]

            def then(ins):
                step[0] += 1
                ins.then_inc(s["act_step"], 1)
                act.wait_ge(s["act_step"], step[0])

            act.dma_start(cs[:], d["c"]).then_inc(s["ld_c"], 16)
            act.dma_start(wmod0[:, :, 0:2 * D], d["wmod"][0][:, :, 0:2 * D]).then_inc(s["ld_mod0"], 16)
            act.wait_ge(s["ld_c"], 16)
            A(scs[:], cs[:], ACT.Silu).then_inc(s["c_silu"], 1)

            def ln_root(n, th):
                chunks = slice(th * HC, (th + 1) * HC)
                act.wait_ge(s["ln_var"], NH * n + th + 1)
                A(sd[:, chunks], mv[:, chunks, 1], ACT.Sqrt, bias=eps[:, 1:2]).then_inc(s["ln_sd"], 1)

            def modulate(n, th, layer, shift, scale, base):
                act.wait_ge(s["ln_T"], NH * n + th + 1)
                if n in (0, 2):
                    act.wait_ge(s["mod_col"], 1 + n // 2)
                for k in range(KC):
                    A(hT[:, k, th * HT:(th + 1) * HT], ps[:, base + 2 * k + th, :], ACT.Identity,
                      bias=modc[:, layer, shift, k:k + 1], scale=modc[:, layer, scale, k:k + 1])\
                        .then_inc(s["ln_h"], 1)

            def layernorm(n, layer, shift, scale, base):
                for th in range(NH):
                    ln_root(n, th)
                    modulate(n, th, layer, shift, scale, base)

            act.wait_ge(s["ones_ready"], 4)
            ln_root(0, 0)
            ln_root(0, 1)
            modulate(0, 0, 0, 0, 1, 0)
            modulate(0, 1, 0, 0, 1, 0)
            act.wait_ge(s["zeroed"], 3)
            act.wait_ge(s["ld_mix"], 64)
            def hc_silu(j):
                act.wait_ge(s["conv_done"], j + 1)
                A(hc[:, j, :], cv[:, j, :], ACT.Silu).then_inc(s["hc_ready"], 1)

            for g, b in enumerate((4, 6, 0, 2)):
                act.wait_ge(s["in_mm"], g + 1)
                A(hpad[:, g, TAPS - 1:], banks(b, 2), ACT.Copy).then_inc(s["in_evac"], 1)
                act.wait_ge(s["in_evac"], g + 1)
                A(cv[:, g, :], hpad[:, g, 0:T], ACT.Identity, scale=small0[:, g, 0:1], bias=small0[:, g, 4:5])\
                    .then_inc(s["tap0_done"], 1)
                if g:
                    hc_silu(g - 1)
            act.wait_ge(s["in_mm"], EC + 1)
            A(gate[:, 0, :], banks(4, 2), ACT.Silu).then_inc(s["in_evac"], 1)
            hc_silu(EC - 1)
            act.wait_ge(s["ld_mix"], 64)
            then(A(alog[:], alog[:], ACT.Exp))
            nc.scalar.mul(aneg[:], alog[:], -1.0).then_inc(s["aneg_ready"], 1)
            act.wait_ge(s["x_mm"], 1)
            A(dtr[:], banks(0, 2), ACT.Copy).then_inc(s["dtr_ready"], 1)
            for j, b in enumerate(DT_BANKS):
                act.wait_ge(s["dt_mm"], j + 1)
                A(cv[:, j, :], banks(b, 2), ACT.Abs, bias=small0[:, j, 5:6]).then_inc(s["abs_done"], 1)
            act.wait_ge(s["abs_done"], EC)
            for j in range(EC):
                A(cv[:, j, :], cv[:, j, :], ACT.Exp, scale=-1.0).then_inc(s["sp_exp"], 1)
                act.wait_ge(s["sp_exp"], j + 1)
                A(hpad[:, j, 0:T], cv[:, j, :], ACT.Identity, bias=ones[:, 0:1]).then_inc(s["sp_w"], 1)
            for j in range(EC):
                act.wait_ge(s["sp_rest"], j + 1)
                A(hpad[:, j, 0:T], hpad[:, j, 0:T], ACT.Ln).then_inc(s["sp_ln"], 1)
            for g, b in GATE_BANKS:
                act.wait_ge(s["in_mm"], EC + g + 1)
                A(gate[:, g, :], banks(b, 2), ACT.Silu).then_inc(s["in_evac"], 1)

            act.wait_ge(s["dt_ready"], EC)
            act.wait_ge(s["aneg_ready"], 1)
            for th in range(NH):
                half = slice(th * HT, (th + 1) * HT)
                if th:
                    act.wait_ge(s["dt_ready"], 2 * EC)

                def copy_bc(it, r, h, first):
                    b, c = bc_banks(r, h)
                    act.wait_ge(s["bc_bcast"], it + 1)
                    if not first:
                        act.wait_ge(s["cmul_dve"], it - 3)
                    A(bsb[:, r % 4, :], ps[:, b, :], ACT.Copy)
                    A(csb[:, r % 4, :], ps[:, c, :], ACT.Copy).then_inc(s["bc_copied"], 1)

                def group(i, first, last_group):
                    for r in range(4):
                        it = NS * th + 4 * i + r
                        if not first:
                            act.wait_ge(s["sum_done"], it - 3)
                        for j in range(EC):
                            last = A(dA[:, r, j, :], dt_[:, j, half], ACT.Exp, scale=aneg[:, 4 * i + r, j:j + 1])
                        last.then_inc(s["dA_ready"], 1)
                        if not (last_group and r >= 2 and th == NH - 1):
                            copy_bc(it + 2, r + 2, th + 1 if last_group and r >= 2 else th, first and r < 2)

                if th == 0:
                    for n in range(2):
                        copy_bc(n, n, 0, True)
                    group(0, True, False)
                with act.Fori(1 if th == 0 else 0, NS // 4 - 1) as i:
                    group(i, False, False)
                group(NS // 4 - 1, False, True)

            layernorm(1, 0, 2, 3, 4)
            act.wait_ge(s["soft_arg"], 1)
            A(ga_[:, :, 0:E0], gl[:, :, 0:E0], ACT.Exp).then_inc(s["soft_exp"], 1)
            act.wait_ge(s["f0_T"], 1)
            A(ffn0_tT, banks(0, 2), ACT.Copy).then_inc(s["f0_tT"], 1)

            layernorm(2, 1, 0, 1, 4)
            act.wait_ge(s["ln_h"], 12)
            for k in range(KC):
                A(sq[:, k, :], hT[:, k, :], ACT.Square).then_inc(s["sq_ready"], 1)
            act.wait_ge(s["ss_mm"], 1)
            A(rinv[:, 0], ps[:, 6, 0:TC], ACT.Sqrt, scale=1.0 / D, bias=eps[:, 0:1]).then_inc(s["rms_sd"], 1)
            act.wait_ge(s["rinv_ready"], 1)
            for c in range(TC):
                act.wait_ge(s["v_mm"], c + 1)
                A(sg[:, c, :], ps[:, 2 * (c % 3) + 1, 0:D], ACT.Sigmoid, scale=rinv[:, 1, c:c + 1]).then_inc(s["o_sb"], 1)
            act.wait_ge(s["z_in"], TC)
            A(zt[:], zif[:], ACT.Tanh, scale=1.0 / CAP).then_inc(s["z_tanh"], 1)
            act.wait_ge(s["z_tanh"], 1)
            A(lw[:, 0], zt[:, :, H:2 * H], ACT.Exp, scale=-CAP).then_inc(s["z_exp"], 1)
            act.wait_ge(s["z_w"], 1)
            A(lw[:, 2], lw[:, 1], ACT.Ln).then_inc(s["z_ln"], 1)
            for g in range(HG):
                act.wait_ge(s["q_mm"], g + 1)
                nc.scalar.mul(qT[:, g, :], banks((2, 6)[g], 2), 0.25).then_inc(s["q_sb"], 1)
            act.wait_ge(s["tok_T"], 1)
            A(agt[:, 2].rearrange("p c h -> p (c h)"), ps[:, 2, 2 * TC * H:3 * TC * H], ACT.Exp, scale=-1.0)\
                .then_inc(s["enm_ready"], 1)
            act.wait_ge(s["q_sb"], HG)
            act.wait_ge(s["v_ones"], 3)
            for g, r in ((0, 2), (0, 3), (1, 2), (1, 3)):
                rows = slice(QD * r, QD * (r + 1))
                A(qbd[rows, g, :, r, :], qT[rows, g, :].rearrange("p (c t) -> p c t", t=P), ACT.Copy)\
                    .then_inc(s["qbd_act"], 1)
            act.wait_ge(s["w_arg"], 1)
            A(wkt[:], wkt[:], ACT.Exp)
            A(dec[:, :, 1:], dec[:, :, 1:], ACT.Exp).then_inc(s["w_exp"], 1)
            for g in range(HG):
                act.wait_ge(s["qw_arg"], g + 1)
                A(qw[:, g, P:], qw[:, g, P:], ACT.Exp).then_inc(s["qw_exp"], 1)

            def head_squares(th):
                heads = slice(th * HC * H, (th + 1) * HC * H)
                act.wait_ge(s["den_ready"], th + 1)
                A(sq_tok[:, heads], ho_head[:, heads], ACT.Square).then_inc(s["num_sq"], 1)

            def head_root(th):
                heads = slice(th * HC, (th + 1) * HC)
                act.wait_ge(s["var_ready"], th + 1)
                A(nden[:, 2, heads], nden[:, 1, heads], ACT.Sqrt, scale=1.0 / DV, bias=eps[:, 0:1]).then_inc(s["var_sd"], 1)

            def sums_out(c):
                act.wait_ge(s["intra_mm"], c + 1)
                A(num[:, c].rearrange("p h v -> p (h v)"), ps[:, 6 + c % 2, 0:H * VE], ACT.Copy).then_inc(s["num_ready"], 1)

            for c in range(TC):
                act.wait_ge(s["arg_masked"], c + 1)
                A(arg[:, c % 2], arg[:, c % 2], ACT.Exp).then_inc(s["e_ready"], 1)
                if c >= 2:
                    sums_out(c - 2)
                if c == TC - 2:
                    head_squares(0)

            def hoT_out(th):
                act.wait_ge(s["ho_T"], th + 1)
                for k in range(KC):
                    A(hoT[:, k, th * HT:(th + 1) * HT], ps[:, 2 * k + th, :], ACT.Copy).then_inc(s["hoT_ready"], 1)

            head_root(0)
            sums_out(TC - 2)
            sums_out(TC - 1)
            hoT_out(0)
            head_squares(1)
            head_root(1)
            for th in range(NH):
                half = slice(th * HT, (th + 1) * HT)
                act.wait_ge(s["x1_ready"], KC * (th + 1))
                for k in range(KC):
                    A(sq[:, k, half], x1T[:, k, half], ACT.Square).then_inc(s["sq2_ready"], 1)
                if th == 0:
                    hoT_out(1)
                act.wait_ge(s["ss2_mm"], th + 1)
                A(sd2[:, 0, half], ps[:, 4 + th, :], ACT.Sqrt, scale=1.0 / D, bias=eps[:, 0:1]).then_inc(s["rms2_sd"], 1)
            for f in range(FC):
                act.wait_ge(s["g_scaled"], f + 1)
                A(sil[:, f % 2, :], sil[:, f % 2, :], ACT.Silu).then_inc(s["sil_ready"], 1)

            def router1_exp(th):
                act.wait_ge(s["z1_mm"], th + 1)
                A(ga_[:, th * HC:(th + 1) * HC].rearrange("p c e -> p (c e)"), ps[:, Z1_BANKS[th], 0:HC * E1], ACT.Exp,
                  scale=-1.0).then_inc(s["z1_exp"], 1)

            ln_root(3, 0)
            modulate(3, 0, 1, 2, 3, 0)
            ln_root(3, 1)
            router1_exp(0)
            modulate(3, 1, 1, 2, 3, 0)
            for th in range(NH):
                def silu(ic, r, first):
                    m = IC * th + ic
                    act.wait_ge(s["up_mm"], m + 1)
                    if not first:
                        act.wait_ge(s["g_ready"], m - 1)
                    A(sa_[:, r, :], ps[:, 2 + r, :], ACT.Silu).then_inc(s["moe_sil"], 1)

                if th == 0:
                    silu(0, 0, True)
                    silu(1, 1, True)
                    router1_exp(1)
                with act.Fori(1 if th == 0 else 0, IC // 2) as i:
                    for j in range(2):
                        silu(2 * i + j, (th + j) % 2, False)
                silu(IC - 1, th, False)

        @block.gpsimd
        def _(pool):
            tt = nc.gpsimd.tensor_tensor
            nc.gpsimd.memset(ones[:], 1.0).then_inc(s["ones_ready"], 1)
            nc.gpsimd.memset(zero16[:], 0.0).then_inc(s["ones_ready"], 1)
            nc.gpsimd.memset(eps[:, 0:1], RMS_EPS).then_inc(s["ones_ready"], 1)
            nc.gpsimd.memset(eps[:, 1:2], LN_EPS).then_inc(s["ones_ready"], 1)
            nc.gpsimd.memset(hpad[:, :, 0:TAPS - 1], 0.0).then_inc(s["zeroed"], 1)
            pool.wait_ge(s["zeroed"], 1)
            nc.gpsimd.memset(bcp[3 * QD:P, :], 0.0).then_inc(s["zeroed"], 1)
            pool.wait_ge(s["zeroed"], 2)
            nc.gpsimd.memset(carry[:], 0.0).then_inc(s["zeroed"], 1)
            pool.wait_ge(s["zeroed"], 3)
            for j in range(EC - 1):
                pool.wait_ge(s["sp_rest"], j + 1)
                tt(dt_[:, j, :], dt_[:, j, :], cv[:, j, :], ALU.subtract).then_inc(s["sp_sub"], 1)
            for j in range(2):
                pool.wait_ge(s["dt_ready"], j + 1)
                tt(u[:, j, 0:HT], dt_[:, j, 0:HT], hc[:, j, 0:HT], ALU.mult).then_inc(s["u_ready"], 1)
            pool.wait_ge(s["dt_ready"], EC)
            pool.wait_ge(s["u_ready"], 2)
            pool.wait_ge(s["u_rest"], 2)

            def dbu(it, r, th, first):
                pool.wait_ge(s["bc_copied"], it + 1)
                if not first:
                    pool.wait_ge(s["cmul_dve"], it - 3)
                tt(pb[:, r], u[:, :, th * HT:(th + 1) * HT], over(bsb[:, r, :].unsqueeze(1), [P, EC, HT]), ALU.mult)\
                    .then_inc(s["dbu_done"], 1)

            for r in range(4):
                if r == 2:
                    pool.wait_ge(s["dt_ready"], 2 * EC)
                dbu(r, r, 0, True)
            with pool.Fori(1, NS // 4) as i:
                for r in range(4):
                    dbu(4 * i + r, r, 0, False)
            pool.wait_ge(s["u_rest"], 2 + EC)
            for r in range(4):
                dbu(NS + r, r, 1, False)
            pool.wait_ge(s["y_evac"], 1)
            tt(hc[:, :, 0:HT], hc[:, :, 0:HT], gate[:, :, 0:HT], ALU.mult).then_inc(s["y_gated_a"], 1)
            with pool.Fori(1, NS // 4) as i:
                for r in range(4):
                    dbu(4 * i + r + NS, r, 1, False)

            pool.wait_ge(s["out_mm"], TC)
            nc.gpsimd.memset(vext[:, :, :, DV:VE], 1.0).then_inc(s["v_ones"], 1)
            pool.wait_ge(s["v_ones"], 1)
            nc.gpsimd.memset(gp[3 * QD:P, :], 0.0).then_inc(s["v_ones"], 1)
            pool.wait_ge(s["v_ones"], 2)
            nc.gpsimd.memset(qbd[:], 0.0).then_inc(s["v_ones"], 1)
            pool.wait_ge(s["v_ones"], 3)
            nc.gpsimd.memset(sbd[:], 0.0).then_inc(s["v_ones"], 1)
            pool.wait_ge(s["v_ones"], 4)
            nc.gpsimd.memset(lif[:], 0.0).then_inc(s["rows_zero"], 1)
            pool.wait_ge(s["rows_zero"], 1)
            nc.gpsimd.memset(rowM[0:3 * QD, :], 0.0).then_inc(s["rows_zero"], 1)
            pool.wait_ge(s["rows_zero"], 2)
            pool.wait_ge(s["ld_attn"], 7 * 16)
            for k in range(KC):
                for w in (wvif, wk, wog, wq):
                    last = nc.gpsimd.tensor_scalar(w[:, k, :], w[:, k, :], small1[:, 0, k:k + 1], None, ALU.mult)
            last.then_inc(s["w_scaled"], 1)
            pool.wait_ge(s["ld_gateup"], 48)
            for k in range(KC):
                for w in (wg, wu):
                    last = nc.gpsimd.tensor_scalar(w[:, k, :], w[:, k, :], small1[:, 1, k:k + 1], None, ALU.mult)
            last.then_inc(s["w_scaled"], 1)
            pool.wait_ge(s["w_scaled"], 2)
            pool.wait_ge(s["q_sb"], 1)
            for r in range(2):
                rows = slice(QD * r, QD * (r + 1))
                nc.gpsimd.tensor_copy(qbd[rows, 0, :, r, :], qT[rows, 0, :].rearrange("p (c t) -> p c t", t=P))\
                    .then_inc(s["qbd_pool"], 1)
                pool.wait_ge(s["qbd_pool"], r + 1)
            pool.wait_ge(s["ld_attn"], 7 * 16)
            tt(sg[:], sg[:], over(mhw[:].unsqueeze(1), [P, TC, D]), ALU.mult).then_inc(s["sg_ready"], 1)
            for c in range(TC):
                pool.wait_ge(s["arg_ready"], c + 1)
                a = arg[:, c % 2]
                nc.gpsimd.affine_select(out=a, in_=a, compare_op=ALU.is_ge, fill=-1e30, base=0,
                                        pattern=[[0, H], [1, P]], channel_multiplier=-1)\
                    .then_inc(s["arg_masked"], 1)
            pool.wait_ge(s["down_mm"], TC)
            nc.gpsimd.memset(dwx[:], 0.0).then_inc(s["dwx_zero"], 1)
            pool.wait_ge(s["dwx_zero"], 1)
            nc.gpsimd.memset(dwp[3 * QD:P, :], 0.0).then_inc(s["dwx_zero"], 1)
            pool.wait_ge(s["dwx_zero"], 2)
            for th in range(NH):
                half = slice(th * HT, (th + 1) * HT)
                pool.wait_ge(s["ln_h"], 12 + KC * (th + 1))
                nc.gpsimd.tensor_copy(h16[:, 0, :, half], hT[:, :, half]).then_inc(s["h_hi"], 1)
                pool.wait_ge(s["h_hi"], th + 1)
                tt(h16[:, 1, :, half], hT[:, :, half], h16[:, 0, :, half], ALU.subtract).then_inc(s["h_split"], 1)
            for th in range(NH):
                def low_part(ic, r):
                    m = IC * th + ic
                    pool.wait_ge(s["ghi_ready"], m + 1)
                    tt(g16[:, r, 1, :], gh1[:, r, :], g16[:, r, 0, :], ALU.subtract).then_inc(s["glo_ready"], 1)

                with pool.Fori(0, IC // 2) as i:
                    for j in range(2):
                        low_part(2 * i + j, (th + j) % 2)
                low_part(IC - 1, th)

        @block.vector
        def _(dve):
            V = nc.vector
            step = [0]

            def then(ins):
                step[0] += 1
                ins.then_inc(s["dve_step"], 1)
                dve.wait_ge(s["dve_step"], step[0])

            dve.wait_ge(s["c_silu"], 1)
            V.tensor_copy(scb[:], over(scs[:].unsqueeze(3), [P, 2, KC, P])).then_inc(s["c_wide"], 1)

            def ln_stats(n, th):
                if n == 0:
                    dve.wait_ge(s[f"ld_x{th}"], 16)
                for c in range(th * HC, (th + 1) * HC):
                    V.bn_stats(st[:, c, :], x[:, c, :]).then_inc(s["ln_stat"], 1)
                for c in range(th * HC, (th + 1) * HC):
                    dve.wait_ge(s["ln_stat"], TC * n + c + 1)
                    last = V.bn_aggr(mv[:, c, :], st[:, c, :])
                last.then_inc(s["ln_var"], 1)

            def ln_norm(n, th):
                chunks = slice(th * HC, (th + 1) * HC)
                dve.wait_ge(s["ln_sd"], NH * n + th + 1)
                then(V.reciprocal(rs[:, chunks], sd[:, chunks]))
                for c in range(th * HC, (th + 1) * HC):
                    V.tensor_scalar(xn[:, c, :], x[:, c, :], mv[:, c, 0:1], rs[:, c:c + 1], ALU.subtract, ALU.mult)\
                        .then_inc(s["ln_norm"], 1)

            def update_and_layernorm(n, ready, psum, g):
                for c in range(0, TC, 2):
                    ready(c)
                    then(V.tensor_tensor(tmpx[:], psum(c), over(g.unsqueeze(1), [P, 2, D]), ALU.mult))
                    then(V.tensor_tensor(x[:, c:c + 2, :], x[:, c:c + 2, :], tmpx[:], ALU.add))
                    if c == HC - 2:
                        ln_stats(n, 0)
                    if c == HC:
                        ln_norm(n, 0)
                ln_stats(n, 1)
                ln_norm(n, 1)

            ln_stats(0, 0)
            ln_norm(0, 0)
            ln_stats(0, 1)
            ln_norm(0, 1)
            dve.wait_ge(s["mod_mm"], 1)
            V.tensor_copy(modc[:, 0, 0:2].rearrange("p n f -> p (n f)"), ps[:, 7, 0:2 * KC]).then_inc(s["mod_raw"], 1)
            dve.wait_ge(s["mod_raw"], 1)
            V.tensor_scalar(modc[:, 0, 1, :], modc[:, 0, 1, :], 1.0, None, ALU.add).then_inc(s["mod_col"], 1)

            dve.wait_ge(s["ld_mix"], 64)
            dve.wait_ge(s["zeroed"], 3)
            for j in range(EC):
                dve.wait_ge(s["tap0_done"], j + 1)
                w = small0[:, j, :]
                for k in range(1, TAPS):
                    last = V.scalar_tensor_tensor(cv[:, j, :], hpad[:, j, k:k + T], w[:, k:k + 1], cv[:, j, :],
                                                  ALU.mult, ALU.add)
                    if k < TAPS - 1:
                        then(last)
                last.then_inc(s["conv_done"], 1)

            def columns_out(l, parts, bank):
                lo, hi = parts
                then(V.tensor_copy(modc[:, l, lo:hi].rearrange("p n f -> p (n f)"), ps[:, bank, lo * KC:hi * KC]))
                for n in range(lo + 1, hi, 2):
                    last = V.tensor_scalar(modc[:, l, n, :], modc[:, l, n, :], 1.0, None, ALU.add)
                return last

            def gates_out(l, bank):
                V.tensor_copy(gbc[:, l], ps[:, bank, :].rearrange("p (a f) -> p a f", a=2)).then_inc(s["gate_raw"], 1)

            def clamp_gates(l):
                g = gbc[:, l]
                then(V.scalar_tensor_tensor(gt1[:], g, -1.0, g, ALU.mult, ALU.max))
                V.tensor_scalar(gt1[:], gt1[:], 0.25, None, ALU.max)
                then(V.tensor_scalar(gt2[:], g, 0.0, 2.0, ALU.is_ge, ALU.mult))
                then(V.scalar_tensor_tensor(g, gt2[:], -1.0, gt1[:], ALU.add, ALU.mult))

            def three_parts(dst, src, high, rest, done):
                a, b, c = (slice(QD * q, QD * (q + 1)) for q in range(3))
                then(V.tensor_copy(high[0:3 * QD], src))
                V.tensor_copy(dst[a], high[a])
                then(V.tensor_tensor(rest[0:3 * QD], src, high[0:3 * QD], ALU.subtract))
                V.tensor_copy(dst[b], rest[b])
                then(V.tensor_copy(high[c], rest[c]))
                V.tensor_tensor(dst[c], rest[c], high[c], ALU.subtract).then_inc(done, 1)

            for j, b in enumerate(DT_BANKS):
                dve.wait_ge(s["abs_done"], j + 1)
                V.tensor_scalar(dt_[:, j, :], banks(b, 2), small0[:, j, 5:6], 0.0, ALU.add, ALU.max)\
                    .then_inc(s["relu_done"], 1)
            for j in range(EC):
                if j == 1:
                    dve.wait_ge(s["bc_mm"], 1)
                    three_parts(bcp, banks(2, 2, 3 * QD), bch, bcr, s["bc_parts"])
                dve.wait_ge(s["sp_w"], j + 1)
                V.scalar_tensor_tensor(cv[:, j, :], hpad[:, j, 0:T], -1.0, cv[:, j, :], ALU.add, ALU.subtract)\
                    .then_inc(s["sp_rest"], 1)
            dve.wait_ge(s["mod_mm"], 2)
            then(columns_out(0, (2, 4), 0))
            gates_out(0, 1)
            dve.wait_ge(s["sp_rest"], EC)
            V.tensor_tensor(dt_[:, EC - 1, :], dt_[:, EC - 1, :], cv[:, EC - 1, :], ALU.subtract).then_inc(s["sp_last"], 1)
            dve.wait_ge(s["sp_last"], 1)
            def dt_and_u(th, first_u):
                half = slice(th * HT, (th + 1) * HT)
                for j in range(EC):
                    dve.wait_ge(s["sp_sub"], min(j + 1, EC - 1))
                    dve.wait_ge(s["sp_ln"], j + 1)
                    V.tensor_tensor(dt_[:, j, half], dt_[:, j, half], hpad[:, j, half], ALU.add).then_inc(s["dt_ready"], 1)
                dve.wait_ge(s["dt_ready"], EC * (th + 1))
                for j in range(first_u, EC):
                    V.tensor_tensor(u[:, j, half], dt_[:, j, half], hc[:, j, half], ALU.mult).then_inc(s["u_rest"], 1)

            dt_and_u(0, 2)
            dt_and_u(1, 0)
            def y_plus_hd(j, half):
                return V.scalar_tensor_tensor(hc[:, j, half], hc[:, j, half], small0[:, j, 6:7], ps[:, j, :],
                                              ALU.mult, ALU.add)

            def scan_first(n, r, th):
                start = 0.0 if th == 0 else carry[:, n, 0:1]
                dve.wait_ge(s["dA_ready"], NS * th + n + 1)
                dve.wait_ge(s["dbu_done"], NS * th + n + 1)
                V.tensor_tensor_scan(pb[:, r, 0, :], dA[:, r, 0, :], pb[:, r, 0, :], start, ALU.mult, ALU.add)

            def scan_rest(n, r, th):
                for j in range(1, EC):
                    start = 0.0 if th == 0 else carry[:, n, j:j + 1]
                    last = V.tensor_tensor_scan(pb[:, r, j, :], dA[:, r, j, :], pb[:, r, j, :], start, ALU.mult, ALU.add)
                last.then_inc(s["scan_done"], 1)

            def scan_step(n, r, th, next_th):
                m = 0 if next_th != th else n + 1
                if next_th < NH:
                    scan_first(m, (r + 1) % 4, next_th)
                dve.wait_ge(s["scan_done"], NS * th + n + 1)
                if th == 0:
                    V.tensor_copy(carry[:, n, :], pb[:, r, :, HT - 1])
                if next_th < NH:
                    scan_rest(m, (r + 1) % 4, next_th)
                dve.wait_ge(s["bc_copied"], NS * th + n + 1)
                V.tensor_tensor(dA[:, r], pb[:, r], over(csb[:, r, :].unsqueeze(1), [P, EC, HT]), ALU.mult)\
                    .then_inc(s["cmul_dve"], 1)

            scan_first(0, 0, 0)
            scan_rest(0, 0, 0)
            for th in range(NH):
                if th:
                    scan_step(0, 0, th, th)
                    dve.wait_ge(s["sum_done"], NS * th)
                    for j in range(EC):
                        last = y_plus_hd(j, slice(0, HT))
                    last.then_inc(s["y_evac"], 1)
                    for r in range(1, 4):
                        scan_step(r, r, th, th)
                        if r == 2:
                            dve.wait_ge(s["mod_mm"], 3)
                            columns_out(1, (0, 4), 6).then_inc(s["mod_col"], 1)
                            gates_out(1, 7)
                with dve.Fori(1 if th else 0, NS // 4 - 1) as i:
                    for r in range(4):
                        scan_step(4 * i + r, r, th, th)
                for r in range(4):
                    scan_step(NS - 4 + r, r, th, th + 1 if r == 3 else th)
            dve.wait_ge(s["gate_raw"], 1)
            clamp_gates(0)
            late = slice(HT, T)
            for j in range(EC + 1):
                if j < EC:
                    if j < EC - 1:
                        dve.wait_ge(s["y_sum"], j + 1)
                    else:
                        dve.wait_ge(s["sum_done"], NH * NS)
                    y_plus_hd(j, late).then_inc(s["y_evac"], 1)
                if j:
                    dve.wait_ge(s["y_evac"], 1 + j)
                    last = V.tensor_tensor(hc[:, j - 1, late], hc[:, j - 1, late], gate[:, j - 1, late], ALU.mult)
            last.then_inc(s["y_gated_b"], 1)

            def out_ready(c):
                dve.wait_ge(s["out_mm"], c + 2)

            def out_psum(c):
                if c < HC:
                    return ps[:, 6 + c // 2, :].rearrange("p (c f) -> p c f", c=2)
                return ps[:, c - HC:c - HC + 2, 0:D]

            update_and_layernorm(1, out_ready, out_psum, gbc[:, 0, 0, :])

            def top2_first(e, ch):
                one, key, v2, v = (a[:, ch, 0:e] for a in (ga_, gb_, gc_, gl))
                n = ch.stop - ch.start

                def wide(a):
                    return over(a.unsqueeze(2), [P, n, e])

                then(V.tensor_reduce(gr[:, 0, ch], v, AX_X, ALU.max))
                then(V.tensor_tensor(key, v, wide(gr[:, 0, ch]), ALU.is_equal))
                then(V.tensor_tensor(key, key, over(rev[:, E1 - e:E1].unsqueeze(1), [P, n, e]), ALU.mult))
                then(V.tensor_reduce(gr[:, 1, ch], key, AX_X, ALU.max))
                then(V.tensor_tensor(one, key, wide(gr[:, 1, ch]), ALU.is_equal))
                then(V.scalar_tensor_tensor(v2, one, -4.0, v, ALU.mult, ALU.add))

            def top2_second(e, ch):
                one, key, v2 = (a[:, ch, 0:e] for a in (ga_, gb_, gc_))
                n = ch.stop - ch.start

                def wide(a):
                    return over(a.unsqueeze(2), [P, n, e])

                then(V.tensor_reduce(gr[:, 2, ch], v2, AX_X, ALU.max))
                then(V.tensor_tensor(key, v2, wide(gr[:, 2, ch]), ALU.is_equal))
                then(V.tensor_tensor(key, key, over(rev[:, E1 - e:E1].unsqueeze(1), [P, n, e]), ALU.mult))
                then(V.tensor_reduce(gr[:, 3, ch], key, AX_X, ALU.max))
                then(V.tensor_tensor(key, key, wide(gr[:, 3, ch]), ALU.is_equal))
                then(V.tensor_tensor(one, one, key, ALU.add))

            def top2_weights(e, ch, scale):
                one, key, v = (a[:, ch, 0:e] for a in (ga_, gb_, gl))
                then(V.tensor_tensor(gr[:, 4, ch], gr[:, 0, ch], gr[:, 2, ch], ALU.add))
                then(V.reciprocal(gr[:, 5, ch], gr[:, 4, ch]))
                then(V.tensor_tensor(key, v, one, ALU.mult))
                then(V.scalar_tensor_tensor(key, key, scale, over(gr[:, 5, ch].unsqueeze(2), [P, ch.stop - ch.start, e]),
                                            ALU.mult, ALU.mult))

            dve.wait_ge(s["f0_mm"], 1)
            pair = ps[:, 0:4, 0:272].rearrange("p b (c n) -> p b c n", c=2)
            v = gl[:, :, 0:E0]
            then(V.tensor_copy(v.rearrange("p (b c) e -> p b c e", c=2), pair[:, :, :, 0:E0]))
            then(V.tensor_reduce(gr[:, 0], v, AX_X, ALU.max))
            V.tensor_tensor(v, v, over(gr[:, 0].unsqueeze(2), [P, TC, E0]), ALU.subtract).then_inc(s["soft_arg"], 1)
            dve.wait_ge(s["soft_exp"], 1)
            then(V.tensor_reduce(gr[:, 1], ga_[:, :, 0:E0], AX_X, ALU.add))
            then(V.reciprocal(gr[:, 2], gr[:, 1]))
            then(V.tensor_tensor(v, ga_[:, :, 0:E0], over(gr[:, 2].unsqueeze(2), [P, TC, E0]), ALU.mult))
            whole = slice(0, TC)
            top2_first(E0, whole)
            top2_second(E0, whole)
            top2_weights(E0, whole, 16.0)
            cw = gb_[:, :, 0:E0].rearrange("p (b c) e -> p b c e", c=2)
            tw = ffn0_t.rearrange("p (b c) n -> p b c n", c=2)
            for c in range(2):
                last = V.tensor_tensor(tw[:, :, c, :].rearrange("p b (e r) -> p b e r", r=RL),
                                       pair[:, :, c, E0:136].rearrange("p b (e r) -> p b e r", r=RL),
                                       over(cw[:, :, c, :].unsqueeze(3), [P, 4, E0, RL]), ALU.mult)
            last.then_inc(s["f0_t"], 1)
            def lora_ready(c):
                dve.wait_ge(s["f0_lora"], c + 2)

            update_and_layernorm(2, lora_ready, lambda c: ps[:, 4 + c // 2, :].rearrange("p (c f) -> p c f", c=2),
                                 gbc[:, 0, 1, :])

            dve.wait_ge(s["gate_raw"], 2)
            clamp_gates(1)
            V.tensor_scalar(gt2[:, 0, :], gbc[:, 1, 1, :], WS, None, ALU.mult)
            dve.wait_ge(s["rms_sd"], 1)
            V.reciprocal(rinv[:, 1], rinv[:, 0]).then_inc(s["rinv_ready"], 1)
            dve.wait_ge(s["rinv_ready"], 1)
            for c in range(TC):
                b = 2 * (c % 3)
                dve.wait_ge(s["v_mm"], c + 1)
                V.scalar_tensor_tensor(zif[:, c, :], ps[:, b, D:D + 2 * H], rinv[:, 1, c:c + 1], bif[:], ALU.mult, ALU.add)\
                    .then_inc(s["z_in"], 1)
                V.tensor_scalar(vext[:, c, :, 0:DV], ps[:, b, 0:D].rearrange("p (h v) -> p h v", h=H),
                                rinv[:, 1, c:c + 1], None, ALU.mult).then_inc(s["v_sb"], 1)
            dve.wait_ge(s["k_mm"], 1)
            V.tensor_copy(kT[:, 0, :], banks(4, 2)).then_inc(s["k_sb"], 1)

            dve.wait_ge(s["rows_zero"], 2)
            dve.wait_ge(s["z_tanh"], 1)
            for q in range(3):
                V.tensor_scalar(lif[:, 1, :, QD * q:QD * q + H], zt[:, :, 0:H], CAP, None, ALU.mult)
            dve.wait_ge(s["z_exp"], 1)
            V.tensor_scalar(lw[:, 1], lw[:, 0], 1.0, None, ALU.add).then_inc(s["z_w"], 1)
            dve.wait_ge(s["z_w"], 1)
            then(V.tensor_scalar(lw[:, 3], lw[:, 1], -1.0, None, ALU.add))
            then(V.tensor_tensor(lw[:, 3], lw[:, 0], lw[:, 3], ALU.subtract))
            then(V.reciprocal(lw[:, 0], lw[:, 1]))
            then(V.tensor_tensor(lw[:, 3], lw[:, 3], lw[:, 0], ALU.mult))
            dve.wait_ge(s["z_ln"], 1)
            then(V.tensor_tensor(lw[:, 3], lw[:, 3], lw[:, 2], ALU.add))
            for q in range(3):
                last = V.tensor_scalar(lif[:, 0, :, QD * q:QD * q + H], lw[:, 3], -1.0, None, ALU.mult)
            last.then_inc(s["lif_ready"], 1)
            dve.wait_ge(s["k_mm"], 2)
            V.tensor_copy(kT[:, 1, :], banks(0, 2)).then_inc(s["k_sb"], 1)
            dve.wait_ge(s["lif_T"], 1)
            R3 = slice(0, 3 * QD)
            then(V.tensor_tensor_scan(rowF[R3, :], banks(4, 2, 3 * QD), rowM[R3, :], 0.0, ALU.add, ALU.add))
            dve.wait_ge(s["lif_T"], 2)
            then(V.tensor_tensor(rowA[R3, :], banks(0, 2, 3 * QD), rowF[R3, :], ALU.subtract))
            then(V.tensor_tensor_scan(rowG[R3, :], rowA[R3, :], rowA[R3, :], -1e30, ALU.max, ALU.max))
            V.tensor_tensor(rowM[R3, :], rowF[R3, :], rowG[R3, :], ALU.add).then_inc(s["row_tok"], 1)
            dve.wait_ge(s["row_tok"], 1)
            three_parts(gp, rowG[R3, :], gh, rowF, s["row_parts"])
            dve.wait_ge(s["tok_T"], 1)
            dve.wait_ge(s["enm_ready"], 1)
            V.tensor_copy(agt[:, 0:2].rearrange("p a c h -> p (a c h)"), ps[:, 2, 0:2 * TC * H])
            dve.wait_ge(s["rr_mm"], 1)
            V.tensor_copy(rbc[:].rearrange("p h c -> p (h c)"), ps[:, 3, 0:H * TC])
            then(V.tensor_copy(rrow[:].rearrange("p g c -> p (g c)"), ps[:, 3, H * TC:(H + HG) * TC]))
            ends = rbc[:].rearrange("p h c -> p c h")
            V.tensor_tensor(wkt[:], agt[:, 0], ends, ALU.subtract)
            V.tensor_tensor(dec[:, :, 1:], rrow[:, :, 0:TC - 1], rrow[:, :, 1:], ALU.subtract).then_inc(s["w_arg"], 1)
            for g in range(HG):
                dve.wait_ge(s["qg_mm"], g + 1)
                V.tensor_tensor(qw[:, g, P:].rearrange("p (c t) -> p c t", t=P),
                                over(rrow[:, g, 0:TC - 1].unsqueeze(2), [P, TC - 1, P]),
                                banks(0, 2)[:, P:].rearrange("p (c t) -> p c t", t=P), ALU.subtract)\
                    .then_inc(s["qw_arg"], 1)
            for r in range(2):
                rows = slice(QD * r, QD * (r + 1))
                V.tensor_copy(qbd[rows, 1, :, r, :], qT[rows, 1, :].rearrange("p (c t) -> p c t", t=P))\
                    .then_inc(s["qbd_dve"], 1)
            dve.wait_ge(s["w_exp"], 1)
            then(V.tensor_tensor(wkt[:], wkt[:], over(rinv[:, 1].unsqueeze(2), [P, TC, H]), ALU.mult))
            dve.wait_ge(s["kT_T"], 1)
            for b in range(4):
                V.tensor_tensor(ks[:, 2 * b:2 * b + 2].rearrange("p c h n -> p (c h) n"),
                                ps[:, 4 + b, :].rearrange("p (ch n) -> p ch n", n=QR),
                                over(wkt[:, 2 * b:2 * b + 2].rearrange("p c h -> p (c h)").unsqueeze(2),
                                     [P, 2 * H, QR]), ALU.mult).then_inc(s["ks_ready"], 1)
            dve.wait_ge(s["qw_exp"], HG)
            V.tensor_tensor(qw[:, :, P:], qw[:, :, P:], qT[:, :, P:], ALU.mult).then_inc(s["qw_ready"], 1)
            for c in range(TC - 1):
                dve.wait_ge(s["state_mm"], 4 * (c // 4) + 4)
                for g in range(HG):
                    col = (c % 4) * HG * VE + g * VE
                    add = ps[:, 2 + c // 4, col:col + VE]
                    if c == 0:
                        last = V.tensor_copy(states[:, c, g, :], add)
                    else:
                        last = V.scalar_tensor_tensor(states[:, c, g, :], states[:, c - 1, g, :], dec[:, g, c:c + 1], add,
                                                      ALU.mult, ALU.add)
                last.then_inc(s["state_done"], 1)
                dve.wait_ge(s["state_done"], c + 1)

            def exponent(c):
                dve.wait_ge(s["g_mm"], c + 1)
                if c >= 2:
                    dve.wait_ge(s["pr_ready"], c - 1)
                V.tensor_tensor(arg[:, c % 2], over(agt[:, 0, c, :].unsqueeze(2), [P, H, P]),
                                banks(4, 2).rearrange("p (h t) -> p h t", h=H), ALU.subtract)\
                    .then_inc(s["arg_ready"], 1)

            nv = num[:].rearrange("p c h v -> p (c h) v")
            flat = [nden[:, a].rearrange("p c h -> p (c h)") for a in range(3)]

            def normalised(th):
                cs_ = slice(th * HC, (th + 1) * HC)
                heads = slice(th * HC * H, (th + 1) * HC * H)
                own = over(rinv[:, 1, cs_].unsqueeze(2), [P, HC, H])
                dve.wait_ge(s["num_ready"], HC * (th + 1))
                den = num[:, cs_, :, DV]
                then(V.scalar_tensor_tensor(nden[:, 0, cs_], den, -1.0, den, ALU.mult, ALU.max))
                then(V.tensor_tensor(nden[:, 0, cs_], nden[:, 0, cs_], own, ALU.mult))
                then(V.tensor_tensor(nden[:, 0, cs_], nden[:, 0, cs_], agt[:, 2, cs_], ALU.max))
                then(V.reciprocal(nden[:, 1, cs_], nden[:, 0, cs_]))
                then(V.tensor_tensor(nden[:, 1, cs_], nden[:, 1, cs_], own, ALU.mult))
                V.tensor_tensor(ho_head[:, heads], nv[:, heads, 0:DV], over(flat[1][:, heads].unsqueeze(2), [P, HC * H, DV]),
                                ALU.mult).then_inc(s["den_ready"], 1)

            def head_sums(th):
                heads = slice(th * HC * H, (th + 1) * HC * H)
                dve.wait_ge(s["num_sq"], th + 1)
                V.tensor_reduce(flat[1][:, heads], sq_tok[:, heads], AX_X, ALU.add).then_inc(s["var_ready"], 1)

            def head_outputs(th):
                heads = slice(th * HC * H, (th + 1) * HC * H)
                toks = slice(th * HC, (th + 1) * HC)
                dve.wait_ge(s["var_sd"], th + 1)
                then(V.reciprocal(flat[0][:, heads], flat[2][:, heads]))
                then(V.tensor_tensor(ho_head[:, heads], ho_head[:, heads],
                                     over(flat[0][:, heads].unsqueeze(2), [P, HC * H, DV]), ALU.mult))
                V.tensor_tensor(ho_tok[:, toks], ho_tok[:, toks], sg[:, toks], ALU.mult).then_inc(s["ho_ready"], 1)

            dve.wait_ge(s["sg_ready"], 1)
            dve.wait_ge(s["enm_ready"], 1)
            dve.wait_ge(s["qbd_act"], 4)
            dve.wait_ge(s["qbd_pool"], 2)
            exponent(0)
            dve.wait_ge(s["v_ones"], 4)
            for r in range(4):
                rows = slice(QD * r, QD * (r + 1))
                last = V.tensor_copy(sbd[rows, :, :, r, :], states[rows])
            last.then_inc(s["sbd_ready"], 1)
            for c in range(TC):
                if c + 1 < TC:
                    exponent(c + 1)
                dve.wait_ge(s["e_ready"], c + 1)
                dve.wait_ge(s["s_mm"], c + 1)
                if c >= 2:
                    dve.wait_ge(s["intra_mm"], c - 1)
                V.scalar_tensor_tensor(pr[:, c % 2].rearrange("p h t -> p (h t)"), banks(2 * (c % 2), 2),
                                       rinv[:, 1, c:c + 1], arg[:, c % 2].rearrange("p h t -> p (h t)"),
                                       ALU.mult, ALU.mult).then_inc(s["pr_ready"], 1)
                if c == TC - 3:
                    normalised(0)
                if c == TC - 2:
                    head_sums(0)
            head_outputs(0)
            normalised(1)
            head_sums(1)

            def x1_out(th):
                half = slice(th * HT, (th + 1) * HT)
                for m in range(KC):
                    dve.wait_ge(s["wo_mm"], KC * th + m + 1)
                    V.tensor_tensor(x1T[:, m, half], hT[:, m, half], ps[:, 4 + 2 * m + th, :], ALU.add)\
                        .then_inc(s["x1_ready"], 1)

            x1_out(0)
            head_outputs(1)
            x1_out(1)
            for th in range(NH):
                dve.wait_ge(s["rms2_sd"], th + 1)
                then(V.reciprocal(sd2[:, 1, th * HT:(th + 1) * HT], sd2[:, 0, th * HT:(th + 1) * HT]))
            for f in range(FC):
                b = 4 * (f % 2)
                dve.wait_ge(s["gu_mm"], f + 1)
                V.tensor_tensor(sil[:, f % 2, :], banks(b, 2), sd2[:, 1], ALU.mult).then_inc(s["g_scaled"], 1)
                dve.wait_ge(s["sil_ready"], f + 1)
                V.tensor_tensor(gg[:, f, :], sil[:, f % 2, :], banks(b + 2, 2), ALU.mult).then_inc(s["gu_used"], 1)
                dve.wait_ge(s["gu_used"], f + 1)
                V.tensor_tensor(gg[:, f, :], gg[:, f, :], sd2[:, 1], ALU.mult).then_inc(s["gg_ready"], 1)
            def down_ready(c):
                dve.wait_ge(s["down_mm"], c + 2)

            update_and_layernorm(3, down_ready, lambda c: ps[:, c:c + 2, 0:D], gbc[:, 1, 0, :])

            def router1_first(th, ch):
                dve.wait_ge(s["z1_exp"], th + 1)
                then(V.tensor_scalar(gl[:, ch], ga_[:, ch], 1.0, None, ALU.add))
                then(V.reciprocal(gl[:, ch], gl[:, ch]))
                top2_first(E1, ch)

            def router1_weights(th, ch):
                top2_weights(E1, ch, 1.0)
                dve.wait_ge(s["dwx_zero"], 2)
                wide = dwx[:].rearrange("p c (q e) -> p c q e", q=3)
                for q in range(3):
                    last = V.tensor_copy(wide[:, ch, q, 0:E1], gb_[:, ch])
                last.then_inc(s["dw_ready"], 1)

            def router1_parts(th):
                half = slice(th * HT, (th + 1) * HT)
                dve.wait_ge(s["dw_T"], th + 1)
                three_parts(dwp[:, half], ps[0:3 * QD, 6 + th, :], dwh[:, half], dwr[:, half], s["dw_parts"])

            early, late = slice(0, HC), slice(HC, TC)
            router1_first(0, early)
            top2_second(E1, early)
            router1_weights(0, early)

            def high_part(m, r, first):
                dve.wait_ge(s["g_ready"], m + 1)
                if not first:
                    dve.wait_ge(s["acc_mm"], m - 1)
                V.tensor_copy(g16[:, r, 0, :], gh1[:, r, :]).then_inc(s["ghi_ready"], 1)

            def gated_shared(m, first):
                r = m % 2
                dve.wait_ge(s["moe_sil"], m + 1)
                if not first:
                    dve.wait_ge(s["glo_ready"], m - 1)
                V.scalar_tensor_tensor(gh1[:, r, :], sa_[:, r, :], 1.0 / WS, ps[:, 4 + r, :], ALU.mult, ALU.mult)\
                    .then_inc(s["g_ready"], 1)
                high_part(m, r, first)

            def gated(th, ic, r):
                m = IC * th + SC + ic
                dve.wait_ge(s["moe_sil"], m + 1)
                V.tensor_tensor(sa_[:, r, :], sa_[:, r, :], ps[:, 4 + r, :], ALU.mult).then_inc(s["moe_prod"], 1)
                dve.wait_ge(s["moe_prod"], RC * th + ic + 1)
                dve.wait_ge(s["glo_ready"], m - 1)
                V.tensor_tensor(gh1[:, r, :], sa_[:, r, :], ps[:, 6 + r, :], ALU.mult).then_inc(s["g_ready"], 1)
                high_part(m, r, False)

            gated_shared(0, True)
            gated_shared(1, True)
            router1_parts(0)
            for th in range(NH):
                gated_shared(IC * th + 2, False)
                if th == 0:
                    router1_first(1, late)
                    for ic in range(2):
                        gated(0, ic, (SC + ic) % 2)
                    top2_second(E1, late)
                    for ic in range(2, 4):
                        gated(0, ic, (SC + ic) % 2)
                    router1_weights(1, late)
                with dve.Fori(2 if th == 0 else 0, RC // 2) as i:
                    for j in range(2):
                        gated(th, 2 * i + j, (th + SC + j) % 2)
                if th + 1 < NH:
                    router1_parts(1)
                if th + 1 < NH:
                    dve.wait_ge(s["acc_mm"], IC * (th + 1))
                    V.tensor_tensor(xn[:, 0:HC, :], banks(0, 2).rearrange("p (c f) -> p c f", c=HC),
                                    over(gt2[:, 0, :].unsqueeze(1), [P, HC, D]), ALU.mult).then_inc(s["y_read"], 1)
                    gated_shared(IC * (th + 1), False)
                    gated_shared(IC * (th + 1) + 1, False)
                    dve.wait_ge(s["y_read"], 1)
                    V.tensor_tensor(x[:, 0:HC, :], x[:, 0:HC, :], xn[:, 0:HC, :], ALU.add).then_inc(s["x_out"], 1)
            for b in range(2):
                if b == 0:
                    dve.wait_ge(s["acc_first"], 1)
                else:
                    dve.wait_ge(s["acc_mm"], 2 * IC)
                V.tensor_tensor(xn[:, 2 * b:2 * b + 2, :], ps[:, b, :].rearrange("p (c f) -> p c f", c=2),
                                over(gt2[:, 0, :].unsqueeze(1), [P, 2, D]), ALU.mult).then_inc(s["y_read"], 1)
            for b in range(2):
                chunks = slice(HC + 2 * b, HC + 2 * b + 2)
                dve.wait_ge(s["y_read"], 2 + b)
                V.tensor_tensor(x[:, chunks, :], x[:, chunks, :], xn[:, 2 * b:2 * b + 2, :], ALU.add)\
                    .then_inc(s["x_out"], 1)


def program(nc, arrays):
    d = {}
    for name, a in arrays.items():
        t = nc.dram_tensor(f"in_{name}_dram", a.shape, mybir.dt.from_np(a.dtype), kind="ExternalInput").ap()
        d[name] = t
    out = nc.dram_tensor("out_0_dram", (T, D), F32, kind="ExternalOutput").ap()
    adaln_two_layers(nc, d, out)


def _rows(w):
    import numpy as np
    return np.ascontiguousarray(w.reshape(-1, 128, w.shape[1]).transpose(1, 0, 2))


def _heads_apart(w):
    import numpy as np
    o = np.zeros((w.shape[0], 8, 32), w.dtype)
    o[:, :, :16] = w.reshape(w.shape[0], 8, 16)
    return o.reshape(w.shape[0], 256)


def kernel(**inputs):
    import numpy as np
    import concourse.bacc as _bacc
    from concourse.bass_utils import run_bass_kernel_spmd as _run

    i = {k: np.asarray(v) for k, v in inputs.items()}
    cat, tile = np.concatenate, np.tile
    bf = i["L1_ffn_w1"].dtype
    cols = lambda v: v.reshape(-1, 128).T
    ar = {}
    ar["x"] = i["L0_attn_hidden_states"].reshape(T, D)
    ar["c"] = np.stack([cols(i["L0_c"].ravel()), cols(i["L1_c"].ravel())], 1)
    ar["wmod"] = np.stack([_rows(i["L0_wmod"]), _rows(i["L1_wmod"])])
    ar["win"] = _rows(i["L0_attn_in_proj_w"].T)
    conv = i["L0_attn_conv_w"].reshape(EC, P, TAPS).transpose(1, 0, 2)
    vecs = [cols(i[n]) for n in ("L0_attn_conv_b", "L0_attn_dt_proj_b", "L0_attn_D")]
    ar["small0"] = cat([conv] + [v[:, :, None] for v in vecs], 2)
    ar["alog"] = i["L0_attn_A_log"].reshape(EC, P, NS).transpose(1, 2, 0)
    xp = i["L0_attn_x_proj_w"].T
    ar["wx"] = _rows(cat([xp[:, :R0]] + [xp[:, R0:]] * 3, 1))
    ar["wdt"] = i["L0_attn_dt_proj_w"].T
    ar["wo0"] = _rows(i["L0_attn_out_proj_w"].T)
    ar["wf0"] = _rows(cat([i["L0_ffn_weight"].T, i["L0_ffn_gate_w"].T, i["L0_ffn_A_w"].reshape(P, D).T], 1))
    ar["wlb"] = i["L0_ffn_B_w"].transpose(0, 2, 1).reshape(P, D)
    ar["norm_w"] = np.stack([cols(i["L1_attn_norm1_w"]), cols(i["L1_attn_norm2_w"])], 1)
    ar["wq"] = _rows(_heads_apart(i["L1_attn_wq"]))
    ar["wk"] = _rows(_heads_apart(i["L1_attn_wk"]))
    ar["wvif"] = _rows(cat([i["L1_attn_wv"], i["L1_attn_w_ig"], i["L1_attn_w_fg"]], 1))
    ar["wog"] = _rows(i["L1_attn_w_og"])
    ar["bif"] = tile(cat([i["L1_attn_b_ig"], i["L1_attn_b_fg"]])[None], (P, 1))
    ar["mhw"] = tile(i["L1_attn_mh_w"][None], (P, 1))
    ar["wout1"] = _rows(i["L1_attn_w_out"])
    ar["wg"] = _rows(i["L1_attn_w_gate"])
    ar["wu"] = _rows(i["L1_attn_w_up"])
    ar["wd"] = _rows(i["L1_attn_w_down"])
    ar["wg1"] = _rows(i["L1_ffn_gate_w"].T)
    inner = i["L1_ffn_w1"].shape[1]

    def all_rows(routed, shared):
        m = cat([routed.reshape(-1, D), shared], 0)
        return cat([m, np.zeros((IC * P - m.shape[0], D), m.dtype)], 0)

    ar["w1"] = _rows(all_rows(i["L1_ffn_w1"], i["L1_ffn_sw1"]).T)
    ar["w3"] = _rows(all_rows(i["L1_ffn_w3"], i["L1_ffn_sw3"]).T)
    ar["w2"] = _rows(all_rows(i["L1_ffn_w2"].transpose(0, 2, 1), i["L1_ffn_sw2"].T))
    row = np.arange(P)
    ar["ident"] = np.eye(P, dtype=np.float32)
    inside = (row < 3 * QD)[:, None, None]
    ar["sel"] = (inside & (row[:, None, None] % QD == np.arange(2 * NS)[None, :, None]) & np.ones((1, 1, P), bool)).astype(bf)
    head = 4 * np.arange(HG)[:, None] + row[None, :] // QD
    ar["selr"] = (inside & (row[:, None, None] % QD == head[None])).astype(bf)
    expert = np.minimum(np.arange(IC * P).reshape(IC, P) // inner, E1)
    ar["selx"] = ((inside & (row[:, None, None] % QD == expert[None, :RC])) * np.float32(1 / WS)).astype(bf)
    ar["rev"] = tile(np.arange(E1, 0, -1, dtype=np.float32)[None], (P, 1))

    nc = _bacc.Bacc("TRN2", target_bir_lowering=False, num_devices=1)
    ar = {k: np.ascontiguousarray(v) for k, v in ar.items()}
    program(nc, ar)
    r = _run(nc, [{f"in_{k}_dram": v for k, v in ar.items()}], core_ids=[0])
    return r.results[0]["out_0_dram"].reshape(1, T, D)
```
